# Optimizing a Trainium2 kernel written in Bass

```python
import numpy as np
import jax
import jax.numpy as jnp

def _softmax(x, axis=-1):
    return jax.nn.softmax(x, axis=axis)

def _gelu(x):
    return jax.nn.gelu(x, approximate=True)

def _silu(x):
    return jax.nn.silu(x)

def _sigmoid(x):
    return jax.nn.sigmoid(x)

def _layernorm(x, axis=-1, eps=1e-05):
    m = jnp.mean(x, axis=axis, keepdims=True)
    v = jnp.var(x, axis=axis, keepdims=True)
    return (x - m) / jnp.sqrt(v + eps)

def _scatter_add(tgt, idx, src, axis=0):
    return tgt.at[idx].add(src)

def _segment_sum(src, seg, n):
    return jax.ops.segment_sum(src, seg, n)
kernel_name = 'mk_seq_preln_d2_jaxref_r8_2b0eb3'

def setup_inputs(seed: int=0):
    np.random.seed(seed)
    _w = jnp.asarray

    def _L0_attn_setup():
        import jax, jax.numpy as jnp
        import numpy as np
        D_MODEL = 128
        H = 16
        DH = 64
        EPS = 1e-05

        def _layernorm(x, g, b):
            mu = jnp.mean(x, axis=-1, keepdims=True)
            var = jnp.var(x, axis=-1, keepdims=True)
            return (x - mu) * jax.lax.rsqrt(var + EPS) * g + b
        key = jax.random.key(seed)
        ks = jax.random.split(key, 16)
        B, L = (4, 512)
        s = 0.02
        inp = {'x': jax.random.normal(ks[0], (B, L, D_MODEL), jnp.float32), 'ln1_g': jnp.ones((D_MODEL,), jnp.float32), 'ln1_b': jnp.zeros((D_MODEL,), jnp.float32), 'Wq': jax.random.normal(ks[1], (D_MODEL, H * DH), jnp.float32) * s, 'bq': jnp.zeros((H * DH,), jnp.float32), 'Wk': jax.random.normal(ks[2], (D_MODEL, H * DH), jnp.float32) * s, 'bk': jnp.zeros((H * DH,), jnp.float32), 'Wv': jax.random.normal(ks[3], (D_MODEL, H * DH), jnp.float32) * s, 'bv': jnp.zeros((H * DH,), jnp.float32), 'Wg': jax.random.normal(ks[4], (D_MODEL, H * DH), jnp.float32) * s, 'bg': jnp.zeros((H * DH,), jnp.float32), 'decay_logit': jnp.zeros((H,), jnp.float32), 'Wo': jax.random.normal(ks[5], (H * DH, D_MODEL), jnp.float32) * s, 'bo': jnp.zeros((D_MODEL,), jnp.float32), 'ln2_g': jnp.ones((D_MODEL,), jnp.float32), 'ln2_b': jnp.zeros((D_MODEL,), jnp.float32), 'W1': jax.random.normal(ks[6], (D_MODEL, 4 * D_MODEL), jnp.float32) * s, 'b1': jnp.zeros((4 * D_MODEL,), jnp.float32), 'W2': jax.random.normal(ks[7], (4 * D_MODEL, D_MODEL), jnp.float32) * s, 'b2': jnp.zeros((D_MODEL,), jnp.float32)}
        return inp
    _L0_attn_in = _L0_attn_setup()

    def _L0_ffn_setup():
        import jax, jax.numpy as jnp
        import numpy as np
        D_MODEL, EXPERT_DIM, NUM_EXPERTS, TOP_K = (128, 256, 16, 2)
        SEQ_LEN, BATCH = (256, 2)
        key = jax.random.key(seed)
        ks = jax.random.split(key, 8)
        s_d = 1.0 / np.sqrt(D_MODEL)
        s_h = 1.0 / np.sqrt(EXPERT_DIM)
        return {'x': jax.random.normal(ks[0], (SEQ_LEN, BATCH, D_MODEL), jnp.float32), 'Wg': jax.random.uniform(ks[1], (D_MODEL, NUM_EXPERTS), jnp.float32, -s_d, s_d), 'bg': jax.random.uniform(ks[2], (NUM_EXPERTS,), jnp.float32, -s_d, s_d), 'bias': jnp.zeros((NUM_EXPERTS,), jnp.float32), 'W1': jax.random.uniform(ks[3], (NUM_EXPERTS, D_MODEL, EXPERT_DIM), jnp.float32, -s_d, s_d), 'b1': jax.random.uniform(ks[4], (NUM_EXPERTS, EXPERT_DIM), jnp.float32, -s_d, s_d), 'W2': jax.random.uniform(ks[5], (NUM_EXPERTS, EXPERT_DIM, D_MODEL), jnp.float32, -s_h, s_h), 'b2': jax.random.uniform(ks[6], (NUM_EXPERTS, D_MODEL), jnp.float32, -s_h, s_h)}
    _L0_ffn_in = _L0_ffn_setup()

    def _L1_attn_setup():
        import jax, jax.numpy as jnp
        import numpy as np
        EMBED = 128
        HEADS = 16
        HEAD_DIM = EMBED // HEADS
        B, T = (2, 256)
        ROPE_THETA = 10000.0

        def _rope(x):
            D = x.shape[-1]
            inv_freq = 1.0 / ROPE_THETA ** (jnp.arange(0, D, 2, dtype=jnp.float32) / D)
            freqs = jnp.arange(x.shape[2], dtype=jnp.float32)[:, None] * inv_freq[None, :]
            cos = jnp.cos(freqs).astype(x.dtype)
            sin = jnp.sin(freqs).astype(x.dtype)
            x1, x2 = (x[..., :D // 2], x[..., D // 2:])
            return jnp.concatenate([x1 * cos - x2 * sin, x2 * cos + x1 * sin], axis=-1)
        key = jax.random.key(seed)
        ks = jax.random.split(key, 5)
        s = 1.0 / np.sqrt(EMBED)
        return {'x': jax.random.normal(ks[0], (B, T, EMBED), dtype=jnp.float32), 'Wq': jax.random.normal(ks[1], (EMBED, EMBED), dtype=jnp.float32) * s, 'bq': jnp.zeros((EMBED,), dtype=jnp.float32), 'Wk': jax.random.normal(ks[2], (EMBED, EMBED), dtype=jnp.float32) * s, 'bk': jnp.zeros((EMBED,), dtype=jnp.float32), 'Wv': jax.random.normal(ks[3], (EMBED, EMBED), dtype=jnp.float32) * s, 'bv': jnp.zeros((EMBED,), dtype=jnp.float32), 'Wo': jax.random.normal(ks[4], (EMBED, EMBED), dtype=jnp.float32) * s, 'bo': jnp.zeros((EMBED,), dtype=jnp.float32)}
    _L1_attn_in = _L1_attn_setup()

    def _L1_ffn_setup():
        import jax, jax.numpy as jnp
        import numpy as np
        from math import sqrt
        B, S, D, H, E, K, FF = (2, 128, 128, 16, 8, 2, 512)
        HD = D // H
        EPS = 1e-05

        def _rope_cache(seq_len, hd):
            inv_freq = 1.0 / 10000.0 ** (jnp.arange(0, hd, 2, dtype=jnp.float32) / hd)
            t = jnp.arange(seq_len, dtype=jnp.float32)
            freqs = t[:, None] * inv_freq[None, :]
            emb = jnp.concatenate([freqs, freqs], axis=-1)
            return (jnp.cos(emb), jnp.sin(emb))

        def _rotate_half(x):
            x1, x2 = jnp.split(x, 2, axis=-1)
            return jnp.concatenate([-x2, x1], axis=-1)

        def _layernorm(x, g, b):
            m = jnp.mean(x, axis=-1, keepdims=True)
            v = jnp.var(x, axis=-1, keepdims=True)
            return (x - m) * jax.lax.rsqrt(v + EPS) * g + b

        def _forward(x, Wq, bq, Wk, bk, Wv, bv, Wo, bo, Wg, bg, W1, b1, W2, b2, g1, be1, g2, be2):
            bsz, seq, d = x.shape
            q = (x @ Wq + bq).reshape(bsz, seq, H, HD).transpose(0, 2, 1, 3)
            k = (x @ Wk + bk).reshape(bsz, seq, H, HD).transpose(0, 2, 1, 3)
            v = (x @ Wv + bv).reshape(bsz, seq, H, HD).transpose(0, 2, 1, 3)
            cos, sin = _rope_cache(seq, HD)
            cos = cos[None, None]
            sin = sin[None, None]
            q = q * cos + _rotate_half(q) * sin
            k = k * cos + _rotate_half(k) * sin
            scores = jnp.einsum('bhqd,bhkd->bhqk', q, k) / sqrt(HD)
            attn = jax.nn.softmax(scores, axis=-1)
            ao = jnp.einsum('bhqk,bhkd->bhqd', attn, v)
            ao = ao.transpose(0, 2, 1, 3).reshape(bsz, seq, d)
            attn_out = ao @ Wo + bo
            x1 = _layernorm(x + attn_out, g1, be1)
            gate_logits = x1 @ Wg + bg
            gate_probs = jax.nn.softmax(gate_logits, axis=-1)
            topk_p, topk_i = jax.lax.top_k(gate_probs, K)
            topk_p = topk_p / jnp.sum(topk_p, axis=-1, keepdims=True)
            comb = jnp.sum(jax.nn.one_hot(topk_i, E, dtype=x.dtype) * topk_p[..., None], axis=-2)
            h = jax.nn.gelu(jnp.einsum('bsd,edf->bsef', x1, W1) + b1, approximate=False)
            y = jnp.einsum('bsef,efd->bsed', h, W2) + b2
            moe_out = jnp.einsum('bse,bsed->bsd', comb, y)
            return _layernorm(x1 + moe_out, g2, be2)
        key = jax.random.key(seed)
        ks = jax.random.split(key, 20)
        std = 0.02
        p = lambda k, sh: jax.random.normal(k, sh, dtype=jnp.float32) * std
        return {'x': jax.random.normal(ks[0], (B, S, D), dtype=jnp.float32), 'Wq': p(ks[1], (D, D)), 'bq': jnp.zeros((D,), jnp.float32), 'Wk': p(ks[2], (D, D)), 'bk': jnp.zeros((D,), jnp.float32), 'Wv': p(ks[3], (D, D)), 'bv': jnp.zeros((D,), jnp.float32), 'Wo': p(ks[4], (D, D)), 'bo': jnp.zeros((D,), jnp.float32), 'Wg': p(ks[5], (D, E)), 'bg': jnp.zeros((E,), jnp.float32), 'W1': p(ks[6], (E, D, FF)), 'b1': jnp.zeros((E, FF), jnp.float32), 'W2': p(ks[7], (E, FF, D)), 'b2': jnp.zeros((E, D), jnp.float32), 'g1': jnp.ones((D,), jnp.float32), 'be1': jnp.zeros((D,), jnp.float32), 'g2': jnp.ones((D,), jnp.float32), 'be2': jnp.zeros((D,), jnp.float32)}
    _L1_ffn_in = _L1_ffn_setup()
    _d = {'L0_attn_x': _L0_attn_in['x'], 'L0_attn_ln1_g': _L0_attn_in['ln1_g'], 'L0_attn_ln1_b': _L0_attn_in['ln1_b'], 'L0_attn_Wq': _L0_attn_in['Wq'], 'L0_attn_bq': _L0_attn_in['bq'], 'L0_attn_Wk': _L0_attn_in['Wk'], 'L0_attn_bk': _L0_attn_in['bk'], 'L0_attn_Wv': _L0_attn_in['Wv'], 'L0_attn_bv': _L0_attn_in['bv'], 'L0_attn_Wg': _L0_attn_in['Wg'], 'L0_attn_bg': _L0_attn_in['bg'], 'L0_attn_decay_logit': _L0_attn_in['decay_logit'], 'L0_attn_Wo': _L0_attn_in['Wo'], 'L0_attn_bo': _L0_attn_in['bo'], 'L0_attn_ln2_g': _L0_attn_in['ln2_g'], 'L0_attn_ln2_b': _L0_attn_in['ln2_b'], 'L0_attn_W1': _L0_attn_in['W1'], 'L0_attn_b1': _L0_attn_in['b1'], 'L0_attn_W2': _L0_attn_in['W2'], 'L0_attn_b2': _L0_attn_in['b2'], 'L0_ffn_Wg': _L0_ffn_in['Wg'], 'L0_ffn_bg': _L0_ffn_in['bg'], 'L0_ffn_bias': _L0_ffn_in['bias'], 'L0_ffn_W1': _L0_ffn_in['W1'], 'L0_ffn_b1': _L0_ffn_in['b1'], 'L0_ffn_W2': _L0_ffn_in['W2'], 'L0_ffn_b2': _L0_ffn_in['b2'], 'L1_attn_Wq': _L1_attn_in['Wq'], 'L1_attn_bq': _L1_attn_in['bq'], 'L1_attn_Wk': _L1_attn_in['Wk'], 'L1_attn_bk': _L1_attn_in['bk'], 'L1_attn_Wv': _L1_attn_in['Wv'], 'L1_attn_bv': _L1_attn_in['bv'], 'L1_attn_Wo': _L1_attn_in['Wo'], 'L1_attn_bo': _L1_attn_in['bo'], 'L1_ffn_Wq': _L1_ffn_in['Wq'], 'L1_ffn_bq': _L1_ffn_in['bq'], 'L1_ffn_Wk': _L1_ffn_in['Wk'], 'L1_ffn_bk': _L1_ffn_in['bk'], 'L1_ffn_Wv': _L1_ffn_in['Wv'], 'L1_ffn_bv': _L1_ffn_in['bv'], 'L1_ffn_Wo': _L1_ffn_in['Wo'], 'L1_ffn_bo': _L1_ffn_in['bo'], 'L1_ffn_Wg': _L1_ffn_in['Wg'], 'L1_ffn_bg': _L1_ffn_in['bg'], 'L1_ffn_W1': _L1_ffn_in['W1'], 'L1_ffn_b1': _L1_ffn_in['b1'], 'L1_ffn_W2': _L1_ffn_in['W2'], 'L1_ffn_b2': _L1_ffn_in['b2'], 'L1_ffn_g1': _L1_ffn_in['g1'], 'L1_ffn_be1': _L1_ffn_in['be1'], 'L1_ffn_g2': _L1_ffn_in['g2'], 'L1_ffn_be2': _L1_ffn_in['be2']}
    _x0 = _d['L0_attn_x']
    _d['L0_attn_x'] = jax.random.normal(jax.random.fold_in(jax.random.key(seed), 1), (4, 1024, 128), dtype=_x0.dtype)
    del _x0
    return _d

def reference(L0_attn_x, L0_attn_ln1_g, L0_attn_ln1_b, L0_attn_Wq, L0_attn_bq, L0_attn_Wk, L0_attn_bk, L0_attn_Wv, L0_attn_bv, L0_attn_Wg, L0_attn_bg, L0_attn_decay_logit, L0_attn_Wo, L0_attn_bo, L0_attn_ln2_g, L0_attn_ln2_b, L0_attn_W1, L0_attn_b1, L0_attn_W2, L0_attn_b2, L0_ffn_Wg, L0_ffn_bg, L0_ffn_bias, L0_ffn_W1, L0_ffn_b1, L0_ffn_W2, L0_ffn_b2, L1_attn_Wq, L1_attn_bq, L1_attn_Wk, L1_attn_bk, L1_attn_Wv, L1_attn_bv, L1_attn_Wo, L1_attn_bo, L1_ffn_Wq, L1_ffn_bq, L1_ffn_Wk, L1_ffn_bk, L1_ffn_Wv, L1_ffn_bv, L1_ffn_Wo, L1_ffn_bo, L1_ffn_Wg, L1_ffn_bg, L1_ffn_W1, L1_ffn_b1, L1_ffn_W2, L1_ffn_b2, L1_ffn_g1, L1_ffn_be1, L1_ffn_g2, L1_ffn_be2):

    def _L0_attn_ref(x, ln1_g, ln1_b, Wq, bq, Wk, bk, Wv, bv, Wg, bg, decay_logit, Wo, bo, ln2_g, ln2_b, W1, b1, W2, b2):
        import jax, jax.numpy as jnp
        import numpy as np
        D_MODEL = 128
        H = 16
        DH = 64
        EPS = 1e-05

        def _layernorm(x, g, b):
            mu = jnp.mean(x, axis=-1, keepdims=True)
            var = jnp.var(x, axis=-1, keepdims=True)
            return (x - mu) * jax.lax.rsqrt(var + EPS) * g + b
        B, L, _ = x.shape
        y = _layernorm(x, ln1_g, ln1_b)

        def proj(W, b):
            return (y @ W + b).reshape(B, L, H, DH).transpose(1, 0, 2, 3)
        q = proj(Wq, bq)
        k = proj(Wk, bk)
        v = proj(Wv, bv)
        g = jax.nn.sigmoid(y @ Wg + bg).reshape(B, L, H, DH).transpose(1, 0, 2, 3)
        decay = jax.nn.sigmoid(decay_logit)[None, :, None]
        scale = DH ** (-0.5)

        def step(state, qkvg):
            q_t, k_t, v_t, g_t = qkvg
            state = decay * state + k_t * v_t
            out_t = g_t * q_t * state * scale
            return (state, out_t)
        state0 = jnp.zeros((B, H, DH), x.dtype)
        _, outs = jax.lax.scan(step, state0, (q, k, v, g))
        o = outs.transpose(1, 0, 2, 3).reshape(B, L, H * DH) @ Wo + bo
        x2 = x + o
        h = _layernorm(x2, ln2_g, ln2_b)
        ff = jax.nn.gelu(h @ W1 + b1, approximate=False) @ W2 + b2
        return x2 + ff

    def _L0_ffn_ref(x, Wg, bg, bias, W1, b1, W2, b2):
        import jax, jax.numpy as jnp
        import numpy as np
        D_MODEL, EXPERT_DIM, NUM_EXPERTS, TOP_K = (128, 256, 16, 2)
        SEQ_LEN, BATCH = (256, 2)
        logits = jnp.einsum('sbd,de->sbe', x, Wg) + bg + bias
        vals, idx = jax.lax.top_k(logits, TOP_K)
        w = jax.nn.softmax(vals - jnp.max(vals, axis=-1, keepdims=True), axis=-1)
        cw = jnp.einsum('sbk,sbke->sbe', w, jax.nn.one_hot(idx, NUM_EXPERTS, dtype=x.dtype))
        h = jax.nn.relu(jnp.einsum('sbd,edh->esbh', x, W1) + b1[:, None, None, :])
        y = jnp.einsum('esbh,ehd->esbd', h, W2) + b2[:, None, None, :]
        out = jnp.einsum('esbd,sbe->sbd', y, cw)
        return out

    def _L1_attn_ref(x, Wq, bq, Wk, bk, Wv, bv, Wo, bo):
        import jax, jax.numpy as jnp
        import numpy as np
        EMBED = 128
        HEADS = 16
        HEAD_DIM = EMBED // HEADS
        B, T = (2, 256)
        ROPE_THETA = 10000.0

        def _rope(x):
            D = x.shape[-1]
            inv_freq = 1.0 / ROPE_THETA ** (jnp.arange(0, D, 2, dtype=jnp.float32) / D)
            freqs = jnp.arange(x.shape[2], dtype=jnp.float32)[:, None] * inv_freq[None, :]
            cos = jnp.cos(freqs).astype(x.dtype)
            sin = jnp.sin(freqs).astype(x.dtype)
            x1, x2 = (x[..., :D // 2], x[..., D // 2:])
            return jnp.concatenate([x1 * cos - x2 * sin, x2 * cos + x1 * sin], axis=-1)
        Bb, Tt, C = x.shape
        H, D = (HEADS, HEAD_DIM)

        def proj(W, b):
            return (jnp.einsum('btc,oc->bto', x, W) + b).reshape(Bb, Tt, H, D).transpose(0, 2, 1, 3)
        q = _rope(proj(Wq, bq))
        k = _rope(proj(Wk, bk))
        v = proj(Wv, bv)
        scale = jnp.sqrt(jnp.asarray(D, dtype=x.dtype))
        scores = jnp.einsum('bhtd,bhsd->bhts', q, k) / scale
        attn = jax.nn.softmax(scores, axis=-1)
        out = jnp.einsum('bhts,bhsd->bhtd', attn, v)
        out = out.transpose(0, 2, 1, 3).reshape(Bb, Tt, C)
        return jnp.einsum('btc,oc->bto', out, Wo) + bo

    def _L1_ffn_ref(x, Wq, bq, Wk, bk, Wv, bv, Wo, bo, Wg, bg, W1, b1, W2, b2, g1, be1, g2, be2):
        import jax, jax.numpy as jnp
        import numpy as np
        from math import sqrt
        B, S, D, H, E, K, FF = (2, 128, 128, 16, 8, 2, 512)
        HD = D // H
        EPS = 1e-05

        def _rope_cache(seq_len, hd):
            inv_freq = 1.0 / 10000.0 ** (jnp.arange(0, hd, 2, dtype=jnp.float32) / hd)
            t = jnp.arange(seq_len, dtype=jnp.float32)
            freqs = t[:, None] * inv_freq[None, :]
            emb = jnp.concatenate([freqs, freqs], axis=-1)
            return (jnp.cos(emb), jnp.sin(emb))

        def _rotate_half(x):
            x1, x2 = jnp.split(x, 2, axis=-1)
            return jnp.concatenate([-x2, x1], axis=-1)

        def _layernorm(x, g, b):
            m = jnp.mean(x, axis=-1, keepdims=True)
            v = jnp.var(x, axis=-1, keepdims=True)
            return (x - m) * jax.lax.rsqrt(v + EPS) * g + b

        def _forward(x, Wq, bq, Wk, bk, Wv, bv, Wo, bo, Wg, bg, W1, b1, W2, b2, g1, be1, g2, be2):
            bsz, seq, d = x.shape
            q = (x @ Wq + bq).reshape(bsz, seq, H, HD).transpose(0, 2, 1, 3)
            k = (x @ Wk + bk).reshape(bsz, seq, H, HD).transpose(0, 2, 1, 3)
            v = (x @ Wv + bv).reshape(bsz, seq, H, HD).transpose(0, 2, 1, 3)
            cos, sin = _rope_cache(seq, HD)
            cos = cos[None, None]
            sin = sin[None, None]
            q = q * cos + _rotate_half(q) * sin
            k = k * cos + _rotate_half(k) * sin
            scores = jnp.einsum('bhqd,bhkd->bhqk', q, k) / sqrt(HD)
            attn = jax.nn.softmax(scores, axis=-1)
            ao = jnp.einsum('bhqk,bhkd->bhqd', attn, v)
            ao = ao.transpose(0, 2, 1, 3).reshape(bsz, seq, d)
            attn_out = ao @ Wo + bo
            x1 = _layernorm(x + attn_out, g1, be1)
            gate_logits = x1 @ Wg + bg
            gate_probs = jax.nn.softmax(gate_logits, axis=-1)
            topk_p, topk_i = jax.lax.top_k(gate_probs, K)
            topk_p = topk_p / jnp.sum(topk_p, axis=-1, keepdims=True)
            comb = jnp.sum(jax.nn.one_hot(topk_i, E, dtype=x.dtype) * topk_p[..., None], axis=-2)
            h = jax.nn.gelu(jnp.einsum('bsd,edf->bsef', x1, W1) + b1, approximate=False)
            y = jnp.einsum('bsef,efd->bsed', h, W2) + b2
            moe_out = jnp.einsum('bse,bsed->bsd', comb, y)
            return _layernorm(x1 + moe_out, g2, be2)
        return _forward(x, Wq, bq, Wk, bk, Wv, bv, Wo, bo, Wg, bg, W1, b1, W2, b2, g1, be1, g2, be2)
    x = L0_attn_x
    x = x + _L0_attn_ref(_layernorm(x, axis=-1), L0_attn_ln1_g, L0_attn_ln1_b, L0_attn_Wq, L0_attn_bq, L0_attn_Wk, L0_attn_bk, L0_attn_Wv, L0_attn_bv, L0_attn_Wg, L0_attn_bg, L0_attn_decay_logit, L0_attn_Wo, L0_attn_bo, L0_attn_ln2_g, L0_attn_ln2_b, L0_attn_W1, L0_attn_b1, L0_attn_W2, L0_attn_b2)
    x = x + _L0_ffn_ref(_layernorm(x, axis=-1), L0_ffn_Wg, L0_ffn_bg, L0_ffn_bias, L0_ffn_W1, L0_ffn_b1, L0_ffn_W2, L0_ffn_b2)
    x = x + _L1_attn_ref(_layernorm(x, axis=-1), L1_attn_Wq, L1_attn_bq, L1_attn_Wk, L1_attn_bk, L1_attn_Wv, L1_attn_bv, L1_attn_Wo, L1_attn_bo)
    x = x + _L1_ffn_ref(_layernorm(x, axis=-1), L1_ffn_Wq, L1_ffn_bq, L1_ffn_Wk, L1_ffn_bk, L1_ffn_Wv, L1_ffn_bv, L1_ffn_Wo, L1_ffn_bo, L1_ffn_Wg, L1_ffn_bg, L1_ffn_W1, L1_ffn_b1, L1_ffn_W2, L1_ffn_b2, L1_ffn_g1, L1_ffn_be1, L1_ffn_g2, L1_ffn_be2)
    return x

_drawn_inputs = setup_inputs


def setup_inputs(seed=0):
    import zlib

    import numpy as np

    out = dict(_drawn_inputs(seed))
    spreads = {'L0_attn_ln1_g': (1.0, 0.6),
     'L0_attn_ln1_b': (0.0, 0.8),
     'L0_attn_bq': (0.0, 0.8),
     'L0_attn_bk': (0.0, 0.8),
     'L0_attn_bv': (0.0, 0.8),
     'L0_attn_bg': (0.0, 0.8),
     'L0_attn_decay_logit': (0.0, 0.8),
     'L0_attn_bo': (0.0, 0.8),
     'L0_attn_ln2_g': (1.0, 0.6),
     'L0_attn_ln2_b': (0.0, 2.0),
     'L0_attn_b1': (0.0, 2.0),
     'L0_attn_b2': (0.0, 0.8),
     'L0_ffn_bias': (0.0, 0.8),
     'L1_attn_bq': (0.0, 2.0),
     'L1_attn_bk': (0.0, 2.0),
     'L1_attn_bv': (0.0, 0.8),
     'L1_attn_bo': (0.0, 0.8),
     'L1_ffn_bq': (0.0, 2.0),
     'L1_ffn_bk': (0.0, 2.0),
     'L1_ffn_bv': (0.0, 0.8),
     'L1_ffn_bo': (0.0, 2.0),
     'L1_ffn_bg': (0.0, 0.47),
     'L1_ffn_b1': (0.0, 2.0),
     'L1_ffn_b2': (0.0, 2.0),
     'L1_ffn_g1': (1.0, 0.6),
     'L1_ffn_be1': (0.0, 0.727),
     'L1_ffn_g2': (1.0, 0.6),
     'L1_ffn_be2': (0.0, 0.8)}
    factors = {'L0_attn_Wq': 8.0,
     'L0_attn_Wk': 8.0,
     'L0_attn_Wv': 8.0,
     'L0_attn_Wg': 8.0,
     'L0_attn_Wo': 8.0,
     'L0_ffn_b1': 58.368,
     'L0_ffn_b2': 33.172,
     'L1_ffn_Wq': 8.0,
     'L1_ffn_Wk': 8.0,
     'L1_ffn_Wv': 8.0,
     'L1_ffn_Wo': 7.88,
     'L1_ffn_W1': 4.466,
     'L1_ffn_W2': 4.006,
     'L0_attn_W1': 8.0,
     'L0_attn_W2': 5.431,
     'L0_ffn_Wg': 4.359,
     'L0_ffn_bg': 8.0,
     'L0_ffn_W1': 6.171,
     'L0_ffn_W2': 4.4,
     'L1_attn_Wq': 8.0,
     'L1_attn_Wk': 8.0,
     'L1_attn_Wv': 3.536,
     'L1_attn_Wo': 3.11}
    for name, (base, spread) in spreads.items():
        noise = np.random.default_rng([zlib.crc32(name.encode()), seed]).standard_normal(out[name].shape)
        drawn = base * np.exp(spread * noise) if base else spread * noise
        out[name] = jnp.asarray(drawn.astype(out[name].dtype))
    for name, factor in factors.items():
        out[name] = (out[name] * factor).astype(out[name].dtype)
    return out
```

```python
import numpy as np
import concourse.bass as bass
from concourse import mybir
from contextlib import ExitStack, contextmanager

F32 = mybir.dt.float32
F32R = mybir.dt.float32r
U32 = mybir.dt.uint32
ALU = mybir.AluOpType
ACT = mybir.ActivationFunctionType
AX = mybir.AxisListType

B, L, D = 4, 1024, 128
P = 128
NT = L // P
HALF = 512
NH = L // HALF
TPH = HALF // P
CH = 16 * 64 // P
FF = 512 // P
HEADS, DH = 16, 8
GH = 4
NG = HEADS // GH
GR = GH * DH
VW = 32
EPS = 1e-5

COLS, at = {}, 0
for name, n in (("ln1_g", 1), ("ln1_b", 1), ("bq", CH), ("bk", CH), ("bv", CH), ("bg", CH), ("decay", CH),
                ("ln2_g", 1), ("ln2_b", 1), ("b1", FF), ("moe0_b1", 32), ("moe1_b1", 32),
                ("att0_bq", 1), ("att0_bk", 1), ("att0_bqr", 1), ("att0_bkr", 1),
                ("att1_bq", 1), ("att1_bk", 1), ("att1_bqr", 1), ("att1_bkr", 1), ("head_mask", GH)):
    COLS[name] = (at, at + n)
    at += n
NCOLS = at
ROWS = {name: i for i, name in enumerate(("bo", "b2", "att0_bv", "att0_bo", "att1_bv", "att1_bo",
                                          "g1", "be1", "g2", "be2"))}
GATES = {name: i for i, name in enumerate(("moe0_bg", "moe0_bias", "moe1_bg", "iota"))}


@contextmanager
def stage(nc, *names):
    with ExitStack() as ctx:
        sems = [ctx.enter_context(nc.semaphore(n)) for n in names]
        with nc.Block() as block:
            yield (block, *sems)
        for s in sems:
            nc.gpsimd.sem_clear(s)
        nc.all_engine_barrier()


def chain(eng, sem):
    done = [0]

    def link(ins):
        done[0] += 1
        ins.then_inc(sem, 1)
        eng.wait_ge(sem, done[0])

    return link


def normalise(nc, t, src, dst, dst_t=None, gain=None, shift=None, row_gain=None, row_shift=None, add=None):
    with stage(nc, "dve_step", "var_ready", "std_ready", "tile_ready", "turned", "turned_used") as \
            (block, dve_step, var_ready, std_ready, tile_ready, turned, turned_used):
        @block.vector
        def _(dve):
            link = chain(dve, dve_step)
            if add is not None:
                link(dve.tensor_tensor(src[:, :, :], add[0], add[1], ALU.add))
            for i in range(NT):
                last = dve.bn_stats(t["stats"][:, i, :], src[:, i, :])
            link(last)
            for i in range(NT):
                last = dve.bn_aggr(t["mv"][:, i, :], t["stats"][:, i, :])
            link(last)
            dve.tensor_scalar(t["var"][:, :], t["mv"][:, :, 1], EPS, None, ALU.add).then_inc(var_ready, 1)
            dve.wait_ge(std_ready, 1)
            link(dve.reciprocal(t["rstd"][:, :], t["std"][:, :]))
            link(dve.tensor_tensor(t["tmp"][:, :], t["rstd"][:, :], t["rstd"][:, :], ALU.mult))
            link(dve.tensor_tensor(t["tmp"][:, :], t["tmp"][:, :], t["var"][:, :], ALU.mult))
            link(dve.tensor_scalar(t["tmp"][:, :], t["tmp"][:, :], -0.5, 1.5, ALU.mult, ALU.add))
            link(dve.tensor_tensor(t["rstd"][:, :], t["rstd"][:, :], t["tmp"][:, :], ALU.mult))
            for i in range(NT):
                last = dve.tensor_scalar(dst[:, i, :], src[:, i, :], t["mv"][:, i, 0:1], t["rstd"][:, i:i + 1],
                                         ALU.subtract, ALU.mult)
                if row_gain is None:
                    last.then_inc(tile_ready, 1)
            if row_gain is not None:
                link(last)
                link(dve.tensor_tensor(dst[:, :, :], dst[:, :, :], row_gain, ALU.mult))
                dve.tensor_tensor(dst[:, :, :], dst[:, :, :], row_shift, ALU.add).then_inc(tile_ready, NT)

        @block.scalar
        def _(act):
            act.wait_ge(var_ready, 1)
            act.activation(t["std"][:, :], t["var"][:, :], ACT.Sqrt).then_inc(std_ready, 1)
            if dst_t is None:
                return
            for h in range(NH):
                act.wait_ge(turned, TPH * (h + 1))
                out, bank = dst_t[:, h * HALF:(h + 1) * HALF], t["psum"][:, h, :]
                if gain is None:
                    act.activation(out, bank, ACT.Copy)
                else:
                    act.activation(out, bank, ACT.Identity, scale=gain, bias=shift)

        @block.tensor
        def _(pe):
            if dst_t is None:
                return
            for i in range(NT):
                pe.wait_ge(tile_ready, i + 1)
                pe.transpose(t["psum"][:, i // TPH, (i % TPH) * P:(i % TPH + 1) * P], dst[:, i, :],
                             t["ident"][:, :]).then_inc(turned, 1)


def recurrence(nc, t, w):
    units = [(c, h) for c in range(CH) for h in range(NH)]
    NB, LAG, BANKS = 3, 2, 6
    psum, col, y_t = t["psum"], t["col"], t["y_t"]
    with stage(nc, "proj_done", "act_used", "dve_used", "scanned", "gated", "out_done", "moe_loaded",
               "x_added") as \
            (block, proj_done, act_used, dve_used, scanned, gated, out_done, moe_loaded, x_added):
        @block.sync
        def _(sp):
            w.load_moe(sp, 0, moe_loaded)
            sp.wait_ge(moe_loaded, 32)

        @block.tensor
        def _(pe):
            def project(u):
                c, h = units[u]
                for i, m in enumerate((w.v, w.k, w.g, w.q)):
                    n = 4 * u + i
                    if n >= BANKS:
                        u0, i0 = divmod(n - BANKS, 4)
                        pe.wait_ge(dve_used if i0 % 2 else act_used, 2 * u0 + i0 // 2 + 1)
                    pe.matmul(psum[:, n % BANKS, :], m[:, c * P:(c + 1) * P], y_t[:, h * HALF:(h + 1) * HALF],
                              start=True, stop=True).then_inc(proj_done, 1)

            def output(u):
                c, h = units[u]
                pe.wait_ge(gated, u + 1)
                for i in range(TPH):
                    last = pe.matmul(psum[:, BANKS + h, i * P:(i + 1) * P], t["gated"][:, u % NB, i * P:(i + 1) * P],
                                     w.o[:, c, :], start=(c == 0 and i == 0), stop=(c == CH - 1),
                                     skip_group_check=True)
                last.then_inc(out_done, 1)

            for u in range(len(units) + LAG):
                if u < len(units):
                    project(u)
                if u >= LAG:
                    output(u - LAG)

        @block.scalar
        def _(act):
            for u, (c, h) in enumerate(units):
                act.wait_ge(proj_done, 4 * u + 1)
                if u >= 2:
                    act.wait_ge(dve_used, 2 * (u - 2) + 1)
                act.activation(t["v"][:, u % 2, :], psum[:, 4 * u % BANKS, :], ACT.Identity,
                               bias=col("bv", c)).then_inc(act_used, 1)
                act.wait_ge(proj_done, 4 * u + 3)
                if u >= 2:
                    act.wait_ge(dve_used, 2 * (u - 2) + 2)
                act.activation(t["g"][:, u % 2, :], psum[:, (4 * u + 2) % BANKS, :], ACT.Sigmoid,
                               bias=col("bg", c)).then_inc(act_used, 1)

        @block.vector
        def _(dve):
            for u, (c, h) in enumerate(units):
                dve.wait_ge(proj_done, 4 * u + 2)
                dve.wait_ge(act_used, 2 * u + 1)
                dve.scalar_tensor_tensor(t["kv"][:, u % 2, :], psum[:, (4 * u + 1) % BANKS, :], col("bk", c),
                                         t["v"][:, u % 2, :], ALU.add, ALU.mult).then_inc(dve_used, 1)
                dve.wait_ge(dve_used, 2 * u + 1)
                if u >= 2:
                    dve.wait_ge(gated, u - 1)
                if h:
                    dve.wait_ge(scanned, u)
                start = t["state"][:, (u - 1) % 2, HALF - 1:HALF] if h else 0.0
                dve.tensor_tensor_scan(t["state"][:, u % 2, :], t["decay"][:, c:c + 1].to_broadcast([P, HALF]),
                                       t["kv"][:, u % 2, :], start, ALU.mult, ALU.add).then_inc(scanned, 1)
                dve.wait_ge(proj_done, 4 * u + 4)
                dve.wait_ge(act_used, 2 * u + 2)
                dve.scalar_tensor_tensor(t["qg"][:, u % 2, :], psum[:, (4 * u + 3) % BANKS, :], col("bq", c),
                                         t["g"][:, u % 2, :], ALU.add, ALU.mult).then_inc(dve_used, 1)
            dve.wait_ge(x_added, 1)
            for h in range(NH):
                dve.wait_ge(out_done, len(units) - NH + h + 1)
                s = slice(h * TPH, (h + 1) * TPH)
                dve.scalar_tensor_tensor(t["x2"][:, s, :], psum[:, BANKS + h, :].rearrange("p (a d) -> p a d", d=D),
                                         64 ** -0.5, t["x2"][:, s, :], ALU.mult, ALU.add)

        @block.gpsimd
        def _(pool):
            pool.tensor_tensor(t["x2"][:, :, :], t["xn"][:, :, :], t["row"]("bo"), ALU.add).then_inc(x_added, 1)
            for u in range(len(units)):
                pool.wait_ge(scanned, u + 1)
                pool.wait_ge(dve_used, 2 * u + 2)
                if u >= NB:
                    pool.wait_ge(out_done, u - NB + 1)
                pool.tensor_tensor(t["gated"][:, u % NB, :], t["state"][:, u % 2, :], t["qg"][:, u % 2, :],
                                   ALU.mult).then_inc(gated, 1)


def feed_forward(nc, t, w):
    psum, col = t["psum"], t["col"]
    with stage(nc, "hidden", "gelued", "out_done", "x_step") as (block, hidden, gelued, out_done, x_step):
        @block.tensor
        def _(pe):
            for n in range(FF * NH):
                f, h = n // NH, n % NH
                if n >= 6:
                    pe.wait_ge(gelued, n - 5)
                pe.matmul(psum[:, n % 6, :], w.w1[:, f * P:(f + 1) * P], t["y_t"][:, h * HALF:(h + 1) * HALF],
                          start=True, stop=True).then_inc(hidden, 1)
            pe.wait_ge(gelued, FF * NH)
            for i in range(NT):
                for f in range(FF):
                    last = pe.matmul(psum[:, 6 + i // TPH, (i % TPH) * P:(i % TPH + 1) * P],
                                     t["ffh"][:, f, i * P:(i + 1) * P], w.w2[:, f, :],
                                     start=(f == 0), stop=(f == FF - 1))
                last.then_inc(out_done, 1)

        @block.scalar
        def _(act):
            for n in range(FF * NH):
                f, h = n // NH, n % NH
                act.wait_ge(hidden, n + 1)
                act.activation(t["ffh"][:, f, h * HALF:(h + 1) * HALF], psum[:, n % 6, :], ACT.Gelu,
                               bias=col("b1", f)).then_inc(gelued, 1)

        @block.gpsimd
        def _(pool):
            link = chain(pool, x_step)
            link(pool.tensor_tensor(t["x"][:, :, :], t["x"][:, :, :], t["x2"][:, :, :], ALU.add))
            link(pool.tensor_tensor(t["x"][:, :, :], t["x"][:, :, :], t["row"]("b2"), ALU.add))

        @block.vector
        def _(dve):
            dve.wait_ge(x_step, 2)
            for h in range(NH):
                dve.wait_ge(out_done, TPH * (h + 1))
                s = slice(h * TPH, (h + 1) * TPH)
                dve.tensor_tensor(t["x"][:, s, :], psum[:, 6 + h, :].rearrange("p (a d) -> p a d", d=D),
                                  t["x"][:, s, :], ALU.add)


def gate(nc, t, w, layer, E):
    psum = t["psum"]
    lg, mx, ix, sel, wt, cw, eq = (t[k] for k in ("lg", "mx8", "ix8", "ixf", "wt", "cw", "eq"))
    L3 = [P, NT, E]
    with stage(nc, "logits", "step", "to_exp", "exped", "cw_ready", "turned", "turned_used", "acc_done") as \
            (block, logits, step, to_exp, exped, cw_ready, turned, turned_used, acc_done):
        @block.tensor
        def _(pe):
            for i in range(NT):
                last = pe.matmul(psum[:, 0, i * E:(i + 1) * E], t["y_t"][:, i * P:(i + 1) * P],
                                 w.gate[layer][:, 0:E], start=True, stop=True)
            last.then_inc(logits, 1)
            pe.wait_ge(cw_ready, 1)
            for i in range(NT):
                last = pe.transpose(psum[0:E, 1 + i // TPH, (i % TPH) * P:(i % TPH + 1) * P], cw[:, i, 0:E],
                                    t["ident"][:, :])
            last.then_inc(turned, 1)
            pe.wait_ge(turned_used, 1)
            for i in range(NT):
                last = pe.matmul(psum[:, 3 + i // TPH, (i % TPH) * P:(i % TPH + 1) * P], t["cw_t"][0:E, i * P:(i + 1) * P],
                                 w.b2[layer][0:E, :], start=True, stop=True)
            last.then_inc(acc_done, 1)

        @block.scalar
        def _(act):
            act.wait_ge(to_exp, 1)
            if layer == 0:
                act.activation(wt[:, :, 1], eq[:, :, 0], ACT.Exp).then_inc(exped, 1)
            else:
                act.activation(lg[:, :, 0:E], lg[:, :, 0:E], ACT.Exp).then_inc(exped, 1)

        @block.vector
        def _(dve):
            link = chain(dve, step)
            v = lg[:, :, 0:E]
            dve.wait_ge(logits, 1)
            link(dve.tensor_tensor(v, psum[:, 0, 0:NT * E].rearrange("p (t e) -> p t e", e=E),
                                   t["grow"](f"moe{layer}_bg", E), ALU.add))
            if layer == 0:
                link(dve.tensor_tensor(v, v, t["grow"]("moe0_bias", E), ALU.add))
            else:
                link(dve.tensor_reduce(wt[:, :, 0], v, AX.X, ALU.max))
                dve.tensor_tensor(v, v, wt[:, :, 0:1].to_broadcast(L3), ALU.subtract).then_inc(to_exp, 1)
                dve.wait_ge(exped, 1)
                link(dve.tensor_reduce(wt[:, :, 0], v, AX.X, ALU.add))
                link(dve.reciprocal(wt[:, :, 1], wt[:, :, 0]))
                link(dve.tensor_tensor(v, v, wt[:, :, 1:2].to_broadcast(L3), ALU.mult))
            for i in range(NT):
                last = dve.max(mx[:, i, :], lg[:, i, 0:E])
            link(last)
            for i in range(NT):
                last = dve.max_index(ix[:, i, :], mx[:, i, :], lg[:, i, 0:E])
            link(last)
            link(dve.tensor_copy(sel[:, :, :], ix[:, :, 0:2]))
            if layer == 0:
                dve.tensor_tensor(eq[:, :, 0], mx[:, :, 1], mx[:, :, 0], ALU.subtract).then_inc(to_exp, 1)
                dve.wait_ge(exped, 1)
                link(dve.tensor_scalar(eq[:, :, 0], wt[:, :, 1], 1.0, None, ALU.add))
                link(dve.reciprocal(wt[:, :, 0], eq[:, :, 0]))
                link(dve.tensor_tensor(wt[:, :, 1], wt[:, :, 1], wt[:, :, 0], ALU.mult))
            else:
                link(dve.tensor_tensor(eq[:, :, 0], mx[:, :, 0], mx[:, :, 1], ALU.add))
                link(dve.reciprocal(eq[:, :, 1], eq[:, :, 0]))
                link(dve.tensor_tensor(wt[:, :, :], mx[:, :, 0:2], eq[:, :, 1:2].to_broadcast([P, NT, 2]), ALU.mult))
            iota = t["grow"]("iota", E)
            link(dve.tensor_tensor(cw[:, :, 0:E], iota, sel[:, :, 0:1].to_broadcast(L3), ALU.is_equal))
            link(dve.tensor_tensor(cw[:, :, 0:E], cw[:, :, 0:E], wt[:, :, 0:1].to_broadcast(L3), ALU.mult))
            link(dve.tensor_tensor(eq[:, :, 0:E], iota, sel[:, :, 1:2].to_broadcast(L3), ALU.is_equal))
            link(dve.tensor_tensor(eq[:, :, 0:E], eq[:, :, 0:E], wt[:, :, 1:2].to_broadcast(L3), ALU.mult))
            dve.tensor_tensor(cw[:, :, 0:E], cw[:, :, 0:E], eq[:, :, 0:E], ALU.add).then_inc(cw_ready, 1)
            dve.wait_ge(turned, 1)
            dve.tensor_copy(t["cw_t"][0:E, :], psum[0:E, 1:3, :].rearrange("p a d -> p (a d)")).then_inc(turned_used, 1)
            dve.wait_ge(acc_done, 1)
            dve.tensor_copy(t["acc"][:, :, :], psum[:, 3:5, :].rearrange("p a (t d) -> p (a t) d", d=D))


def experts(nc, t, w, layer, E, F, func):
    psum, col, acc, cw = t["psum"], t["col"], t["acc"], t["cw"]
    units = [(e, h) for e in range(E) for h in range(NH)]
    BANKS = 6
    with stage(nc, "hidden", "activated", "y_done", "y_used") as (block, hidden, activated, y_done, y_used):
        @block.tensor
        def _(pe):
            def up(u):
                e, h = units[u]
                for f in range(F):
                    n = u * F + f
                    if n >= BANKS:
                        pe.wait_ge(activated, n - BANKS + 1)
                    c = (e * F + f) * P
                    pe.matmul(psum[:, n % BANKS, :], w.m1[:, c:c + P], t["y_t"][:, h * HALF:(h + 1) * HALF],
                              start=True, stop=True).then_inc(hidden, 1)

            def down(u):
                e, h = units[u]
                pe.wait_ge(activated, F * (u + 1))
                if u >= 2:
                    pe.wait_ge(y_used, TPH * (u - 1))
                for i in range(TPH):
                    for f in range(F):
                        c = (e * F + f) * P
                        last = pe.matmul(psum[:, BANKS + u % 2, i * P:(i + 1) * P],
                                         t["moe_h"][:, u % 2, f, i * P:(i + 1) * P], w.m2[:, c:c + P],
                                         start=(f == 0), stop=(f == F - 1))
                    last.then_inc(y_done, 1)

            up(0)
            for u in range(len(units)):
                if u + 1 < len(units):
                    up(u + 1)
                down(u)

        @block.scalar
        def _(act):
            for u, (e, h) in enumerate(units):
                if u >= 2:
                    act.wait_ge(y_done, TPH * (u - 1))
                for f in range(F):
                    n = u * F + f
                    act.wait_ge(hidden, n + 1)
                    act.activation(t["moe_h"][:, u % 2, f, :], psum[:, n % BANKS, :], func,
                                   bias=col(f"moe{layer}_b1", e * F + f)).then_inc(activated, 1)

        @block.vector
        def _(dve):
            for u, (e, h) in enumerate(units):
                for i in range(TPH):
                    tile = h * TPH + i
                    dve.wait_ge(y_done, TPH * (u + 1))
                    if u >= NH:
                        dve.wait_ge(y_used, TPH * (u - NH) + i + 1)
                    dve.scalar_tensor_tensor(acc[:, tile, :], psum[:, BANKS + u % 2, i * P:(i + 1) * P],
                                             cw[:, tile, e:e + 1], acc[:, tile, :],
                                             ALU.mult, ALU.add).then_inc(y_used, 1)


def add_to_x(nc, t, what):
    with stage(nc, "unused") as (block, _s):
        @block.vector
        def _(dve):
            dve.tensor_tensor(t["x"][:, :, :], t["x"][:, :, :], what[:, :, :], ALU.add)


def attention_inputs(nc, t, w, layer, a):
    psum, col = t["psum"], t["col"]
    wq, wk, wqr, wkr, wv, wo = w.att[layer]
    jobs = [(k, h) for k in range(2) for h in range(NH)]
    with stage(nc, "proj_done", "rot_used", "summed", "high", "low", "v_done", "v_set", "rot_a") as \
            (block, proj_done, rot_used, summed, high, low, v_done, v_set, rot_a):
        @block.tensor
        def _(pe):
            for n, (k, h) in enumerate(jobs):
                if n >= 2:
                    pe.wait_ge(rot_used, n - 1)
                for i, m in enumerate(((wq, wqr), (wk, wkr))[k]):
                    pe.matmul(psum[:, 2 * (n % 2) + i, :], m, t["y_t"][:, h * HALF:(h + 1) * HALF],
                              start=True, stop=True).then_inc(proj_done, 1)
            for i in range(NT):
                last = pe.matmul(psum[:, 4 + i // TPH, (i % TPH) * P:(i % TPH + 1) * P], t["y_t"][:, i * P:(i + 1) * P],
                                 wv, start=True, stop=True)
                if i % TPH == TPH - 1:
                    last.then_inc(v_done, 1)

        @block.vector
        def _(dve):
            for n, (k, h) in enumerate(jobs):
                s = slice(h * HALF, (h + 1) * HALF)
                name = "qk"[k]
                dve.wait_ge(proj_done, 2 * n + 1)
                if n >= 2:
                    dve.wait_ge(summed, n - 1)
                dve.scalar_tensor_tensor(a["ra"][:, n % 2, :], psum[:, 2 * (n % 2), :], col(f"att{layer}_b{name}"),
                                         t["cos"][:, s], ALU.add, ALU.mult).then_inc(rot_a, 1)
                dve.wait_ge(proj_done, 2 * n + 2)
                dve.scalar_tensor_tensor(a["rb"][:, n % 2, :], psum[:, 2 * (n % 2) + 1, :],
                                         col(f"att{layer}_b{name}r"), t["sin"][:, s],
                                         ALU.add, ALU.mult).then_inc(rot_used, 1)
            for h in range(NH):
                dve.wait_ge(v_done, h + 1)
                ts = slice(h * TPH, (h + 1) * TPH)
                bias = t["rows"][:, ROWS[f"att{layer}_bv"], :].rearrange("p (h d) -> p h d", d=DH)
                for i in range(TPH):
                    dve.tensor_tensor(a["v"][:, h * TPH + i, :, 0:DH],
                                      psum[:, 4 + h, i * P:(i + 1) * P].rearrange("p (h d) -> p h d", d=DH),
                                      bias, ALU.add)

        @block.gpsimd
        def _(pool):
            pool.memset(a["v"][:, :, :, DH:DH + 1], 1.0)
            pool.memset(a["v"][:, :, :, DH + 1:VW], 0.0)
            for n, (k, h) in enumerate(jobs):
                pool.wait_ge(rot_a, n + 1)
                pool.wait_ge(rot_used, n + 1)
                if n >= 2:
                    pool.wait_ge(low, n - 1)
                pool.tensor_tensor(a["rot"][:, n % 2, :], a["ra"][:, n % 2, :], a["rb"][:, n % 2, :],
                                   ALU.add).then_inc(summed, 1)
                s = slice(h * HALF, (h + 1) * HALF)
                hi, lo = ((a["qh"], a["ql"]), (a["kh"], a["kl"]))[k]
                pool.wait_ge(high, n + 1)
                pool.tensor_tensor(lo[:, s], a["rot"][:, n % 2, :], hi[:, s].bitcast(F32),
                                   ALU.subtract).then_inc(low, 1)

        @block.scalar
        def _(act):
            for n, (k, h) in enumerate(jobs):
                s = slice(h * HALF, (h + 1) * HALF)
                act.wait_ge(summed, n + 1)
                act.activation((a["qh"], a["kh"])[k][:, s], a["rot"][:, n % 2, :], ACT.Copy).then_inc(high, 1)


def attention(nc, t, w, layer, a):
    psum = t["psum"]
    NQ, NKF, NP = 3, 2, 8
    UN = GH * NT
    S_BANK, M_BANK, O_BANK = 0, 4, 6
    fills = [("max", 0, u, h) for u in range(UN) for h in range(NH)]
    first = len(fills)
    per_group = []
    for g in range(NG):
        at_unit = {u: [] for u in range(-1, UN + 1)}
        at_unit[-1].append(("turn_max", g, 0, 0))
        for u in range(UN):
            if g + 1 < NG:
                at_unit[u] += [("max", g + 1, u, h) for h in range(NH)]
            if u == 3 and g >= 1:
                at_unit[u] += [("turn_out", g - 1, 0, h) for h in range(NH)]
        if g == NG - 1:
            at_unit[UN] += [("turn_out", g, 0, h) for h in range(NH)]
        per_group.append(at_unit)
        for u in range(-1, UN + 1):
            fills += at_unit[u]
    with stage(nc, "loaded0", "loaded1", "loaded2", "ext_zero", "masked", "filled", "used", "merged", "ext_set",
               "scored", "exped", "pv_done", "out_copied", "recip", "moe_loaded", "o_turned", "o_copied",
               "y_done", "x_step", "ones_set") as \
            (block, loaded0, loaded1, loaded2, ext_zero, masked, filled, used, merged, ext_set,
             scored, exped, pv_done, out_copied, recip, moe_loaded, o_turned, o_copied, y_done, x_step, ones_set):
        loaded = (loaded0, loaded1, loaded2)

        @block.sync
        def _(sp):
            for g in range(NG):
                if g == 1 and layer == 0:
                    w.load_moe(sp, 1, moe_loaded)
                if g >= NQ:
                    sp.wait_ge(scored, UN * (g - NQ + 1))
                if g >= NKF:
                    sp.wait_ge(masked, GH * (g - NKF + 1))
                r = slice(g * GR, (g + 1) * GR)
                for i, (q, k) in enumerate((("qh", "kh"), ("qh", "kl"), ("ql", "kh"))):
                    rows = slice(i * GR, (i + 1) * GR)
                    sp.dma_start(a["qs"][rows, g % NQ, :].bitcast(F32), a[q][r, :].bitcast(F32)).then_inc(loaded[g % NQ], 16)
                    sp.dma_start(a["kf"][rows, g % NKF, :].bitcast(F32), a[k][r, :].bitcast(F32)).then_inc(loaded[g % NQ], 16)
            if layer == 0:
                sp.wait_ge(moe_loaded, 32)

        @block.gpsimd
        def _(pool):
            pool.tensor_tensor(t["x"][:, :, :], t["x"][:, :, :], t["row"](f"att{layer}_bo"), ALU.add)\
                .then_inc(x_step, 1) if layer == 0 else \
                pool.tensor_tensor(t["x2"][:, :, :], t["xn"][:, :, :], t["row"](f"att{layer}_bo"), ALU.add)\
                .then_inc(x_step, 1)
            pool.wait_ge(x_step, 1)
            for n in range(NKF):
                pool.memset(a["kf"][3 * GR:P, n, :].bitcast(F32), 1.0).then_inc(ones_set, 1)
            for n in range(NQ):
                pool.memset(a["qs"][3 * GR:P, n, :].bitcast(F32), 0.0).then_inc(ext_zero, 1)
            pool.wait_ge(ones_set, NKF)
            for g in range(NG):
                if g >= NQ:
                    pool.wait_ge(scored, UN * (g - NQ + 1))
                    pool.wait_ge(masked, GH * g)
                    pool.memset(a["qs"][3 * GR:P, g % NQ, :].bitcast(F32), 0.0).then_inc(ext_zero, 1)
                pool.wait_ge(ext_zero, NQ + max(0, g - NQ + 1))
                pool.wait_ge(loaded[g % NQ], 96 * (g // NQ + 1))
                for j in range(GH):
                    pool.tensor_scalar(a["kp"][:, g % NQ, j, :], a["kf"][:, g % NKF, :].bitcast(F32),
                                       t["col"]("head_mask", j), 1.0, ALU.mult, ALU.mult).then_inc(masked, 1)

        @block.tensor
        def _(pe):
            made = [0]

            def fill(kind, g, u, h):
                n = made[0]
                made[0] += 1
                bank = psum[:, M_BANK + n % 2, :]
                if n >= 2:
                    pe.wait_ge(used, n - 1)
                if kind == "max":
                    j, i = divmod(u, NT)
                    if (u, h) == (0, 0):
                        pe.wait_ge(loaded[g % NQ], 96 * (g // NQ + 1))
                        pe.wait_ge(ext_zero, NQ + max(0, g - NQ + 1))
                    if (i, h) == (0, 0):
                        pe.wait_ge(masked, GH * g + j + 1)
                    pe.matmul(bank, a["qs"][:, g % NQ, i * P:(i + 1) * P],
                              a["kp"][:, g % NQ, j, h * HALF:(h + 1) * HALF], start=True, stop=True).then_inc(filled, 1)
                elif kind == "turn_max":
                    pe.wait_ge(merged, g + 1)
                    pe.transpose(bank[0:UN, 0:P], a["mx"][:, g % 2, :], t["ident"][:, :]).then_inc(filled, 1)
                else:
                    pe.wait_ge(out_copied, g + 1)
                    for i in range(TPH):
                        q = (h * TPH + i) * P
                        last = pe.transpose(bank[:, i * P:(i + 1) * P], a["o_raw"][:, q:q + P], t["ident"][:, :])
                    last.then_inc(filled, 1)

            def score(g, u):
                i, j = divmod(u, GH)
                n = UN * g + u
                if u == 0:
                    pe.wait_ge(ext_set, g + 1)
                if n >= 2:
                    pe.wait_ge(exped, n - 1)
                for h in range(NH):
                    last = pe.matmul(psum[:, S_BANK + 2 * (n % 2) + h, :], a["kp"][:, g % NQ, j, i * P:(i + 1) * P],
                                     a["qs"][:, g % NQ, h * HALF:(h + 1) * HALF], start=True, stop=True)
                last.then_inc(scored, 1)

            def weigh(g, i):
                pe.wait_ge(exped, UN * g + GH * (i + 1))
                if i == 0 and g >= 1:
                    pe.wait_ge(out_copied, g)
                for h in range(NH):
                    for j in range(GH):
                        slot = (GH * i + j) % NP
                        last = pe.matmul(psum[GR * j:GR * j + VW, O_BANK + h, :], a["v"][:, i, GH * g + j, :],
                                         a["p"][:, slot, h * HALF:(h + 1) * HALF], start=(i == 0), stop=(i == NT - 1))
                last.then_inc(pv_done, 1)

            for f in fills[:first]:
                fill(*f)
            for g in range(NG):
                for f in per_group[g][-1]:
                    fill(*f)
                if g >= 1:
                    weigh(g - 1, NT - 1)
                for u in range(UN):
                    score(g, u)
                    for f in per_group[g][u]:
                        fill(*f)
                    if u % GH == GH - 1 and u >= 2 * GH - 1:
                        weigh(g, u // GH - 1)
            weigh(NG - 1, NT - 1)
            for f in per_group[NG - 1][UN]:
                fill(*f)
            for i in range(NT):
                if i % TPH == 0:
                    pe.wait_ge(used, len(fills))
                pe.transpose(psum[:, S_BANK + i // TPH, (i % TPH) * P:(i % TPH + 1) * P], a["o"][:, i, :],
                             t["ident"][:, :]).then_inc(o_turned, 1)
            for i in range(NT):
                pe.wait_ge(o_copied, i // TPH + 1)
                last = pe.matmul(psum[:, M_BANK + i // TPH, (i % TPH) * P:(i % TPH + 1) * P], t["y_t"][:, i * P:(i + 1) * P],
                                 w.att[layer][5], start=True, stop=True)
                if i % TPH == TPH - 1:
                    last.then_inc(y_done, 1)

        @block.scalar
        def _(act):
            for g in range(NG):
                for u in range(UN):
                    n = UN * g + u
                    act.wait_ge(scored, n + 1)
                    if n >= NP:
                        act.wait_ge(pv_done, (n - NP) // GH + 1)
                    act.activation(a["p"][:, n % NP, :],
                                   psum[:, S_BANK + 2 * (n % 2):S_BANK + 2 * (n % 2) + 2, :].rearrange("p a d -> p (a d)"),
                                   ACT.Exp, scale=DH ** -0.5).then_inc(exped, 1)
                act.wait_ge(pv_done, NT * (g + 1))
                if g >= 1:
                    n = fills.index(("turn_out", g - 1, 0, NH - 1))
                    act.wait_ge(filled, n + 1)
                act.activation(a["o_raw"][:, :], psum[:, O_BANK:O_BANK + 2, :].rearrange("p a d -> p (a d)"),
                               ACT.Copy).then_inc(out_copied, 1)
            for h in range(NH):
                act.wait_ge(o_turned, TPH * (h + 1))
                act.activation(t["y_t"][:, h * HALF:(h + 1) * HALF], psum[:, S_BANK + h, :], ACT.Copy)\
                    .then_inc(o_copied, 1)

        @block.vector
        def _(dve):
            recips = 0
            for n, (kind, g, u, h) in enumerate(fills):
                bank = psum[:, M_BANK + n % 2, :]
                dve.wait_ge(filled, n + 1)
                if kind == "max":
                    j, i = divmod(u, NT)
                    if (u, h) == (0, 0) and g >= 1:
                        dve.wait_ge(merged, g)
                    dve.tensor_reduce(a["mh"][:, u, h:h + 1], bank, AX.X, ALU.max).then_inc(used, 1)
                    if (u, h) == (UN - 1, NH - 1):
                        dve.wait_ge(used, n + 1)
                        dve.tensor_reduce(a["mx"][:, g % 2, :], a["mh"][:, :, :], AX.X, ALU.max).then_inc(merged, 1)
                elif kind == "turn_max":
                    dve.wait_ge(used, n)
                    dve.tensor_tensor(a["qs"][3 * GR:P, g % NQ, :].rearrange("p (i c) -> p i c", c=P),
                                      bank[0:UN, 0:P].unsqueeze(1).to_broadcast([UN, NT, P]),
                                      t["neg_diag"][3 * GR:P, :, :], ALU.mult).then_inc(ext_set, 1)
                    dve.wait_ge(ext_set, g + 1)
                    dve.sem_inc(used, 1)
                else:
                    out = bank.rearrange("p (i j c) -> p i j c", i=TPH, j=GH)
                    if h >= 0:
                        recips += 1
                        dve.reciprocal(a["rs"][:, recips % 2, :, :], out[:, :, :, DH]).then_inc(recip, 1)
                        dve.wait_ge(recip, recips)
                    o = a["o"][:, h * TPH:(h + 1) * TPH, g * GR:(g + 1) * GR].rearrange("p i (j c) -> p i j c", c=DH)
                    dve.tensor_tensor(o, out[:, :, :, 0:DH],
                                      a["rs"][:, recips % 2, :, :].unsqueeze(3).to_broadcast([P, TPH, GH, DH]),
                                      ALU.mult).then_inc(used, 1)
            dve.wait_ge(x_step, 1)
            for h in range(NH):
                dve.wait_ge(y_done, h + 1)
                s = slice(h * TPH, (h + 1) * TPH)
                x = t["x"] if layer == 0 else t["x2"]
                dve.tensor_tensor(x[:, s, :], psum[:, M_BANK + h, :].rearrange("p (a d) -> p a d", d=D),
                                  x[:, s, :], ALU.add)


class Weights:
    pass


def build(nc, x_in, cols_in, rows_in, gates_in, ident_in, cos_in, sin_in, diag_in, w0_in, wo_in, w1_in, w2_in,
          att_in, gate_in, b2_in, m1_in, m2_in, out):
    with ExitStack() as ctx:
        names = {}

        def sb(name, shape, dt=F32, where=ctx):
            names[name] = names.get(name, 0) + 1
            return where.enter_context(nc.sbuf_tensor(f"{name}_{names[name]}", shape, dt))

        t = {}
        t["psum"] = ctx.enter_context(nc.psum_tensor("psum", [P, 8, HALF], F32))
        for name in ("x", "xn", "x2"):
            t[name] = sb(name, [P, NT, D])
        t["y_t"] = sb("y_t", [P, L])
        cols, rows, gates = sb("cols", [P, NCOLS]), sb("rows", [P, len(ROWS), D]), sb("gates", [P, len(GATES), 16])
        t["rows"] = rows
        t["ident"] = sb("ident", [P, P])
        t["cos"], t["sin"] = sb("cos", [P, L]), sb("sin", [P, L])
        t["neg_diag"] = sb("neg_diag", [P, NT, P])
        t["decay"] = sb("decay", [P, CH])
        t["stats"], t["mv"] = sb("stats", [P, NT, 6]), sb("mv", [P, NT, 2])
        for name in ("var", "std", "rstd", "tmp"):
            t[name] = sb(name, [P, NT])
        t["col"] = lambda name, i=0: cols[:, COLS[name][0] + i:COLS[name][0] + i + 1]
        t["row"] = lambda name: rows[:, ROWS[name]:ROWS[name] + 1, :].to_broadcast([P, NT, D])
        t["grow"] = lambda name, E: gates[:, GATES[name]:GATES[name] + 1, 0:E].to_broadcast([P, NT, E])

        w = Weights()
        m1, m2 = sb("m1", [P, 32 * P]), sb("m2", [P, 32 * P])
        w.m1, w.m2 = m1, m2
        att = sb("att", [P, 2, 6, P])
        w.att = [[att[:, i, k, :] for k in range(6)] for i in range(2)]
        gate_w, b2 = sb("gate_w", [P, 2, 16]), sb("b2", [16, 2, D])
        w.gate, w.b2 = [gate_w[:, i, :] for i in range(2)], [b2[:, i, :] for i in range(2)]

        def load_moe(eng, layer, sem):
            eng.dma_start(m1[:, :], m1_in[layer]).then_inc(sem, 16)
            eng.dma_start(m2[:, :], m2_in[layer]).then_inc(sem, 16)

        w.load_moe = load_moe

        with stage(nc, "loaded", "decayed") as (block, loaded, decayed):
            @block.sync
            def _(sp):
                n = 0
                for to, of in ((cols[:, :], cols_in), (rows[:, :, :], rows_in), (gates[:, :, :], gates_in),
                               (t["ident"][:, :], ident_in), (t["cos"][:, :], cos_in), (t["sin"][:, :], sin_in),
                               (t["neg_diag"][3 * GR:P, :, :], diag_in), (att[:, :, :, :], att_in),
                               (gate_w[:, :, :], gate_in), (b2[:, :, :], b2_in)):
                    sp.dma_start(to, of).then_inc(loaded, 16)
                    n += 16
                sp.wait_ge(loaded, n)

            @block.scalar
            def _(act):
                act.wait_ge(loaded, 160)
                lo, hi = COLS["decay"]
                act.activation(t["decay"][:, :], cols[:, lo:hi], ACT.Sigmoid)

        x_v = x_in.rearrange("b (i p) d -> b p i d", p=P)
        out_v = out.rearrange("b (i p) d -> b p i d", p=P)

        with nc.Fori(0, B) as b:
            with ExitStack() as scope:
                w0, wo = sb("w0", [P, 4, CH * P], where=scope), sb("wo", [P, CH, D], where=scope)
                w.q, w.k, w.v, w.g = (w0[:, i, :] for i in range(4))
                w.o = wo
                w.w1, w.w2 = sb("w1", [P, FF * P], where=scope), sb("w2", [P, FF, D], where=scope)
                for name, n in (("v", 2), ("g", 2), ("kv", 2), ("state", 2), ("qg", 2), ("gated", 3)):
                    t[name] = sb(name, [P, n, HALF], where=scope)
                t["ffh"] = sb("ffh", [P, FF, L], where=scope)
                with stage(nc, "x_loaded", "w_loaded") as (block, x_loaded, w_loaded):
                    @block.sync
                    def _(sp):
                        sp.dma_start(t["x"][:, :, :], x_v[bass.ds(b, 1), :, :, :]).then_inc(x_loaded, 16)
                        for i in range(4):
                            sp.dma_start(w0[:, i, :], w0_in[i]).then_inc(w_loaded, 16)
                        sp.dma_start(wo[:, :, :], wo_in).then_inc(w_loaded, 16)
                        sp.dma_start(w.w1[:, :], w1_in).then_inc(w_loaded, 16)
                        sp.dma_start(w.w2[:, :, :], w2_in).then_inc(w_loaded, 16)
                        sp.wait_ge(x_loaded, 16)
                        sp.wait_ge(w_loaded, 112)
                normalise(nc, t, t["x"], t["xn"])
                normalise(nc, t, t["xn"], t["x2"], t["y_t"], t["col"]("ln1_g"), t["col"]("ln1_b"))
                recurrence(nc, t, w)
                normalise(nc, t, t["x2"], t["xn"], t["y_t"], t["col"]("ln2_g"), t["col"]("ln2_b"))
                feed_forward(nc, t, w)

            def mixture(layer, E, F, func):
                with ExitStack() as scope:
                    t["acc"] = sb("acc", [P, NT, D], where=scope)
                    t["moe_h"] = sb("moe_h", [P, 2, F, HALF], where=scope)
                    for name in ("lg", "eq", "cw"):
                        t[name] = sb(name, [P, NT, 16], where=scope)
                    t["mx8"], t["ix8"] = sb("mx8", [P, NT, 8], where=scope), sb("ix8", [P, NT, 8], U32, where=scope)
                    t["ixf"], t["wt"] = sb("ixf", [P, NT, 2], where=scope), sb("wt", [P, NT, 2], where=scope)
                    t["cw_t"] = sb("cw_t", [16, L], where=scope)
                    gate(nc, t, w, layer, E)
                    experts(nc, t, w, layer, E, F, func)
                    if layer == 0:
                        add_to_x(nc, t, t["acc"])
                    else:
                        normalise(nc, t, t["acc"], t["x2"], row_gain=t["row"]("g2"), row_shift=t["row"]("be2"),
                                  add=(t["acc"][:, :, :], t["xn"][:, :, :]))
                        add_to_x(nc, t, t["x2"])

            def attend(layer):
                with ExitStack() as scope:
                    a = {}
                    for name in ("qh", "ql", "kh", "kl"):
                        a[name] = sb(name, [P, L], F32R, where=scope)
                    a["v"] = sb("v_ext", [P, NT, HEADS, VW], where=scope)
                    with ExitStack() as inner:
                        for name in ("ra", "rb", "rot"):
                            a[name] = sb(name, [P, 2, HALF], where=inner)
                        attention_inputs(nc, t, w, layer, a)
                    a["qs"] = sb("qs", [P, 3, L], F32R, where=scope)
                    a["kf"] = sb("kf", [P, 2, L], F32R, where=scope)
                    a["kp"] = sb("kp", [P, 3, GH, L], F32R, where=scope)
                    a["p"] = sb("p", [P, 8, L], where=scope)
                    a["o_raw"] = sb("o_raw", [P, L], where=scope)
                    a["o"] = sb("o", [P, NT, D], where=scope)
                    a["mh"] = sb("mh", [P, GH * NT, NH], where=scope)
                    a["mx"] = sb("mx", [P, 2, GH * NT], where=scope)
                    a["rs"] = sb("rs", [P, 2, TPH, GH], where=scope)
                    attention(nc, t, w, layer, a)

            normalise(nc, t, t["x"], t["xn"], t["y_t"])
            mixture(0, 16, 2, ACT.Relu)
            normalise(nc, t, t["x"], t["xn"], t["y_t"])
            attend(0)
            normalise(nc, t, t["x"], t["xn"], t["y_t"])
            attend(1)
            normalise(nc, t, t["x2"], t["xn"], t["y_t"], row_gain=t["row"]("g1"), row_shift=t["row"]("be1"))
            mixture(1, 8, 4, ACT.Gelu)
            with stage(nc, "stored") as (block, stored):
                @block.sync
                def _(sp):
                    sp.dma_start(out_v[bass.ds(b, 1), :, :, :], t["x"][:, :, :]).then_inc(stored, 16)
                    sp.wait_ge(stored, 16)


def layout(i):
    def cols(a):
        return np.reshape(a, (-1, P)).T

    def swap(a):
        s = np.reshape(a, (*a.shape[:-1], HEADS, 2, DH // 2))
        return np.reshape(s[..., ::-1, :], a.shape)

    c = np.zeros((P, NCOLS), np.float32)
    r = np.arange(P)

    def put(name, a):
        c[:, COLS[name][0]:COLS[name][1]] = a

    put("ln1_g", cols(i["L0_attn_ln1_g"])), put("ln1_b", cols(i["L0_attn_ln1_b"]))
    for n in "qkvg":
        put("b" + n, cols(i["L0_attn_b" + n]))
    put("decay", cols(np.repeat(i["L0_attn_decay_logit"], 64)))
    put("ln2_g", cols(i["L0_attn_ln2_g"])), put("ln2_b", cols(i["L0_attn_ln2_b"]))
    put("b1", cols(i["L0_attn_b1"]))
    put("moe0_b1", cols(i["L0_ffn_b1"])), put("moe1_b1", cols(i["L1_ffn_b1"]))
    for k, name in enumerate(("L1_attn_", "L1_ffn_")):
        for n in "qk":
            put(f"att{k}_b{n}", cols(i[f"{name}b{n}"]))
            put(f"att{k}_b{n}r", cols(swap(i[f"{name}b{n}"])))
    put("head_mask", (r[:, None] % GR // DH == np.arange(GH)[None]).astype(np.float32))
    rows = {"bo": "L0_attn_bo", "b2": "L0_attn_b2", "att0_bv": "L1_attn_bv", "att0_bo": "L1_attn_bo",
            "att1_bv": "L1_ffn_bv", "att1_bo": "L1_ffn_bo", "g1": "L1_ffn_g1", "be1": "L1_ffn_be1",
            "g2": "L1_ffn_g2", "be2": "L1_ffn_be2"}
    row = np.stack([i[rows[n]] for n in ROWS])
    gates = np.zeros((len(GATES), 16), np.float32)
    gates[0], gates[1], gates[2, 0:8], gates[3] = i["L0_ffn_bg"], i["L0_ffn_bias"], i["L1_ffn_bg"], np.arange(16)

    inv = (1.0 / np.float32(10000.0) ** (np.arange(0, DH, 2, dtype=np.float32) / np.float32(DH))).astype(np.float32)
    angle = (np.arange(L, dtype=np.float32)[None] * inv[r % (DH // 2)][:, None]).astype(np.float32)
    sign = np.where(r % DH < DH // 2, -1, 1).astype(np.float32)[:, None]
    diag = np.zeros((GR, NT, P), np.float32)
    diag[np.arange(GR), np.arange(GR) % NT, :] = -1.0

    att = []
    for wq, wk, wv, wo in ((i["L1_attn_Wq"].T, i["L1_attn_Wk"].T, i["L1_attn_Wv"].T, i["L1_attn_Wo"].T),
                           (i["L1_ffn_Wq"], i["L1_ffn_Wk"], i["L1_ffn_Wv"], i["L1_ffn_Wo"])):
        att.append(np.stack([wq, wk, swap(wq), swap(wk), wv, wo], 1))
    gate_w = np.zeros((P, 2, 16), np.float32)
    gate_w[:, 0, :], gate_w[:, 1, 0:8] = i["L0_ffn_Wg"], i["L1_ffn_Wg"]
    b2 = np.zeros((16, 2, D), np.float32)
    b2[:, 0], b2[0:8, 1] = i["L0_ffn_b2"], i["L1_ffn_b2"]

    def up(w):
        return np.reshape(w.transpose(1, 0, 2), (P, -1))

    def down(w):
        return np.reshape(np.reshape(w, (w.shape[0], -1, P, D)).transpose(2, 0, 1, 3), (P, -1))

    arrays = {
        "x": i["L0_attn_x"], "cols": c, "rows": np.broadcast_to(row[None], (P, *row.shape)),
        "gates": np.broadcast_to(gates[None], (P, *gates.shape)), "ident": np.eye(P, dtype=np.float32),
        "cos": np.cos(angle), "sin": np.sin(angle) * sign, "diag": diag,
        "w0": np.stack([i["L0_attn_W" + n] for n in "qkvg"]),
        "wo": np.reshape(i["L0_attn_Wo"], (CH, P, D)).transpose(1, 0, 2), "w1": i["L0_attn_W1"],
        "w2": np.reshape(i["L0_attn_W2"], (FF, P, D)).transpose(1, 0, 2),
        "att": np.stack(att, 1), "gate": gate_w, "b2": b2,
        "m1": np.stack([up(i["L0_ffn_W1"]), up(i["L1_ffn_W1"])]),
        "m2": np.stack([down(i["L0_ffn_W2"]), down(i["L1_ffn_W2"])]),
    }
    return {k: np.ascontiguousarray(v) for k, v in arrays.items()}


def kernel(**inputs):
    import concourse.bacc as bacc
    from concourse.bass_utils import run_bass_kernel_spmd

    nc = bacc.Bacc("TRN2", target_bir_lowering=False, num_devices=1, dynamic_dma_scratch_size=2048)
    arrays = {f"in_{k}": v for k, v in layout({k: np.asarray(v) for k, v in inputs.items()}).items()}
    args = [nc.dram_tensor(k, v.shape, mybir.dt.from_np(v.dtype), kind="ExternalInput").ap() for k, v in arrays.items()]
    out = nc.dram_tensor("out", (B, L, D), F32, kind="ExternalOutput").ap()
    build(nc, *args, out)
    return run_bass_kernel_spmd(nc, [arrays], core_ids=[0]).results[0]["out"]
```

```python
import numpy as np
import concourse.bass as bass
from concourse import mybir
from contextlib import ExitStack, contextmanager

F32 = mybir.dt.float32
F32R = mybir.dt.float32r
U32 = mybir.dt.uint32
ALU = mybir.AluOpType
ACT = mybir.ActivationFunctionType
AX = mybir.AxisListType

B, L, D = 4, 1024, 128
P = 128
NT = L // P
HALF = 512
NH = L // HALF
TPH = HALF // P
CH = 16 * 64 // P
FF = 512 // P
HEADS, DH = 16, 8
GH = 4
NG = HEADS // GH
GR = GH * DH
VW = 32
EPS = 1e-5

COLS, at = {}, 0
for name, n in (("ln1_g", 1), ("ln1_b", 1), ("bq", CH), ("bk", CH), ("bv", CH), ("bg", CH), ("decay", CH),
                ("ln2_g", 1), ("ln2_b", 1), ("b1", FF),
                ("att0_bq", 1), ("att0_bk", 1), ("att0_bqr", 1), ("att0_bkr", 1),
                ("att1_bq", 1), ("att1_bk", 1), ("att1_bqr", 1), ("att1_bkr", 1), ("head_mask", GH)):
    COLS[name] = (at, at + n)
    at += n
NCOLS = at
ROWS = {name: i for i, name in enumerate(("bo", "b2", "att0_bv", "att0_bo", "att1_bv", "att1_bo",
                                          "g1", "be1", "g2", "be2"))}
GATES = {name: i for i, name in enumerate(("moe0_bg", "moe0_bias", "moe1_bg", "iota"))}


FIRST_LOADS = 7


INV = 8
PLACES = 6
SLOT_TILES = 80
CONSTS, at = {}, 0
for name, n in (("iota", P), ("iota128", B * NT), ("keep", 16 * B * NT), ("before", P), ("ones", P),
                ("place", 2 * B * NT), ("unfilled", SLOT_TILES)):
    CONSTS[name] = (at, at + n)
    at += n
NCONSTS = at


@contextmanager
def stage(nc, *names):
    with ExitStack() as ctx:
        sems = [ctx.enter_context(nc.semaphore(n)) for n in names]
        with nc.Block() as block:
            yield (block, *sems)
        for s in sems:
            nc.gpsimd.sem_clear(s)
        nc.all_engine_barrier()


def chain(eng, sem):
    done = [0]

    def link(ins):
        done[0] += 1
        ins.then_inc(sem, 1)
        eng.wait_ge(sem, done[0])

    return link


def normalise(nc, t, src, dst, dst_t=None, gain=None, shift=None, row_gain=None, row_shift=None, ahead=None):
    with stage(nc, "dve_step", "var_ready", "std_ready", "tile_ready", "turned", "fetched") as \
            (block, dve_step, var_ready, std_ready, tile_ready, turned, fetched):
        @block.vector
        def _(dve):
            link = chain(dve, dve_step)
            for i in range(NT):
                last = dve.bn_stats(t["stats"][:, i, :], src[:, i, :])
            link(last)
            for i in range(NT):
                last = dve.bn_aggr(t["mv"][:, i, :], t["stats"][:, i, :])
            link(last)
            dve.tensor_scalar(t["var"][:, :], t["mv"][:, :, 1], EPS, None, ALU.add).then_inc(var_ready, 1)
            dve.wait_ge(std_ready, 1)
            link(dve.reciprocal(t["rstd"][:, :], t["std"][:, :]))
            link(dve.tensor_tensor(t["tmp"][:, :], t["rstd"][:, :], t["rstd"][:, :], ALU.mult))
            link(dve.tensor_tensor(t["tmp"][:, :], t["tmp"][:, :], t["var"][:, :], ALU.mult))
            link(dve.tensor_scalar(t["tmp"][:, :], t["tmp"][:, :], -0.5, 1.5, ALU.mult, ALU.add))
            link(dve.tensor_tensor(t["rstd"][:, :], t["rstd"][:, :], t["tmp"][:, :], ALU.mult))
            for i in range(NT):
                last = dve.tensor_scalar(dst[:, i, :], src[:, i, :], t["mv"][:, i, 0:1], t["rstd"][:, i:i + 1],
                                         ALU.subtract, ALU.mult)
                if row_gain is None:
                    last.then_inc(tile_ready, 1)
            if row_gain is not None:
                link(last)
                link(dve.tensor_tensor(dst[:, :, :], dst[:, :, :], row_gain, ALU.mult))
                dve.tensor_tensor(dst[:, :, :], dst[:, :, :], row_shift, ALU.add).then_inc(tile_ready, NT)

        if ahead is not None:
            @block.sync
            def _(sp):
                fetch(sp, t, ahead, fetched)

        @block.scalar
        def _(act):
            act.wait_ge(var_ready, 1)
            act.activation(t["std"][:, :], t["var"][:, :], ACT.Sqrt).then_inc(std_ready, 1)
            if dst_t is None:
                return
            for h in range(NH):
                act.wait_ge(turned, TPH * (h + 1))
                out, bank = dst_t[:, h * HALF:(h + 1) * HALF], t["psum"][:, h, :]
                if gain is None:
                    act.activation(out, bank, ACT.Copy)
                else:
                    act.activation(out, bank, ACT.Identity, scale=gain, bias=shift)

        @block.tensor
        def _(pe):
            if dst_t is None:
                return
            for i in range(NT):
                pe.wait_ge(tile_ready, i + 1)
                pe.transpose(t["psum"][:, i // TPH, (i % TPH) * P:(i % TPH + 1) * P], dst[:, i, :],
                             t["ident"][:, :]).then_inc(turned, 1)


def recurrence(nc, t, w):
    units = [(c, h) for c in range(CH) for h in range(NH)]
    NB, LAG, BANKS = 3, 2, 6
    psum, col, y_t = t["psum"], t["col"], t["y_t"]
    with stage(nc, "proj_done", "act_used", "dve_used", "scanned", "gated", "out_done", "x_added") as \
            (block, proj_done, act_used, dve_used, scanned, gated, out_done, x_added):
        @block.tensor
        def _(pe):
            def project(u):
                c, h = units[u]
                for i, m in enumerate((w.v, w.k, w.g, w.q)):
                    n = 4 * u + i
                    if n >= BANKS:
                        u0, i0 = divmod(n - BANKS, 4)
                        pe.wait_ge(dve_used if i0 % 2 else act_used, 2 * u0 + i0 // 2 + 1)
                    pe.matmul(psum[:, n % BANKS, :], m[:, c * P:(c + 1) * P], y_t[:, h * HALF:(h + 1) * HALF],
                              start=True, stop=True).then_inc(proj_done, 1)

            def output(u):
                c, h = units[u]
                pe.wait_ge(gated, u + 1)
                for i in range(TPH):
                    last = pe.matmul(psum[:, BANKS + h, i * P:(i + 1) * P], t["gated"][:, u % NB, i * P:(i + 1) * P],
                                     w.o[:, c, :], start=(c == 0 and i == 0), stop=(c == CH - 1),
                                     skip_group_check=True)
                last.then_inc(out_done, 1)

            pe.wait_ge(t["first_loaded"], FIRST_LOADS * 16)
            for u in range(len(units) + LAG):
                if u < len(units):
                    project(u)
                if u >= LAG:
                    output(u - LAG)

        @block.scalar
        def _(act):
            for u, (c, h) in enumerate(units):
                act.wait_ge(proj_done, 4 * u + 1)
                if u >= 2:
                    act.wait_ge(dve_used, 2 * (u - 2) + 1)
                act.activation(t["v"][:, u % 2, :], psum[:, 4 * u % BANKS, :], ACT.Identity,
                               bias=col("bv", c)).then_inc(act_used, 1)
                act.wait_ge(proj_done, 4 * u + 3)
                if u >= 2:
                    act.wait_ge(dve_used, 2 * (u - 2) + 2)
                act.activation(t["g"][:, u % 2, :], psum[:, (4 * u + 2) % BANKS, :], ACT.Sigmoid,
                               bias=col("bg", c)).then_inc(act_used, 1)

        @block.vector
        def _(dve):
            for u, (c, h) in enumerate(units):
                dve.wait_ge(proj_done, 4 * u + 2)
                dve.wait_ge(act_used, 2 * u + 1)
                dve.scalar_tensor_tensor(t["kv"][:, u % 2, :], psum[:, (4 * u + 1) % BANKS, :], col("bk", c),
                                         t["v"][:, u % 2, :], ALU.add, ALU.mult).then_inc(dve_used, 1)
                dve.wait_ge(dve_used, 2 * u + 1)
                if u >= 2:
                    dve.wait_ge(gated, u - 1)
                if h:
                    dve.wait_ge(scanned, u)
                start = t["state"][:, (u - 1) % 2, HALF - 1:HALF] if h else 0.0
                dve.tensor_tensor_scan(t["state"][:, u % 2, :], t["decay"][:, c:c + 1].to_broadcast([P, HALF]),
                                       t["kv"][:, u % 2, :], start, ALU.mult, ALU.add).then_inc(scanned, 1)
                dve.wait_ge(proj_done, 4 * u + 4)
                dve.wait_ge(act_used, 2 * u + 2)
                dve.scalar_tensor_tensor(t["qg"][:, u % 2, :], psum[:, (4 * u + 3) % BANKS, :], col("bq", c),
                                         t["g"][:, u % 2, :], ALU.add, ALU.mult).then_inc(dve_used, 1)
            dve.wait_ge(x_added, 1)
            for h in range(NH):
                dve.wait_ge(out_done, len(units) - NH + h + 1)
                s = slice(h * TPH, (h + 1) * TPH)
                dve.scalar_tensor_tensor(t["x2"][:, s, :], psum[:, BANKS + h, :].rearrange("p (a d) -> p a d", d=D),
                                         64 ** -0.5, t["x2"][:, s, :], ALU.mult, ALU.add)

        @block.gpsimd
        def _(pool):
            pool.tensor_tensor(t["x2"][:, :, :], t["xn"][:, :, :], t["row"]("bo"), ALU.add).then_inc(x_added, 1)
            for u in range(len(units)):
                pool.wait_ge(scanned, u + 1)
                pool.wait_ge(dve_used, 2 * u + 2)
                if u >= NB:
                    pool.wait_ge(out_done, u - NB + 1)
                pool.tensor_tensor(t["gated"][:, u % NB, :], t["state"][:, u % 2, :], t["qg"][:, u % 2, :],
                                   ALU.mult).then_inc(gated, 1)


def feed_forward(nc, t, w):
    psum, col = t["psum"], t["col"]
    with stage(nc, "hidden", "gelued", "out_done", "x_step") as (block, hidden, gelued, out_done, x_step):
        @block.tensor
        def _(pe):
            for n in range(FF * NH):
                f, h = n // NH, n % NH
                if n >= 6:
                    pe.wait_ge(gelued, n - 5)
                pe.matmul(psum[:, n % 6, :], w.w1[:, f * P:(f + 1) * P], t["y_t"][:, h * HALF:(h + 1) * HALF],
                          start=True, stop=True).then_inc(hidden, 1)
            pe.wait_ge(gelued, FF * NH)
            for i in range(NT):
                for f in range(FF):
                    last = pe.matmul(psum[:, 6 + i // TPH, (i % TPH) * P:(i % TPH + 1) * P],
                                     t["ffh"][:, f, i * P:(i + 1) * P], w.w2[:, f, :],
                                     start=(f == 0), stop=(f == FF - 1))
                last.then_inc(out_done, 1)

        @block.scalar
        def _(act):
            for n in range(FF * NH):
                f, h = n // NH, n % NH
                act.wait_ge(hidden, n + 1)
                act.activation(t["ffh"][:, f, h * HALF:(h + 1) * HALF], psum[:, n % 6, :], ACT.Gelu,
                               bias=col("b1", f)).then_inc(gelued, 1)

        @block.gpsimd
        def _(pool):
            link = chain(pool, x_step)
            link(pool.tensor_tensor(t["x"](), t["x"](), t["x2"][:, :, :], ALU.add))
            link(pool.tensor_tensor(t["x"](), t["x"](), t["row"]("b2"), ALU.add))

        @block.vector
        def _(dve):
            dve.wait_ge(x_step, 2)
            for h in range(NH):
                dve.wait_ge(out_done, TPH * (h + 1))
                s = slice(h * TPH, (h + 1) * TPH)
                dve.tensor_tensor(t["x"](h * TPH, TPH), psum[:, 6 + h, :].rearrange("p (a d) -> p a d", d=D),
                                  t["x"](h * TPH, TPH), ALU.add)


def pick_two(dve, link, t, layer, E, to_exp, exped):
    lg, mx, ix, sel, wt, tmp = (t[k] for k in ("lg", "mx8", "ix8", "sel", "wt", "tmp2"))
    L3 = [P, B * NT, E]
    if layer:
        link(dve.tensor_reduce(tmp[:, :, 0], lg[:, :, :], AX.X, ALU.max))
        dve.tensor_tensor(lg[:, :, :], lg[:, :, :], tmp[:, :, 0:1].to_broadcast(L3), ALU.subtract).then_inc(to_exp, 1)
        dve.wait_ge(exped, 1)
        link(dve.tensor_reduce(tmp[:, :, 0], lg[:, :, :], AX.X, ALU.add))
        link(dve.reciprocal(tmp[:, :, 1], tmp[:, :, 0]))
        link(dve.tensor_tensor(lg[:, :, :], lg[:, :, :], tmp[:, :, 1:2].to_broadcast(L3), ALU.mult))
    for i in range(B * NT):
        last = dve.max(mx[:, i, :], lg[:, i, :])
    link(last)
    for i in range(B * NT):
        last = dve.max_index(ix[:, i, :], mx[:, i, :], lg[:, i, :])
    link(last)
    link(dve.tensor_copy(sel[:, :, :], ix[:, :, 0:2]))
    if layer:
        link(dve.tensor_tensor(tmp[:, :, 0], mx[:, :, 0], mx[:, :, 1], ALU.add))
        link(dve.reciprocal(tmp[:, :, 1], tmp[:, :, 0]))
        link(dve.tensor_tensor(wt[:, :, :], mx[:, :, 0:2], tmp[:, :, 1:2].to_broadcast([P, B * NT, 2]), ALU.mult))
    else:
        dve.tensor_tensor(tmp[:, :, 0], mx[:, :, 1], mx[:, :, 0], ALU.subtract).then_inc(to_exp, 1)
        dve.wait_ge(exped, 1)
        link(dve.tensor_scalar(tmp[:, :, 0], tmp[:, :, 1], 1.0, None, ALU.add))
        link(dve.reciprocal(wt[:, :, 0], tmp[:, :, 0]))
        link(dve.tensor_tensor(wt[:, :, 1], tmp[:, :, 1], wt[:, :, 0], ALU.mult))


def route(nc, t, layer, E, tiles):
    psum, T, TE = t["psum"], B * NT, B * NT * E
    lg, sel, oh0, oh1, both, pos, cnt, upto = (t[k] for k in ("lg", "sel", "oh0", "oh1", "both", "pos", "cnt", "upto"))
    per, end, base = t["per"], t["end"], t["base"]
    L3 = [P, T, E]
    iota = t["iota"]
    with stage(nc, "step", "to_exp", "exped", "both_ready", "counted") as \
            (block, step, to_exp, exped, both_ready, counted):
        @block.scalar
        def _(act):
            act.wait_ge(to_exp, 1)
            if layer:
                act.activation(lg[:, :, :], lg[:, :, :], ACT.Exp).then_inc(exped, 1)
            else:
                act.activation(t["tmp2"][:, :, 1], t["tmp2"][:, :, 0], ACT.Exp).then_inc(exped, 1)

        @block.tensor
        def _(pe):
            pe.wait_ge(both_ready, 1)
            both_flat = both[:, :, :].rearrange("p t e -> p (t e)")
            pe.matmul(psum[:, 0, 0:TE], t["before"][:, :], both_flat, start=True, stop=True)
            pe.matmul(psum[:, 1, 0:TE], t["ones"][:, :], both_flat, start=True, stop=True).then_inc(counted, 1)

        @block.vector
        def _(dve):
            link = chain(dve, step)
            pick_two(dve, link, t, layer, E, to_exp, exped)
            experts_row = iota[:, 0:E].unsqueeze(1).to_broadcast(L3)
            dve.tensor_tensor(oh0[:, :, :], experts_row, sel[:, :, 0:1].to_broadcast(L3), ALU.is_equal)
            link(dve.tensor_tensor(oh1[:, :, :], experts_row, sel[:, :, 1:2].to_broadcast(L3), ALU.is_equal))
            link(dve.tensor_tensor(both[:, :, :], oh0[:, :, :], oh1[:, :, :], ALU.add))
            dve.sem_inc(both_ready, 1)
            dve.wait_ge(counted, 1)
            link(dve.tensor_copy(cnt[:, :, :], psum[:, 1, 0:TE].rearrange("p (t e) -> p e t", e=E)))
            link(dve.tensor_tensor_scan(upto[:, :, :].rearrange("p e t -> p (e t)"), t["keep"][:, 0:TE],
                                        cnt[:, :, :].rearrange("p e t -> p (e t)"), 0.0, ALU.mult, ALU.add))
            link(dve.tensor_tensor(cnt[:, :, :], upto[:, :, :], cnt[:, :, :], ALU.subtract))
            link(dve.tensor_tensor(t["over"][:, :, :], upto[:, :, T - 1:T].to_broadcast([P, E, T]),
                                   t["iota128"][:, 0:T].unsqueeze(1).to_broadcast([P, E, T]), ALU.is_gt))
            link(dve.tensor_reduce(per[:, 0:E], t["over"][:, :, :], AX.X, ALU.add))
            link(dve.tensor_tensor_scan(end[:, 0:E], t["ones"][:, 0:E], per[:, 0:E], 0.0, ALU.mult, ALU.add))
            link(dve.tensor_tensor(base[:, 0:E], end[:, 0:E], per[:, 0:E], ALU.subtract))
            link(dve.tensor_scalar(base[:, 0:E], base[:, 0:E], float(P), None, ALU.mult))
            link(dve.tensor_tensor(pos[:, :, :], psum[:, 0, 0:TE].rearrange("p (t e) -> p t e", e=E),
                                   cnt[:, :, :].rearrange("p e t -> p t e"), ALU.add))
            link(dve.tensor_tensor(pos[:, :, :], pos[:, :, :], base[:, 0:E].unsqueeze(1).to_broadcast(L3), ALU.add))
            dve.tensor_tensor(oh0[:, :, :], oh0[:, :, :], pos[:, :, :], ALU.mult)
            link(dve.tensor_tensor(oh1[:, :, :], oh1[:, :, :], pos[:, :, :], ALU.mult))
            dve.tensor_reduce(sel[:, :, 0], oh0[:, :, :], AX.X, ALU.add)
            link(dve.tensor_reduce(sel[:, :, 1], oh1[:, :, :], AX.X, ALU.add))
            row = [1, tiles, E]
            link(dve.tensor_tensor(t["ended"][:, 0:tiles, :], iota[0:1, 0:tiles].unsqueeze(2).to_broadcast(row),
                                   end[0:1, 0:E].unsqueeze(1).to_broadcast(row), ALU.is_ge))
            link(dve.tensor_reduce(t["who"][:, 0:tiles], t["ended"][:, 0:tiles, :], AX.X, ALU.add))
            dve.tensor_scalar(t["expert_of"][:, 0:tiles], t["who"][:, 0:tiles], float(E - 1), None, ALU.min)


def floor(dve, link, x, lowest):
    link(dve.tensor_scalar(x, x, -lowest, None, ALU.add))
    link(dve.tensor_scalar(x, x, float(3 * 2 ** 22), None, ALU.add))
    link(dve.tensor_scalar(x, x, -float(3 * 2 ** 22), None, ALU.add))


def invert(nc, t, tiles):
    psum, T = t["psum"], B * NT
    sel, hi, lo, G = t["sel"], t["hi"], t["lo"], INV
    pairs = 2 * T
    flat = lambda a: a[:, :, :].rearrange("p t k -> p (t k)")
    with stage(nc, "step", "lo_ready", "hi_ready", "used") as (block, step, lo_ready, hi_ready, used):
        @block.vector
        def _(dve):
            link = chain(dve, step)
            link(dve.tensor_scalar(hi[:, :, :], sel[:, :, :], 1.0 / P, None, ALU.mult))
            floor(dve, link, hi[:, :, :], 0.5 - 0.5 / P)
            link(dve.scalar_tensor_tensor(lo[:, :, :], hi[:, :, :], -float(P), sel[:, :, :], ALU.mult, ALU.add))
            for c in range(pairs // G):
                if c >= 2:
                    dve.wait_ge(used, G * (c - 1))
                dve.tensor_tensor(t["lo_hot"][:, c % 2, :, :], t["iota"][:, 0:P].unsqueeze(1).to_broadcast([P, G, P]),
                                  flat(lo)[:, c * G:(c + 1) * G].unsqueeze(2).to_broadcast([P, G, P]),
                                  ALU.is_equal).then_inc(lo_ready, 1)
                for n in range(c * G, (c + 1) * G):
                    dve.tensor_scalar(t["hi_hot"][:, n % (2 * G), 0:tiles], t["iota"][:, 0:tiles],
                                      flat(hi)[:, n:n + 1], t["place"][:, n:n + 1],
                                      ALU.is_equal, ALU.mult).then_inc(hi_ready, 1)
            dve.wait_ge(used, pairs)
            v, place, token = psum[:, 2, 0:tiles], t["place_f"][:, 0:tiles], t["token_f"][:, 0:tiles]
            link(dve.tensor_scalar(token, v, -1.0, 0.0, ALU.add, ALU.max))
            link(dve.tensor_scalar(token, token, 0.5, None, ALU.mult))
            floor(dve, link, token, 0.25)
            link(dve.tensor_scalar(place, v, 0.0, None, ALU.is_equal))
            link(dve.tensor_tensor(place, place, t["unfilled"][:, 0:tiles], ALU.mult))
            link(dve.tensor_tensor(place, place, v, ALU.add))
            link(dve.tensor_scalar(place, place, -1.0, None, ALU.add))
            dve.tensor_copy(t["token_of"][:, 0:tiles], token)
            dve.tensor_copy(t["place_of"][:, 0:tiles], place)

        @block.tensor
        def _(pe):
            for n in range(pairs):
                if n % G == 0:
                    pe.wait_ge(lo_ready, n // G + 1)
                pe.wait_ge(hi_ready, n + 1)
                last = pe.matmul(psum[:, 2, 0:tiles], t["lo_hot"][:, (n // G) % 2, n % G, :],
                                 t["hi_hot"][:, n % (2 * G), 0:tiles], start=(n == 0), stop=(n == pairs - 1))
                last.then_inc(used, 1)


def expert_tiles(nc, t, it, KT, F, func):
    psum, W1, W2, B1 = t["psum"], 0, F * P, 2 * F * P
    B2 = B1 + F
    NX, NST = PLACES, 3
    with stage(nc, "indices", "staged", "turned", "x_ready", "hidden", "activated", "y_done", "y_ready") as \
            (block, indices, staged, turned, x_ready, hidden, activated, y_done, y_ready):
        def moved(sems, counts, i):
            n = i % NX
            turns = len(range(n, KT, NX))
            return sems[n], it * (16 * turns) + (counts[n] + 16 * (i // NX + 1))

        @block.gpsimd
        def _(pool):
            pool.tensor_copy(t["token_now"][:, 0:KT], t["token_of"][:, bass.ds(it * KT, KT)]).then_inc(indices, 1)
            pool.tensor_copy(t["place_now"][:, 0:KT], t["place_of"][:, bass.ds(it * KT, KT)]).then_inc(indices, 1)
            pool.wait_ge(indices, 2)

            def gather(i):
                if i >= NX:
                    pool.wait_ge(turned, i - NX + 1)
                pool.indirect_dma_start(t["x_in"][:, i % NX, :], None, t["n_rows"],
                                        bass.IndirectOffsetOnAxis(ap=t["token_now"][:, i:i + 1], axis=0))\
                    .then_inc(t["gathered"][i % NX], 16)

            for i in range(NX - 1):
                gather(i)
            for i in range(KT):
                if i + NX - 1 < KT:
                    gather(i + NX - 1)
                pool.wait_ge(y_ready, i + 1)
                pool.indirect_dma_start(t["answers"],
                                        bass.IndirectOffsetOnAxis(ap=t["place_now"][:, i:i + 1], axis=0),
                                        t["y_out"][:, i % NX, :], None).then_inc(t["scattered"][i % NX], 16)
            for i in range(KT - NX, KT):
                pool.wait_ge(*moved(t["scattered"], t["scatters"], i))

        @block.tensor
        def _(pe):
            def turn(i):
                pe.wait_ge(*moved(t["gathered"], t["gathers"], i))
                if i >= 2:
                    pe.wait_ge(x_ready, i - 1)
                pe.transpose(psum[:, i % 2, 0:P], t["x_in"][:, i % NX, :], t["ident"][:, :]).then_inc(turned, 1)

            def up(i):
                pe.wait_ge(x_ready, i + 1)
                pe.wait_ge(staged, i + 1)
                if i >= 2:
                    pe.wait_ge(activated, F * (i - 1))
                for f in range(F):
                    last = pe.matmul(psum[:, 2 + i % 2, f * P:(f + 1) * P],
                                     t["stage"][:, i % NST, W1 + f * P:W1 + (f + 1) * P], t["x_t"][:, i % 2, :],
                                     start=True, stop=True)
                last.then_inc(hidden, 1)

            def down(i):
                pe.wait_ge(activated, F * (i + 1))
                if i >= 2:
                    pe.wait_ge(y_ready, i - 1)
                for f in range(F):
                    last = pe.matmul(psum[:, 4 + i % 2, 0:P], t["hid"][:, i % 2, f, :],
                                     t["stage"][:, i % NST, W2 + f * P:W2 + (f + 1) * P],
                                     start=(f == 0), stop=(f == F - 1))
                last.then_inc(y_done, 1)

            for i in range(KT + 2):
                if i < KT:
                    turn(i)
                if 1 <= i <= KT:
                    up(i - 1)
                if i >= 2:
                    down(i - 2)

        @block.scalar
        def _(act):
            for i in range(KT):
                act.wait_ge(hidden, i + 1)
                if i >= 2:
                    act.wait_ge(y_done, i - 1)
                for f in range(F):
                    act.activation(t["hid"][:, i % 2, f, :], psum[:, 2 + i % 2, f * P:(f + 1) * P], func,
                                   bias=t["stage"][:, i % NST, B1 + f:B1 + f + 1]).then_inc(activated, 1)

        @block.vector
        def _(dve):
            def x_copy(i):
                dve.wait_ge(turned, i + 1)
                if i >= 2:
                    dve.wait_ge(hidden, i - 1)
                dve.tensor_copy(t["x_t"][:, i % 2, :], psum[:, i % 2, 0:P]).then_inc(x_ready, 1)

            def y_copy(i):
                dve.wait_ge(y_done, i + 1)
                if i >= NX:
                    dve.wait_ge(*moved(t["scattered"], t["scatters"], i - NX))
                dve.tensor_tensor(t["y_out"][:, i % NX, :], psum[:, 4 + i % 2, 0:P],
                                  t["stage"][:, i % NST, B2:B2 + P], ALU.add).then_inc(y_ready, 1)

            def stage_weights(i):
                e = dve.value_load(t["expert_of"][0:1, bass.ds(it * KT + i, 1)], min_val=0, max_val=t["E"] - 1)
                if i >= NST:
                    dve.wait_ge(y_ready, i - NST + 1)
                dve.tensor_copy(t["stage"][:, i % NST, :], t["ew"][:, bass.ds(e, 1), :]
                                .rearrange("p a c -> p (a c)")).then_inc(staged, 1)

            stage_weights(0)
            for i in range(KT + 2):
                if i < KT:
                    x_copy(i)
                if i >= 2:
                    y_copy(i - 2)
                if i + 1 < KT:
                    stage_weights(i + 1)


def fetch(sp, t, b, sem):
    sp.dma_start(t["back"][:, :, :, :], t["answers"][bass.ds(b * (2 * L), 2 * L), :]
                 .rearrange("(i p k) d -> p i k d", p=P, k=2)).then_inc(sem, 16)
    sp.wait_ge(sem, 16)


def combine(nc, t, b, out, base):
    with stage(nc, "copied", "step") as (block, copied, step):
        @block.vector
        def _(dve):
            dve.tensor_copy(t["w_now"][:, :, :], t["wt"][:, bass.ds(b * NT, NT), :]).then_inc(copied, 1)
            dve.wait_ge(copied, 1)
            for i in range(NT):
                dve.scalar_tensor_tensor(t["mixed"][:, i, :], t["back"][:, i, 0, :], t["w_now"][:, i, 0:1],
                                         base(i, 1).rearrange("p a d -> p (a d)"), ALU.mult, ALU.add).then_inc(step, 1)
            for i in range(NT):
                dve.wait_ge(step, i + 1)
                dve.scalar_tensor_tensor(out(i, 1).rearrange("p a d -> p (a d)"), t["back"][:, i, 1, :],
                                         t["w_now"][:, i, 1:2], t["mixed"][:, i, :], ALU.mult, ALU.add)


def logits(nc, t, w, layer, b, E):
    with stage(nc, "done", "step", "stored") as (block, done, step, stored):
        @block.sync
        def _(sp):
            sp.dma_start(t["n_rows"][bass.ds(b * L, L), :].rearrange("(i p) d -> p i d", p=P),
                         t["xn"][:, :, :]).then_inc(stored, 16)
            sp.wait_ge(stored, 16)

        @block.tensor
        def _(pe):
            for i in range(NT):
                last = pe.matmul(t["psum"][:, 0, i * E:(i + 1) * E], t["y_t"][:, i * P:(i + 1) * P],
                                 w.gate[layer][:, 0:E], start=True, stop=True)
            last.then_inc(done, 1)

        @block.vector
        def _(dve):
            v = t["lg"][:, bass.ds(b * NT, NT), :]
            dve.wait_ge(done, 1)
            dve.tensor_tensor(v, t["psum"][:, 0, 0:NT * E].rearrange("p (t e) -> p t e", e=E),
                              t["grow"](f"moe{layer}_bg", E), ALU.add).then_inc(step, 1)
            if layer == 0:
                dve.wait_ge(step, 1)
                dve.tensor_tensor(v, v, t["grow"]("moe0_bias", E), ALU.add)

        if layer == 1:
            @block.gpsimd
            def _(pool):
                pool.tensor_copy(t["n_view"](), t["xn"][:, :, :])


def add_to_x(nc, t, what):
    with stage(nc, "unused") as (block, _s):
        @block.vector
        def _(dve):
            dve.tensor_tensor(t["x"](), t["x"](), what[:, :, :], ALU.add)


def attention_inputs(nc, t, w, layer, a, b):
    psum, col = t["psum"], t["col"]
    wq, wk, wqr, wkr, wv, wo = w.att[layer]
    jobs = [(k, h) for k in range(2) for h in range(NH)]
    with stage(nc, "proj_done", "rot_used", "summed", "high", "low", "v_done", "stored", "rot_a", "fetched") as \
            (block, proj_done, rot_used, summed, high, low, v_done, stored, rot_a, fetched):
        @block.sync
        def _(sp):
            if layer == 0:
                fetch(sp, t, (b + 1) % B, fetched)
            for k, (hi, lo) in enumerate((("qh", "ql"), ("kh", "kl"))):
                sp.wait_ge(high, NH * (k + 1))
                sp.dma_start(t["parts"][bass.ds(b, 1), 2 * k, :, :], a[hi][:, :].bitcast(F32)).then_inc(stored, 16)
                sp.wait_ge(low, NH * (k + 1))
                sp.dma_start(t["parts"][bass.ds(b, 1), 2 * k + 1, :, :], a[lo][:, :].bitcast(F32)).then_inc(stored, 16)
            sp.wait_ge(stored, 64)

        @block.tensor
        def _(pe):
            for n, (k, h) in enumerate(jobs):
                if n >= 2:
                    pe.wait_ge(rot_used, n - 1)
                for i, m in enumerate(((wq, wqr), (wk, wkr))[k]):
                    pe.matmul(psum[:, 2 * (n % 2) + i, :], m, t["y_t"][:, h * HALF:(h + 1) * HALF],
                              start=True, stop=True).then_inc(proj_done, 1)
            for i in range(NT):
                last = pe.matmul(psum[:, 4 + i // TPH, (i % TPH) * P:(i % TPH + 1) * P], t["y_t"][:, i * P:(i + 1) * P],
                                 wv, start=True, stop=True)
                if i % TPH == TPH - 1:
                    last.then_inc(v_done, 1)

        @block.vector
        def _(dve):
            def take_low(n):
                k, h = jobs[n]
                s = slice(h * HALF, (h + 1) * HALF)
                hi, lo = ((a["qh"], a["ql"]), (a["kh"], a["kl"]))[k]
                dve.wait_ge(high, n + 1)
                dve.tensor_tensor(lo[:, s], a["rot"][:, n % 2, :], hi[:, s].bitcast(F32),
                                  ALU.subtract).then_inc(low, 1)

            for n, (k, h) in enumerate(jobs):
                s = slice(h * HALF, (h + 1) * HALF)
                name = "qk"[k]
                dve.wait_ge(proj_done, 2 * n + 1)
                if n >= 2:
                    dve.wait_ge(summed, n - 1)
                    dve.wait_ge(low, n - 1)
                dve.scalar_tensor_tensor(a["ra"][:, n % 2, :], psum[:, 2 * (n % 2), :], col(f"att{layer}_b{name}"),
                                         t["cos"][:, s], ALU.add, ALU.mult).then_inc(rot_a, 1)
                dve.wait_ge(proj_done, 2 * n + 2)
                dve.scalar_tensor_tensor(a["rb"][:, n % 2, :], psum[:, 2 * (n % 2) + 1, :],
                                         col(f"att{layer}_b{name}r"), t["sin"][:, s],
                                         ALU.add, ALU.mult).then_inc(rot_used, 1)
                dve.wait_ge(rot_a, n + 1)
                dve.wait_ge(rot_used, n + 1)
                dve.tensor_tensor(a["rot"][:, n % 2, :], a["ra"][:, n % 2, :], a["rb"][:, n % 2, :],
                                  ALU.add).then_inc(summed, 1)
                if n:
                    take_low(n - 1)
            take_low(len(jobs) - 1)
            for h in range(NH):
                dve.wait_ge(v_done, h + 1)
                bias = t["rows"][:, ROWS[f"att{layer}_bv"]:ROWS[f"att{layer}_bv"] + 1, :].to_broadcast([P, TPH, D])
                dve.tensor_tensor(t["v_all"][:, bass.ds(b * NT + h * TPH, TPH), :],
                                  psum[:, 4 + h, :].rearrange("p (i d) -> p i d", d=D), bias, ALU.add)

        @block.gpsimd
        def _(pool):
            pool.tensor_tensor(t["sum"](), (t["x"]() if layer == 0 else t["xn"][:, :, :]),
                               t["row"](f"att{layer}_bo"), ALU.add)

        @block.scalar
        def _(act):
            for n, (k, h) in enumerate(jobs):
                s = slice(h * HALF, (h + 1) * HALF)
                act.wait_ge(summed, n + 1)
                act.activation((a["qh"], a["kh"])[k][:, s], a["rot"][:, n % 2, :], ACT.Copy).then_inc(high, 1)


UN = GH * NT
NKF = 2
NP = 8
S_BANK, NS = 0, 3
M_BANK, NM = 3, 3
O_BANK = 6


def load_group(sp, t, a, b, g, place, sem):
    r = slice(g * GR, (g + 1) * GR)
    for i, (q, k) in enumerate(((0, 2), (0, 3), (1, 2))):
        rows = slice(i * GR, (i + 1) * GR)
        sp.dma_start(a["qs"][rows, g, :].bitcast(F32), t["parts"][bass.ds(b, 1), q, r, :]).then_inc(sem, 16)
        sp.dma_start(a["kf"][rows, place, :].bitcast(F32), t["parts"][bass.ds(b, 1), k, r, :]).then_inc(sem, 16)


def mask_group(pool, t, a, g, place, masked):
    for j in range(GH):
        pool.tensor_scalar(a["kp"][:, g, j, :], a["kf"][:, place, :].bitcast(F32),
                           t["col"]("head_mask", j), 1.0, ALU.mult, ALU.mult).then_inc(masked, 1)


def score_for_maximum(pe, a, bank, g, u, h):
    j, i = divmod(u, NT)
    return pe.matmul(bank, a["qs"][:, g, i * P:(i + 1) * P], a["kp"][:, g, j, h * HALF:(h + 1) * HALF],
                     start=True, stop=True)


def attention_start(nc, t, a):
    psum = t["psum"]
    with stage(nc, "loaded0", "loaded1", "loaded2", "cleared", "masked", "filled", "used") as \
            (block, loaded0, loaded1, loaded2, cleared, masked, filled, used):
        loaded = (loaded0, loaded1, loaded2)

        @block.sync
        def _(sp):
            for g in range(3):
                if g >= NKF:
                    sp.wait_ge(masked, GH * (g - NKF + 1))
                load_group(sp, t, a, 0, g, g % NKF, loaded[g])

        @block.gpsimd
        def _(pool):
            link = chain(pool, cleared)
            link(pool.memset(a["v"][:, :, :, DH:DH + 1], 1.0))
            link(pool.memset(a["v"][:, :, :, DH + 1:VW], 0.0))
            for n in range(NKF):
                link(pool.memset(a["kf"][3 * GR:P, n, :].bitcast(F32), 1.0))
            for g in range(NG):
                link(pool.memset(a["qs"][3 * GR:P, g, :].bitcast(F32), 0.0))
            for g in range(3):
                pool.wait_ge(loaded[g], 96)
                mask_group(pool, t, a, g, g % NKF, masked)

        @block.tensor
        def _(pe):
            pe.wait_ge(loaded[0], 96)
            pe.wait_ge(cleared, 2 + NKF + NG)
            for n in range(UN * NH):
                u, h = divmod(n, NH)
                if u % NT == 0 and h == 0:
                    pe.wait_ge(masked, u // NT + 1)
                if n >= NM:
                    pe.wait_ge(used, n - NM + 1)
                score_for_maximum(pe, a, psum[:, M_BANK + n % NM, :], 0, u, h).then_inc(filled, 1)

        @block.vector
        def _(dve):
            for n in range(UN * NH):
                dve.wait_ge(filled, n + 1)
                dve.tensor_reduce(a["mh"][:, n // NH, n % NH:n % NH + 1], psum[:, M_BANK + n % NM, :],
                                  AX.X, ALU.max).then_inc(used, 1)
            dve.wait_ge(used, UN * NH)
            dve.tensor_reduce(a["mx"][:, 0, :], a["mh"][:, :, :], AX.X, ALU.max)


def attention(nc, t, w, layer, a, b):
    psum = t["psum"]
    fills, per_group = [], []
    for g in range(NG):
        at_unit = {u: [] for u in range(-1, UN + 1)}
        at_unit[-1].append(("turn_max", g, 0, 0))
        for u in range(UN):
            at_unit[u] += [("max", g + 1, u, h) for h in range(NH)]
            if u == 8 and g >= 1:
                at_unit[u] += [("turn_out", g - 1, 0, h) for h in range(NH)]
        if g == NG - 1:
            at_unit[UN] += [("turn_out", g, 0, h) for h in range(NH)]
        per_group.append(at_unit)
        for u in range(-1, UN + 1):
            fills += at_unit[u]
    with stage(nc, "loaded0", "loaded1", "loaded2", "loaded3", "cleared", "masked", "v_set", "filled", "used",
               "merged", "ext_set", "scored", "exped", "weighed", "out_copied", "recip", "o_turned", "o_copied",
               "y_done") as \
            (block, loaded0, loaded1, loaded2, loaded3, cleared, masked, v_set, filled, used,
             merged, ext_set, scored, exped, weighed, out_copied, recip, o_turned, o_copied, y_done):
        loaded = (loaded0, loaded1, loaded2, loaded3)
        ahead = [(b, NG - 1)] + [((b + 1) % B, g) for g in range(NG - 1)]

        @block.sync
        def _(sp):
            for m, (seq, g) in enumerate(ahead):
                if m:
                    sp.wait_ge(scored, NH * UN * m)
                if m >= NKF:
                    sp.wait_ge(masked, GH * (m - NKF + 1))
                load_group(sp, t, a, seq, g, m % NKF, loaded[m])

        @block.gpsimd
        def _(pool):
            pool.tensor_copy(a["v"][:, :, :, 0:DH],
                             t["v_all"][:, bass.ds(b * NT, NT), :].rearrange("p i (h d) -> p i h d", d=DH))\
                .then_inc(v_set, 1)
            pool.wait_ge(v_set, 1)
            for m, (seq, g) in enumerate(ahead):
                if m:
                    pool.wait_ge(scored, NH * UN * m)
                    pool.wait_ge(masked, GH * m)
                pool.memset(a["qs"][3 * GR:P, g, :].bitcast(F32), 0.0).then_inc(cleared, 1)
                pool.wait_ge(cleared, m + 1)
                pool.wait_ge(loaded[m], 96)
                mask_group(pool, t, a, g, m % NKF, masked)

        @block.tensor
        def _(pe):
            made = [0]

            def fill(kind, g, u, h):
                n = made[0]
                made[0] += 1
                bank = psum[:, M_BANK + n % NM, :]
                if n >= NM:
                    pe.wait_ge(used, n - NM + 1)
                if kind == "max":
                    m = g - (NG - 1)
                    if m >= 0 and (u, h) == (0, 0):
                        pe.wait_ge(loaded[m], 96)
                        pe.wait_ge(cleared, m + 1)
                    if m >= 0 and u % NT == 0 and h == 0:
                        pe.wait_ge(masked, GH * m + u // NT + 1)
                    score_for_maximum(pe, a, bank, g % NG, u, h).then_inc(filled, 1)
                elif kind == "turn_max":
                    if g:
                        pe.wait_ge(merged, g)
                    pe.transpose(bank[0:UN, 0:P], a["mx"][:, g % 2, :], t["ident"][:, :]).then_inc(filled, 1)
                else:
                    pe.wait_ge(out_copied, g + 1)
                    for i in range(TPH):
                        q = (h * TPH + i) * P
                        last = pe.transpose(bank[:, i * P:(i + 1) * P], a["o_raw"][:, q:q + P], t["ident"][:, :])
                    last.then_inc(filled, 1)

            def score(g, u, h):
                i, j = divmod(u, GH)
                n = NH * (UN * g + u) + h
                if (u, h) == (0, 0):
                    pe.wait_ge(ext_set, g + 1)
                if n >= NS:
                    pe.wait_ge(exped, n - NS + 1)
                pe.matmul(psum[:, S_BANK + n % NS, :], a["kp"][:, g, j, i * P:(i + 1) * P],
                          a["qs"][:, g, h * HALF:(h + 1) * HALF], start=True, stop=True).then_inc(scored, 1)

            def weigh(k):
                g, (i, h) = k // (NT * NH), divmod(k % (NT * NH), NH)
                pe.wait_ge(exped, NH * (UN * g + GH * (i + 1)))
                if (i, h) == (0, 0):
                    pe.wait_ge(out_copied, g) if g else pe.wait_ge(v_set, 1)
                for j in range(GH):
                    slot = (GH * i + j) % NP
                    last = pe.matmul(psum[GR * j:GR * j + VW, O_BANK + h, :], a["v"][:, i, GH * g + j, :],
                                     a["p"][:, slot, h * HALF:(h + 1) * HALF], start=(i == 0), stop=(i == NT - 1))
                last.then_inc(weighed, 1)

            for g in range(NG):
                for f in per_group[g][-1]:
                    fill(*f)
                for u in range(UN):
                    todo = list(per_group[g][u])
                    for h in range(NH):
                        score(g, u, h)
                        fill(*todo.pop(0))
                    for f in todo:
                        fill(*f)
                    n = UN * g + u
                    if n % 2 and n >= GH + 1:
                        weigh((n - GH - 1) // 2)
            for k in range(NG * NT * NH - 2, NG * NT * NH):
                weigh(k)
            for f in per_group[NG - 1][UN]:
                fill(*f)
            pe.wait_ge(used, len(fills))
            for i in range(NT):
                pe.transpose(psum[:, S_BANK + i // TPH, (i % TPH) * P:(i % TPH + 1) * P], a["o"][:, i, :],
                             t["ident"][:, :]).then_inc(o_turned, 1)
            for i in range(NT):
                pe.wait_ge(o_copied, i // TPH + 1)
                last = pe.matmul(psum[:, M_BANK + i // TPH, (i % TPH) * P:(i % TPH + 1) * P], t["y_t"][:, i * P:(i + 1) * P],
                                 w.att[layer][5], start=True, stop=True)
                if i % TPH == TPH - 1:
                    last.then_inc(y_done, 1)

        @block.scalar
        def _(act):
            def copy_out(g):
                act.wait_ge(weighed, NT * NH * (g + 1))
                if g >= 1:
                    act.wait_ge(filled, fills.index(("turn_out", g - 1, 0, NH - 1)) + 1)
                act.activation(a["o_raw"][:, :], psum[:, O_BANK:O_BANK + 2, :].rearrange("p a d -> p (a d)"),
                               ACT.Copy).then_inc(out_copied, 1)

            for g in range(NG):
                for u in range(UN):
                    n = UN * g + u
                    if u == GH and g >= 1:
                        copy_out(g - 1)
                    if n >= NP:
                        act.wait_ge(weighed, NH * ((n - NP) // GH + 1))
                    for h in range(NH):
                        act.wait_ge(scored, NH * n + h + 1)
                        act.activation(a["p"][:, n % NP, h * HALF:(h + 1) * HALF],
                                       psum[:, S_BANK + (NH * n + h) % NS, :],
                                       ACT.Exp, scale=DH ** -0.5).then_inc(exped, 1)
            copy_out(NG - 1)
            for h in range(NH):
                act.wait_ge(o_turned, TPH * (h + 1))
                act.activation(t["y_t"][:, h * HALF:(h + 1) * HALF], psum[:, S_BANK + h, :], ACT.Copy)\
                    .then_inc(o_copied, 1)

        @block.vector
        def _(dve):
            recips = 0
            for n, (kind, g, u, h) in enumerate(fills):
                bank = psum[:, M_BANK + n % NM, :]
                dve.wait_ge(filled, n + 1)
                if kind == "max":
                    if (u, h) == (0, 0) and g >= 2:
                        dve.wait_ge(merged, g - 1)
                    dve.tensor_reduce(a["mh"][:, u, h:h + 1], bank, AX.X, ALU.max).then_inc(used, 1)
                    if (u, h) == (UN - 1, NH - 1):
                        dve.wait_ge(used, n + 1)
                        dve.tensor_reduce(a["mx"][:, g % 2, :], a["mh"][:, :, :], AX.X, ALU.max).then_inc(merged, 1)
                elif kind == "turn_max":
                    if n:
                        dve.wait_ge(used, n)
                    dve.tensor_tensor(a["qs"][3 * GR:P, g, :].rearrange("p (i c) -> p i c", c=P),
                                      bank[0:UN, 0:P].unsqueeze(1).to_broadcast([UN, NT, P]),
                                      t["neg_diag"][3 * GR:P, :, :], ALU.mult).then_inc(ext_set, 1)
                    dve.wait_ge(ext_set, g + 1)
                    dve.sem_inc(used, 1)
                else:
                    out = bank.rearrange("p (i j c) -> p i j c", i=TPH, j=GH)
                    recips += 1
                    dve.reciprocal(a["rs"][:, recips % 2, :, :], out[:, :, :, DH]).then_inc(recip, 1)
                    dve.wait_ge(recip, recips)
                    o = a["o"][:, h * TPH:(h + 1) * TPH, g * GR:(g + 1) * GR].rearrange("p i (j c) -> p i j c", c=DH)
                    dve.tensor_tensor(o, out[:, :, :, 0:DH],
                                      a["rs"][:, recips % 2, :, :].unsqueeze(3).to_broadcast([P, TPH, GH, DH]),
                                      ALU.mult).then_inc(used, 1)
            for h in range(NH):
                dve.wait_ge(y_done, h + 1)
                dve.tensor_tensor(t["sum"](h * TPH, TPH), psum[:, M_BANK + h, :].rearrange("p (a d) -> p a d", d=D),
                                  t["sum"](h * TPH, TPH), ALU.add)


class Weights:
    pass


def build(nc, x_in, cols_in, rows_in, gates_in, ident_in, cos_in, sin_in, diag_in, w0_in, wo_in, w1_in, w2_in,
          att_in, gate_in, consts_in, moe0_in, moe1_in, out):
    with ExitStack() as ctx:
        names = {}

        def sb(name, shape, dt=F32, where=ctx):
            names[name] = names.get(name, 0) + 1
            return where.enter_context(nc.sbuf_tensor(f"{name}_{names[name]}", shape, dt))

        t = {}
        t["psum"] = ctx.enter_context(nc.psum_tensor("psum", [P, 8, HALF], F32))
        for name in ("xn", "x2"):
            t[name] = sb(name, [P, NT, D])
        x_all = sb("x_all", [P, B * NT, D])
        t["y_t"] = sb("y_t", [P, L])
        cols, rows, gates = sb("cols", [P, NCOLS]), sb("rows", [P, len(ROWS), D]), sb("gates", [P, len(GATES), 16])
        t["rows"] = rows
        t["ident"] = sb("ident", [P, P])
        t["parts"] = nc.dram_tensor("qk_parts", [B, 4, P, L], F32).ap()
        t["moe_loaded"] = ctx.enter_context(nc.semaphore("moe_loaded"))
        t["first_loaded"] = ctx.enter_context(nc.semaphore("first_loaded"))
        t["neg_diag"] = sb("neg_diag", [P, NT, P])
        t["decay"] = sb("decay", [P, CH])
        t["stats"], t["mv"] = sb("stats", [P, NT, 6]), sb("mv", [P, NT, 2])
        for name in ("var", "std", "rstd", "tmp"):
            t[name] = sb(name, [P, NT])
        t["col"] = lambda name, i=0: cols[:, COLS[name][0] + i:COLS[name][0] + i + 1]
        t["row"] = lambda name: rows[:, ROWS[name]:ROWS[name] + 1, :].to_broadcast([P, NT, D])
        t["grow"] = lambda name, E: gates[:, GATES[name]:GATES[name] + 1, 0:E].to_broadcast([P, NT, E])

        w = Weights()
        att = sb("att", [P, 2, 6, P])
        w.att = [[att[:, i, k, :] for k in range(6)] for i in range(2)]
        gate_w = sb("gate_w", [P, 2, 16])
        w.gate = [gate_w[:, i, :] for i in range(2)]
        t["wt"], t["w_now"] = sb("wt", [P, B * NT, 2]), sb("w_now", [P, NT, 2])
        t["n_rows"] = nc.dram_tensor("n_rows", [B * L, D], F32).ap()
        t["answers"] = nc.dram_tensor("answers", [2 * B * L + SLOT_TILES * P, D], F32).ap()
        t["gathered"], t["scattered"] = ([ctx.enter_context(nc.semaphore(f"{n}{i}")) for i in range(PLACES)]
                                         for n in ("gathered", "scattered"))
        t["gathers"], t["scatters"] = [0] * PLACES, [0] * PLACES

        def view(tiles, b):
            return lambda i=0, n=NT: tiles[:, bass.ds(b * NT + i, n), :]

        x_v = x_in.rearrange("b (i p) d -> p (b i) d", p=P)
        with stage(nc, "loaded", "decayed") as (block, loaded, decayed):
            @block.sync
            def _(sp):
                n = 0
                for to, of in ((cols[:, :], cols_in), (rows[:, :, :], rows_in), (gates[:, :, :], gates_in),
                               (t["ident"][:, :], ident_in), 
                               (t["neg_diag"][3 * GR:P, :, :], diag_in), (att[:, :, :, :], att_in),
                               (gate_w[:, :, :], gate_in), (x_all[:, :, :], x_v)):
                    sp.dma_start(to, of).then_inc(loaded, 16)
                    n += 16
                sp.wait_ge(loaded, n)

            @block.scalar
            def _(act):
                act.wait_ge(loaded, 16 * 8)
                lo, hi = COLS["decay"]
                act.activation(t["decay"][:, :], cols[:, lo:hi], ACT.Sigmoid)

        out_v = out.rearrange("b (i p) d -> b p i d", p=P)

        with ExitStack() as scope:
            w0, wo = sb("w0", [P, 4, CH * P], where=scope), sb("wo", [P, CH, D], where=scope)
            w.q, w.k, w.v, w.g = (w0[:, i, :] for i in range(4))
            w.o = wo
            w.w1, w.w2 = sb("w1", [P, FF * P], where=scope), sb("w2", [P, FF, D], where=scope)
            for name, n in (("v", 2), ("g", 2), ("kv", 2), ("state", 2), ("qg", 2), ("gated", 3)):
                t[name] = sb(name, [P, n, HALF], where=scope)
            t["ffh"] = sb("ffh", [P, FF, L], where=scope)
            loads = [(w0[:, i, :], w0_in[i]) for i in range(4)]
            loads += [(wo[:, :, :], wo_in), (w.w1[:, :], w1_in), (w.w2[:, :, :], w2_in)]
            assert len(loads) == FIRST_LOADS
            for to, of in loads:
                nc.sync.dma_start(to, of).then_inc(t["first_loaded"], 16)
            with nc.Fori(0, B) as b:
                t["x"] = view(x_all, b)
                normalise(nc, t, t["x"](), t["xn"])
                normalise(nc, t, t["xn"], t["x2"], t["y_t"], t["col"]("ln1_g"), t["col"]("ln1_b"))
                recurrence(nc, t, w)
                normalise(nc, t, t["x2"], t["xn"], t["y_t"], t["col"]("ln2_g"), t["col"]("ln2_b"))
                feed_forward(nc, t, w)

        def mixture(layer, E, F, func, rounds, KT, prepare):
            W, tiles, T = 2 * F * P + F + D, rounds * KT, B * NT
            with ExitStack() as scope:
                t["E"] = E
                t["ew"] = sb("ew", [P, E, W], where=scope)
                nc.sync.dma_start(t["ew"][:, :, :], (moe0_in, moe1_in)[layer]).then_inc(t["moe_loaded"], 16)
                for name in ("lg", "oh0", "oh1", "both", "pos"):
                    t[name] = sb(name, [P, T, E], where=scope)
                for name in ("cnt", "upto", "over"):
                    t[name] = sb(name, [P, E, T], where=scope)
                for name in ("per", "end", "base"):
                    t[name] = sb(name, [P, 16], where=scope)
                consts = sb("consts", [P, NCONSTS], where=scope)
                for name, (lo, hi) in CONSTS.items():
                    t[name] = consts[:, lo:hi]
                t["mx8"], t["ix8"] = sb("mx8", [P, T, 8], where=scope), sb("ix8", [P, T, 8], U32, where=scope)
                t["sel"], t["tmp2"] = sb("sel", [P, T, 2], where=scope), sb("tmp2", [P, T, 2], where=scope)
                t["ended"], t["who"] = sb("ended", [1, tiles, E], where=scope), sb("who", [1, tiles], where=scope)
                t["expert_of"] = sb("expert_of", [1, tiles], U32, where=scope)
                t["stage"] = sb("stage", [P, 3, W], where=scope)
                t["hi"], t["lo"] = sb("hi", [P, T, 2], where=scope), sb("lo", [P, T, 2], where=scope)
                t["lo_hot"], t["hi_hot"] = sb("lo_hot", [P, 2, INV, P], where=scope), sb("hi_hot", [P, 2 * INV, tiles], where=scope)
                for name in ("place_f", "token_f"):
                    t[name] = sb(name, [P, tiles], where=scope)
                for name in ("place_of", "token_of"):
                    t[name] = sb(name, [P, tiles], U32, where=scope)
                for name in ("place_now", "token_now"):
                    t[name] = sb(name, [P, KT], U32, where=scope)
                for name in ("x_in", "y_out"):
                    t[name] = sb(name, [P, PLACES, D], where=scope)
                t["x_t"], t["hid"] = sb("x_t", [P, 2, P], where=scope), sb("hid", [P, 2, F, P], where=scope)
                nc.sync.dma_start(consts[:, :], consts_in).then_inc(t["moe_loaded"], 16)
                with nc.Fori(0, B) as b:
                    t["x"], t["n_view"] = view(x_all, b), view(n_all, b)
                    prepare(b)
                    logits(nc, t, w, layer, b, E)
                for eng in (nc.vector, nc.tensor, nc.gpsimd):
                    eng.wait_ge(t["moe_loaded"], 32 * (layer + 1))
                route(nc, t, layer, E, tiles)
                invert(nc, t, tiles)
                with nc.Fori(0, rounds) as it:
                    expert_tiles(nc, t, it, KT, F, func)
                for n in range(PLACES):
                    for counts in (t["gathers"], t["scatters"]):
                        counts[n] += 16 * rounds * len(range(n, KT, PLACES))

        def fetch_first(scope):
            t["back"] = sb("back", [P, NT, 2, D], where=scope)
            t["mixed"] = sb("mixed", [P, NT, D], where=scope)
            with stage(nc, "fetched") as (block, fetched):
                @block.sync
                def _(sp):
                    fetch(sp, t, 0, fetched)

        n_all = sb("n_all", [P, B * NT, D])
        mixture(0, 16, 2, ACT.Relu, 5, 16, lambda b: normalise(nc, t, t["x"](), t["xn"], t["y_t"]))

        for layer in range(2):
            with ExitStack() as scope:
                a = {}
                t["v_all"] = sb("v_all", [P, B * NT, D], where=scope)
                target = (x_all, n_all)[layer]
                with ExitStack() as inner:
                    t["cos"], t["sin"] = sb("cos", [P, L], where=inner), sb("sin", [P, L], where=inner)
                    for name in ("qh", "ql", "kh", "kl"):
                        a[name] = sb(name, [P, L], F32R, where=inner)
                    for name in ("ra", "rb", "rot"):
                        a[name] = sb(name, [P, 2, HALF], where=inner)
                    with stage(nc, "loaded") as (block, loaded):
                        @block.sync
                        def _(sp):
                            sp.dma_start(t["cos"][:, :], cos_in).then_inc(loaded, 16)
                            sp.dma_start(t["sin"][:, :], sin_in).then_inc(loaded, 16)
                            sp.wait_ge(loaded, 32)
                    if layer == 0:
                        fetch_first(inner)
                    with nc.Fori(0, B) as b:
                        t["x"], t["sum"] = view(x_all, b), view(target, b)
                        if layer == 0:
                            combine(nc, t, b, t["x"], t["x"])
                        normalise(nc, t, t["x"](), t["xn"], t["y_t"])
                        attention_inputs(nc, t, w, layer, a, b)
                a["v"] = sb("v_ext", [P, NT, HEADS, VW], where=scope)
                a["qs"] = sb("qs", [P, NG, L], F32R, where=scope)
                a["kf"] = sb("kf", [P, NKF, L], F32R, where=scope)
                a["kp"] = sb("kp", [P, NG, GH, L], F32R, where=scope)
                a["p"] = sb("p", [P, NP, L], where=scope)
                a["o_raw"] = sb("o_raw", [P, L], where=scope)
                a["o"] = t["x2"]
                a["mh"] = sb("mh", [P, UN, NH], where=scope)
                a["mx"] = sb("mx", [P, 2, UN], where=scope)
                a["rs"] = sb("rs", [P, 2, TPH, GH], where=scope)
                attention_start(nc, t, a)
                with nc.Fori(0, B) as b:
                    t["sum"] = view(target, b)
                    attention(nc, t, w, layer, a, b)

        mixture(1, 8, 4, ACT.Gelu, 4, 18,
                lambda b: normalise(nc, t, t["n_view"](), t["xn"], t["y_t"],
                                    row_gain=t["row"]("g1"), row_shift=t["row"]("be1")))
        with ExitStack() as scope:
            fetch_first(scope)
            with nc.Fori(0, B) as b:
                t["x"] = view(x_all, b)
                combine(nc, t, b, lambda i, n: t["xn"][:, i:i + n, :], view(n_all, b))
                normalise(nc, t, t["xn"], t["x2"], row_gain=t["row"]("g2"), row_shift=t["row"]("be2"),
                          ahead=(b + 1) % B)
                add_to_x(nc, t, t["x2"])
                with stage(nc, "stored") as (block, stored):
                    @block.sync
                    def _(sp):
                        sp.dma_start(out_v[bass.ds(b, 1), :, :, :], t["x"]()).then_inc(stored, 16)
                        sp.wait_ge(stored, 16)

def layout(i):
    def cols(a):
        return np.reshape(a, (-1, P)).T

    def swap(a):
        s = np.reshape(a, (*a.shape[:-1], HEADS, 2, DH // 2))
        return np.reshape(s[..., ::-1, :], a.shape)

    c = np.zeros((P, NCOLS), np.float32)
    r = np.arange(P)

    def put(name, a):
        c[:, COLS[name][0]:COLS[name][1]] = a

    put("ln1_g", cols(i["L0_attn_ln1_g"])), put("ln1_b", cols(i["L0_attn_ln1_b"]))
    for n in "qkvg":
        put("b" + n, cols(i["L0_attn_b" + n]))
    put("decay", cols(np.repeat(i["L0_attn_decay_logit"], 64)))
    put("ln2_g", cols(i["L0_attn_ln2_g"])), put("ln2_b", cols(i["L0_attn_ln2_b"]))
    put("b1", cols(i["L0_attn_b1"]))
    for k, name in enumerate(("L1_attn_", "L1_ffn_")):
        for n in "qk":
            put(f"att{k}_b{n}", cols(i[f"{name}b{n}"]))
            put(f"att{k}_b{n}r", cols(swap(i[f"{name}b{n}"])))
    put("head_mask", (r[:, None] % GR // DH == np.arange(GH)[None]).astype(np.float32))
    rows = {"bo": "L0_attn_bo", "b2": "L0_attn_b2", "att0_bv": "L1_attn_bv", "att0_bo": "L1_attn_bo",
            "att1_bv": "L1_ffn_bv", "att1_bo": "L1_ffn_bo", "g1": "L1_ffn_g1", "be1": "L1_ffn_be1",
            "g2": "L1_ffn_g2", "be2": "L1_ffn_be2"}
    row = np.stack([i[rows[n]] for n in ROWS])
    gates = np.zeros((len(GATES), 16), np.float32)
    gates[0], gates[1], gates[2, 0:8], gates[3] = i["L0_ffn_bg"], i["L0_ffn_bias"], i["L1_ffn_bg"], np.arange(16)

    inv = (1.0 / np.float32(10000.0) ** (np.arange(0, DH, 2, dtype=np.float32) / np.float32(DH))).astype(np.float32)
    angle = (np.arange(L, dtype=np.float32)[None] * inv[r % (DH // 2)][:, None]).astype(np.float32)
    sign = np.where(r % DH < DH // 2, -1, 1).astype(np.float32)[:, None]
    diag = np.zeros((GR, NT, P), np.float32)
    diag[np.arange(GR), np.arange(GR) % NT, :] = -1.0

    att = []
    for wq, wk, wv, wo in ((i["L1_attn_Wq"].T, i["L1_attn_Wk"].T, i["L1_attn_Wv"].T, i["L1_attn_Wo"].T),
                           (i["L1_ffn_Wq"], i["L1_ffn_Wk"], i["L1_ffn_Wv"], i["L1_ffn_Wo"])):
        att.append(np.stack([wq, wk, swap(wq), swap(wk), wv, wo], 1))
    gate_w = np.zeros((P, 2, 16), np.float32)
    gate_w[:, 0, :], gate_w[:, 1, 0:8] = i["L0_ffn_Wg"], i["L1_ffn_Wg"]
    consts = np.zeros((P, NCONSTS), np.float32)
    for name, value in (("iota", np.arange(P)), ("iota128", P * np.arange(B * NT)),
                        ("keep", np.arange(16 * B * NT) % (B * NT) != 0), ("before", r[:, None] < r[None, :]),
                        ("ones", np.ones(P)),
                        ("place", 1 + (2 * P * np.arange(B * NT)[:, None] + 2 * r[:, None, None]
                                       + np.arange(2)).reshape(P, -1)),
                        ("unfilled", 1 + 2 * B * L + P * np.arange(SLOT_TILES) + r[:, None])):
        consts[:, CONSTS[name][0]:CONSTS[name][1]] = value

    def expert_weights(name):
        w1, w2, b1, b2 = (i[name + n] for n in ("W1", "W2", "b1", "b2"))
        e = w1.shape[0]
        return np.concatenate([
            w1.transpose(1, 0, 2), np.reshape(np.reshape(w2, (e, -1, P, D)).transpose(2, 0, 1, 3), (P, e, -1)),
            np.reshape(b1, (e, -1, P)).transpose(2, 0, 1), np.broadcast_to(b2[None], (P, e, D))], 2)

    arrays = {
        "x": i["L0_attn_x"], "cols": c, "rows": np.broadcast_to(row[None], (P, *row.shape)),
        "gates": np.broadcast_to(gates[None], (P, *gates.shape)), "ident": np.eye(P, dtype=np.float32),
        "cos": np.cos(angle), "sin": np.sin(angle) * sign, "diag": diag,
        "w0": np.stack([i["L0_attn_W" + n] for n in "qkvg"]),
        "wo": np.reshape(i["L0_attn_Wo"], (CH, P, D)).transpose(1, 0, 2), "w1": i["L0_attn_W1"],
        "w2": np.reshape(i["L0_attn_W2"], (FF, P, D)).transpose(1, 0, 2),
        "att": np.stack(att, 1), "gate": gate_w, "consts": consts,
        "moe0": expert_weights("L0_ffn_"), "moe1": expert_weights("L1_ffn_"),
    }
    return {k: np.ascontiguousarray(v) for k, v in arrays.items()}


def kernel(**inputs):
    import concourse.bacc as bacc
    from concourse.bass_utils import run_bass_kernel_spmd

    nc = bacc.Bacc("TRN2", target_bir_lowering=False, num_devices=1, dynamic_dma_scratch_size=2048)
    arrays = {f"in_{k}": v for k, v in layout({k: np.asarray(v) for k, v in inputs.items()}).items()}
    args = [nc.dram_tensor(k, v.shape, mybir.dt.from_np(v.dtype), kind="ExternalInput").ap() for k, v in arrays.items()]
    out = nc.dram_tensor("out", (B, L, D), F32, kind="ExternalOutput").ap()
    build(nc, *args, out)
    return run_bass_kernel_spmd(nc, [arrays], core_ids=[0]).results[0]["out"]
```

```python
import numpy as np
import concourse.bass as bass
from concourse import mybir
from contextlib import ExitStack, contextmanager

F32 = mybir.dt.float32
F32R = mybir.dt.float32r
U32 = mybir.dt.uint32
ALU = mybir.AluOpType
ACT = mybir.ActivationFunctionType
AX = mybir.AxisListType

B, L, D = 4, 1024, 128
P = 128
NT = L // P
HALF = 512
NH = L // HALF
TPH = HALF // P
CH = 16 * 64 // P
FF = 512 // P
HEADS, DH = 16, 8
GH = 4
NG = HEADS // GH
GR = GH * DH
VW = 32
EPS = 1e-5

COLS, at = {}, 0
for name, n in (("ln1_g", 1), ("ln1_b", 1), ("bq", CH), ("bk", CH), ("bv", CH), ("bg", CH), ("decay", CH),
                ("ln2_g", 1), ("ln2_b", 1), ("b1", FF),
                ("att0_bq", 1), ("att0_bk", 1), ("att0_bqr", 1), ("att0_bkr", 1),
                ("att1_bq", 1), ("att1_bk", 1), ("att1_bqr", 1), ("att1_bkr", 1), ("head_mask", GH)):
    COLS[name] = (at, at + n)
    at += n
NCOLS = at
ROWS = {name: i for i, name in enumerate(("bo", "b2", "att0_bv", "att0_bo", "att1_bv", "att1_bo",
                                          "g1", "be1", "g2", "be2"))}
GATES = {name: i for i, name in enumerate(("moe0_bg", "moe0_bias", "moe1_bg"))}


FIRST_LOADS = 13


INV = 8
PLACES = 8
SLOT_TILES = 80
CONSTS, at = {}, 0
for name, n in (("iota", P), ("iota128", B * NT), ("keep", 16 * B * NT), ("before", P), ("ones", P),
                ("place", 2 * B * NT), ("unfilled", SLOT_TILES)):
    CONSTS[name] = (at, at + n)
    at += n
NCONSTS = at


@contextmanager
def stage(nc, *names):
    with ExitStack() as ctx:
        sems = [ctx.enter_context(nc.semaphore(n)) for n in names]
        with nc.Block() as block:
            yield (block, *sems)
        numbers = sorted(s.num for s in sems)
        first = 0
        for n in range(1, len(numbers) + 1):
            if n == len(numbers) or numbers[n] != numbers[n - 1] + 1:
                nc.gpsimd.sem_clear(range(numbers[first], numbers[n - 1] + 1))
                first = n
        nc.all_engine_barrier()


def chain(eng, sem):
    done = [0]

    def link(ins):
        done[0] += 1
        ins.then_inc(sem, 1)
        eng.wait_ge(sem, done[0])

    return link


NORM = ("step", "var_ready", "std_ready", "tile_ready", "turned", "y_copied")


def norm_vector(dve, t, sems, src, dst, twice=None, row_gain=None, row_shift=None):
    step, var_ready, std_ready, tile_ready = sems[:4]
    link = chain(dve, step)
    ways = 1 if twice is None else 2
    var, std, rstd, tmp = (t[k][:, 0:ways, :] for k in ("var", "std", "rstd", "tmp"))
    for i in range(NT):
        last = dve.bn_stats(t["stats"][:, i, :], src[:, i, :])
    link(last)
    for i in range(NT):
        last = dve.bn_aggr(t["mv"][:, i, :], t["stats"][:, i, :])
    link(last)
    last = dve.tensor_scalar(t["var"][:, 0, :], t["mv"][:, :, 1], EPS, None, ALU.add)
    if twice is not None:
        last = dve.tensor_scalar(t["var"][:, 1, :], t["mv"][:, :, 1], 1 + EPS, EPS * EPS, ALU.mult, ALU.add)
    last.then_inc(var_ready, 1)
    dve.wait_ge(std_ready, 1)
    link(dve.reciprocal(rstd, std))
    link(dve.tensor_tensor(tmp, rstd, rstd, ALU.mult))
    link(dve.tensor_tensor(tmp, tmp, var, ALU.mult))
    link(dve.tensor_scalar(tmp, tmp, -0.5, 1.5, ALU.mult, ALU.add))
    link(dve.tensor_tensor(rstd, rstd, tmp, ALU.mult))
    for way, to in ((1, twice), (0, dst)):
        if to is None:
            continue
        for i in range(NT):
            last = dve.tensor_scalar(to[:, i, :], src[:, i, :], t["mv"][:, i, 0:1], t["rstd"][:, way, i:i + 1],
                                     ALU.subtract, ALU.mult)
            if row_gain is None and way == ways - 1:
                last.then_inc(tile_ready, 1)
    if row_gain is not None:
        link(last)
        link(dve.tensor_tensor(dst[:, :, :], dst[:, :, :], row_gain, ALU.mult))
        dve.tensor_tensor(dst[:, :, :], dst[:, :, :], row_shift, ALU.add).then_inc(tile_ready, NT)


def norm_scalar_root(act, t, sems, ways=1):
    act.wait_ge(sems[1], 1)
    act.activation(t["std"][:, 0:ways, :], t["var"][:, 0:ways, :], ACT.Sqrt).then_inc(sems[2], 1)


def norm_scalar_copy(act, t, sems, dst_t, gain=None, shift=None, bank0=0):
    turned, y_copied = sems[4:6]
    for h in range(NH):
        act.wait_ge(turned, TPH * (h + 1))
        out, bank = dst_t[:, h * HALF:(h + 1) * HALF], t["psum"][:, bank0 + h, :]
        if gain is None:
            act.activation(out, bank, ACT.Copy).then_inc(y_copied, 1)
        else:
            act.activation(out, bank, ACT.Identity, scale=gain, bias=shift).then_inc(y_copied, 1)


def norm_tensor(pe, t, sems, dst, bank0=0):
    for i in range(NT):
        pe.wait_ge(sems[3], i + 1)
        pe.transpose(t["psum"][:, bank0 + i // TPH, (i % TPH) * P:(i % TPH + 1) * P], dst[:, i, :],
                     t["ident"][:, :]).then_inc(sems[4], 1)


def split_inputs(act, t, sems, high):
    for h in range(NH):
        act.wait_ge(sems[5], h + 1)
        s = slice(h * HALF, (h + 1) * HALF)
        act.activation(t["y_high"][:, s], t["y_f"][:, s], ACT.Copy).then_inc(high, 1)


def take_low_inputs(dve, t, high):
    for h in range(NH):
        dve.wait_ge(high, h + 1)
        s = slice(h * HALF, (h + 1) * HALF)
        dve.tensor_tensor(t["y_low"][:, s], t["y_f"][:, s], t["y_high"][:, s].bitcast(F32), ALU.subtract)


def recurrence_start(nc, t, w):
    with stage(nc, *NORM, "high", "w_high") as (block, *sems, high, w_high):
        @block.sync
        def _(sp):
            sp.wait_ge(t["first_loaded"], 16 * (FIRST_LOADS - 4))

        @block.vector
        def _(dve):
            norm_vector(dve, t, sems, t["x"](), t["xn"], twice=t["yn"])
            for i in range(4):
                dve.wait_ge(w_high, i + 1)
                dve.tensor_tensor(w.low[:, i, :], t["ffh"][:, i, :], w.high[:, i, :].bitcast(F32),
                                  ALU.subtract)
            take_low_inputs(dve, t, high)

        @block.scalar
        def _(act):
            norm_scalar_root(act, t, sems, 2)
            act.wait_ge(t["weights_loaded"], 16 * 4)
            for i in range(4):
                act.activation(w.high[:, i, :], t["ffh"][:, i, :], ACT.Copy).then_inc(w_high, 1)
            norm_scalar_copy(act, t, sems, t["y_f"], t["col"]("ln1_g"), t["col"]("ln1_b"))
            split_inputs(act, t, sems, high)

        @block.tensor
        def _(pe):
            norm_tensor(pe, t, sems, t["yn"])


def recurrence(nc, t, w):
    units = [(c, h) for c in range(CH) for h in range(NH)]
    NB, LAG, BANKS = 3, 2, 6
    psum, col = t["psum"], t["col"]
    with stage(nc, *NORM, "proj_done", "act_used", "dve_used", "scanned", "gated", "out_done", "x_added", "x_summed") as \
            (block, *sems, proj_done, act_used, dve_used, scanned, gated, out_done, x_added, x_summed):
        @block.tensor
        def _(pe):
            def project(u):
                c, h = units[u]
                for i, m in enumerate((2, 1, 3, 0)):
                    n = 4 * u + i
                    if n >= BANKS:
                        u0, i0 = divmod(n - BANKS, 4)
                        pe.wait_ge(dve_used if i0 % 2 else act_used, 2 * u0 + i0 // 2 + 1)
                    for k, (a, y) in enumerate(((w.high, "y_high"), (w.high, "y_low"), (w.low, "y_high"))):
                        last = pe.matmul(psum[:, n % BANKS, :], a[:, m, c * P:(c + 1) * P],
                                         t[y][:, h * HALF:(h + 1) * HALF], start=(k == 0), stop=(k == 2))
                    last.then_inc(proj_done, 1)

            def output(u):
                c, h = units[u]
                pe.wait_ge(gated, u + 1)
                for i in range(TPH):
                    last = pe.matmul(psum[:, BANKS + h, i * P:(i + 1) * P], t["gated"][:, u % NB, i * P:(i + 1) * P],
                                     w.o[:, c, :], start=(c == 0 and i == 0), stop=(c == CH - 1),
                                     skip_group_check=True)
                last.then_inc(out_done, 1)

            for u in range(len(units) + LAG):
                if u < len(units):
                    project(u)
                if u >= LAG:
                    output(u - LAG)
            norm_tensor(pe, t, sems, t["xn"])

        @block.scalar
        def _(act):
            for u, (c, h) in enumerate(units):
                act.wait_ge(proj_done, 4 * u + 1)
                if u >= 2:
                    act.wait_ge(dve_used, 2 * (u - 2) + 1)
                act.activation(t["v"][:, u % 2, :], psum[:, 4 * u % BANKS, :], ACT.Identity,
                               bias=col("bv", c)).then_inc(act_used, 1)
                act.wait_ge(proj_done, 4 * u + 3)
                if u >= 2:
                    act.wait_ge(dve_used, 2 * (u - 2) + 2)
                act.activation(t["g"][:, u % 2, :], psum[:, (4 * u + 2) % BANKS, :], ACT.Sigmoid,
                               bias=col("bg", c)).then_inc(act_used, 1)
            norm_scalar_root(act, t, sems)
            norm_scalar_copy(act, t, sems, t["y_t"], col("ln2_g"), col("ln2_b"))

        @block.vector
        def _(dve):
            for u, (c, h) in enumerate(units):
                dve.wait_ge(proj_done, 4 * u + 2)
                dve.wait_ge(act_used, 2 * u + 1)
                dve.scalar_tensor_tensor(t["kv"][:, u % 2, :], psum[:, (4 * u + 1) % BANKS, :], col("bk", c),
                                         t["v"][:, u % 2, :], ALU.add, ALU.mult).then_inc(dve_used, 1)
                dve.wait_ge(dve_used, 2 * u + 1)
                if u >= 2:
                    dve.wait_ge(gated, u - 1)
                if h:
                    dve.wait_ge(scanned, u)
                start = t["state"][:, (u - 1) % 2, HALF - 1:HALF] if h else 0.0
                dve.tensor_tensor_scan(t["state"][:, u % 2, :], t["decay"][:, c:c + 1].to_broadcast([P, HALF]),
                                       t["kv"][:, u % 2, :], start, ALU.mult, ALU.add).then_inc(scanned, 1)
                dve.wait_ge(proj_done, 4 * u + 4)
                dve.wait_ge(act_used, 2 * u + 2)
                dve.scalar_tensor_tensor(t["qg"][:, u % 2, :], psum[:, (4 * u + 3) % BANKS, :], col("bq", c),
                                         t["g"][:, u % 2, :], ALU.add, ALU.mult).then_inc(dve_used, 1)
            dve.wait_ge(x_added, 1)
            for h in range(NH):
                dve.wait_ge(out_done, len(units) - NH + h + 1)
                s = slice(h * TPH, (h + 1) * TPH)
                dve.scalar_tensor_tensor(t["x2"][:, s, :], psum[:, BANKS + h, :].rearrange("p (a d) -> p a d", d=D),
                                         64 ** -0.5, t["x2"][:, s, :], ALU.mult, ALU.add).then_inc(x_summed, 1)
            dve.wait_ge(x_summed, NH)
            norm_vector(dve, t, sems, t["x2"], t["xn"])

        @block.gpsimd
        def _(pool):
            pool.tensor_tensor(t["x2"][:, :, :], t["xn"][:, :, :], t["row"]("bo"), ALU.add).then_inc(x_added, 1)
            for u in range(len(units)):
                pool.wait_ge(scanned, u + 1)
                pool.wait_ge(dve_used, 2 * u + 2)
                if u >= NB:
                    pool.wait_ge(out_done, u - NB + 1)
                pool.tensor_tensor(t["gated"][:, u % NB, :], t["state"][:, u % 2, :], t["qg"][:, u % 2, :],
                                   ALU.mult).then_inc(gated, 1)


def feed_forward(nc, t, w):
    psum, col = t["psum"], t["col"]
    with stage(nc, *NORM, "high", "hidden", "gelued", "out_done", "x_step") as \
            (block, *sems, high, hidden, gelued, out_done, x_step):
        @block.tensor
        def _(pe):
            for n in range(FF * NH):
                f, h = n // NH, n % NH
                if n >= 4:
                    pe.wait_ge(gelued, n - 3)
                pe.matmul(psum[:, n % 4, :], w.w1[:, f * P:(f + 1) * P], t["y_t"][:, h * HALF:(h + 1) * HALF],
                          start=True, stop=True).then_inc(hidden, 1)
            norm_tensor(pe, t, sems, t["yn"], 4)
            pe.wait_ge(gelued, FF * NH)
            for i in range(NT):
                for f in range(FF):
                    last = pe.matmul(psum[:, 6 + i // TPH, (i % TPH) * P:(i % TPH + 1) * P],
                                     t["ffh"][:, f, i * P:(i + 1) * P], w.w2[:, f, :],
                                     start=(f == 0), stop=(f == FF - 1))
                last.then_inc(out_done, 1)

        @block.scalar
        def _(act):
            norm_scalar_root(act, t, sems, 2)
            for n in range(FF * NH):
                f, h = n // NH, n % NH
                act.wait_ge(hidden, n + 1)
                act.activation(t["ffh"][:, f, h * HALF:(h + 1) * HALF], psum[:, n % 4, :], ACT.Gelu,
                               bias=col("b1", f)).then_inc(gelued, 1)
            norm_scalar_copy(act, t, sems, t["y_f"], t["col"]("ln1_g"), t["col"]("ln1_b"), 4)
            split_inputs(act, t, sems, high)

        @block.gpsimd
        def _(pool):
            link = chain(pool, x_step)
            link(pool.tensor_tensor(t["x"](), t["x"](), t["x2"][:, :, :], ALU.add))
            link(pool.tensor_tensor(t["x"](), t["x"](), t["row"]("b2"), ALU.add))

        @block.vector
        def _(dve):
            norm_vector(dve, t, sems, t["x_next"](), t["xn"], twice=t["yn"])
            take_low_inputs(dve, t, high)
            dve.wait_ge(x_step, 2)
            for h in range(NH):
                dve.wait_ge(out_done, TPH * (h + 1))
                s = slice(h * TPH, (h + 1) * TPH)
                dve.tensor_tensor(t["x"](h * TPH, TPH), psum[:, 6 + h, :].rearrange("p (a d) -> p a d", d=D),
                                  t["x"](h * TPH, TPH), ALU.add)


def pick_two(dve, link, t, layer, E, to_exp, exped):
    lg, mx, ix, sel, wt, tmp = (t[k] for k in ("lg", "mx8", "ix8", "sel", "wt", "tmp2"))
    L3 = [P, B * NT, E]
    if layer:
        link(dve.tensor_reduce(tmp[:, :, 0], lg[:, :, :], AX.X, ALU.max))
        dve.tensor_tensor(lg[:, :, :], lg[:, :, :], tmp[:, :, 0:1].to_broadcast(L3), ALU.subtract).then_inc(to_exp, 1)
        dve.wait_ge(exped, 1)
        link(dve.tensor_reduce(tmp[:, :, 0], lg[:, :, :], AX.X, ALU.add))
        link(dve.reciprocal(tmp[:, :, 1], tmp[:, :, 0]))
        link(dve.tensor_tensor(lg[:, :, :], lg[:, :, :], tmp[:, :, 1:2].to_broadcast(L3), ALU.mult))
    for i in range(B * NT):
        last = dve.max(mx[:, i, :], lg[:, i, :])
    link(last)
    for i in range(B * NT):
        last = dve.max_index(ix[:, i, :], mx[:, i, :], lg[:, i, :])
    link(last)
    link(dve.tensor_copy(sel[:, :, :], ix[:, :, 0:2]))
    if layer:
        link(dve.tensor_tensor(tmp[:, :, 0], mx[:, :, 0], mx[:, :, 1], ALU.add))
        link(dve.reciprocal(tmp[:, :, 1], tmp[:, :, 0]))
        link(dve.tensor_tensor(wt[:, :, :], mx[:, :, 0:2], tmp[:, :, 1:2].to_broadcast([P, B * NT, 2]), ALU.mult))
    else:
        dve.tensor_tensor(tmp[:, :, 0], mx[:, :, 1], mx[:, :, 0], ALU.subtract).then_inc(to_exp, 1)
        dve.wait_ge(exped, 1)
        link(dve.tensor_scalar(tmp[:, :, 0], tmp[:, :, 1], 1.0, None, ALU.add))
        link(dve.reciprocal(wt[:, :, 0], tmp[:, :, 0]))
        link(dve.tensor_tensor(wt[:, :, 1], tmp[:, :, 1], wt[:, :, 0], ALU.mult))


def route(nc, t, layer, E, tiles):
    psum, T, TE = t["psum"], B * NT, B * NT * E
    lg, sel, oh0, oh1, both, pos, cnt, upto = (t[k] for k in ("lg", "sel", "oh0", "oh1", "both", "pos", "cnt", "upto"))
    per, end, base = t["per"], t["end"], t["base"]
    L3 = [P, T, E]
    iota = t["iota"]
    with stage(nc, "step", "to_exp", "exped", "both_ready", "counted") as \
            (block, step, to_exp, exped, both_ready, counted):
        @block.scalar
        def _(act):
            act.wait_ge(to_exp, 1)
            if layer:
                act.activation(lg[:, :, :], lg[:, :, :], ACT.Exp).then_inc(exped, 1)
            else:
                act.activation(t["tmp2"][:, :, 1], t["tmp2"][:, :, 0], ACT.Exp).then_inc(exped, 1)

        @block.tensor
        def _(pe):
            pe.wait_ge(both_ready, 1)
            both_flat = both[:, :, :].rearrange("p t e -> p (t e)")
            pe.matmul(psum[:, 0, 0:TE], t["before"][:, :], both_flat, start=True, stop=True)
            pe.matmul(psum[:, 1, 0:TE], t["ones"][:, :], both_flat, start=True, stop=True).then_inc(counted, 1)

        @block.vector
        def _(dve):
            link = chain(dve, step)
            pick_two(dve, link, t, layer, E, to_exp, exped)
            experts_row = iota[:, 0:E].unsqueeze(1).to_broadcast(L3)
            dve.tensor_tensor(oh0[:, :, :], experts_row, sel[:, :, 0:1].to_broadcast(L3), ALU.is_equal)
            link(dve.tensor_tensor(oh1[:, :, :], experts_row, sel[:, :, 1:2].to_broadcast(L3), ALU.is_equal))
            link(dve.tensor_tensor(both[:, :, :], oh0[:, :, :], oh1[:, :, :], ALU.add))
            dve.sem_inc(both_ready, 1)
            dve.wait_ge(counted, 1)
            link(dve.tensor_copy(cnt[:, :, :], psum[:, 1, 0:TE].rearrange("p (t e) -> p e t", e=E)))
            link(dve.tensor_tensor_scan(upto[:, :, :].rearrange("p e t -> p (e t)"), t["keep"][:, 0:TE],
                                        cnt[:, :, :].rearrange("p e t -> p (e t)"), 0.0, ALU.mult, ALU.add))
            link(dve.tensor_tensor(cnt[:, :, :], upto[:, :, :], cnt[:, :, :], ALU.subtract))
            link(dve.tensor_tensor(t["over"][:, :, :], upto[:, :, T - 1:T].to_broadcast([P, E, T]),
                                   t["iota128"][:, 0:T].unsqueeze(1).to_broadcast([P, E, T]), ALU.is_gt))
            link(dve.tensor_reduce(per[:, 0:E], t["over"][:, :, :], AX.X, ALU.add))
            link(dve.tensor_tensor_scan(end[:, 0:E], t["ones"][:, 0:E], per[:, 0:E], 0.0, ALU.mult, ALU.add))
            link(dve.tensor_tensor(base[:, 0:E], end[:, 0:E], per[:, 0:E], ALU.subtract))
            link(dve.tensor_scalar(base[:, 0:E], base[:, 0:E], float(P), None, ALU.mult))
            link(dve.tensor_tensor(pos[:, :, :], psum[:, 0, 0:TE].rearrange("p (t e) -> p t e", e=E),
                                   cnt[:, :, :].rearrange("p e t -> p t e"), ALU.add))
            link(dve.tensor_tensor(pos[:, :, :], pos[:, :, :], base[:, 0:E].unsqueeze(1).to_broadcast(L3), ALU.add))
            dve.tensor_tensor(oh0[:, :, :], oh0[:, :, :], pos[:, :, :], ALU.mult)
            link(dve.tensor_tensor(oh1[:, :, :], oh1[:, :, :], pos[:, :, :], ALU.mult))
            dve.tensor_reduce(sel[:, :, 0], oh0[:, :, :], AX.X, ALU.add)
            link(dve.tensor_reduce(sel[:, :, 1], oh1[:, :, :], AX.X, ALU.add))
            row = [1, tiles, E]
            link(dve.tensor_tensor(t["ended"][:, 0:tiles, :], iota[0:1, 0:tiles].unsqueeze(2).to_broadcast(row),
                                   end[0:1, 0:E].unsqueeze(1).to_broadcast(row), ALU.is_ge))
            link(dve.tensor_reduce(t["who"][:, 0:tiles], t["ended"][:, 0:tiles, :], AX.X, ALU.add))
            dve.tensor_scalar(t["expert_of"][:, 0:tiles], t["who"][:, 0:tiles], float(E - 1), None, ALU.min)


def floor(dve, link, x, lowest):
    link(dve.tensor_scalar(x, x, -lowest, None, ALU.add))
    link(dve.tensor_scalar(x, x, float(3 * 2 ** 22), None, ALU.add))
    link(dve.tensor_scalar(x, x, -float(3 * 2 ** 22), None, ALU.add))


def invert(nc, t, tiles):
    psum, T = t["psum"], B * NT
    sel, hi, lo, G = t["sel"], t["hi"], t["lo"], INV
    pairs = 2 * T
    flat = lambda a: a[:, :, :].rearrange("p t k -> p (t k)")
    with stage(nc, "step", "lo_ready", "hi_ready", "used") as (block, step, lo_ready, hi_ready, used):
        @block.vector
        def _(dve):
            link = chain(dve, step)
            link(dve.tensor_scalar(hi[:, :, :], sel[:, :, :], 1.0 / P, None, ALU.mult))
            floor(dve, link, hi[:, :, :], 0.5 - 0.5 / P)
            link(dve.scalar_tensor_tensor(lo[:, :, :], hi[:, :, :], -float(P), sel[:, :, :], ALU.mult, ALU.add))
            for c in range(pairs // G):
                if c >= 2:
                    dve.wait_ge(used, G * (c - 1))
                dve.tensor_tensor(t["lo_hot"][:, c % 2, :, :], t["iota"][:, 0:P].unsqueeze(1).to_broadcast([P, G, P]),
                                  flat(lo)[:, c * G:(c + 1) * G].unsqueeze(2).to_broadcast([P, G, P]),
                                  ALU.is_equal).then_inc(lo_ready, 1)
                for n in range(c * G, (c + 1) * G):
                    dve.tensor_scalar(t["hi_hot"][:, n % (2 * G), 0:tiles], t["iota"][:, 0:tiles],
                                      flat(hi)[:, n:n + 1], t["place"][:, n:n + 1],
                                      ALU.is_equal, ALU.mult).then_inc(hi_ready, 1)
            dve.wait_ge(used, pairs)
            v, place, token = psum[:, 2, 0:tiles], t["place_f"][:, 0:tiles], t["token_f"][:, 0:tiles]
            link(dve.tensor_scalar(token, v, -1.0, 0.0, ALU.add, ALU.max))
            link(dve.tensor_scalar(token, token, 0.5, None, ALU.mult))
            floor(dve, link, token, 0.25)
            link(dve.tensor_scalar(place, v, 0.0, None, ALU.is_equal))
            link(dve.tensor_tensor(place, place, t["unfilled"][:, 0:tiles], ALU.mult))
            link(dve.tensor_tensor(place, place, v, ALU.add))
            link(dve.tensor_scalar(place, place, -1.0, None, ALU.add))
            dve.tensor_copy(t["token_of"][:, 0:tiles], token)
            dve.tensor_copy(t["place_of"][:, 0:tiles], place)

        @block.tensor
        def _(pe):
            for n in range(pairs):
                if n % G == 0:
                    pe.wait_ge(lo_ready, n // G + 1)
                pe.wait_ge(hi_ready, n + 1)
                last = pe.matmul(psum[:, 2, 0:tiles], t["lo_hot"][:, (n // G) % 2, n % G, :],
                                 t["hi_hot"][:, n % (2 * G), 0:tiles], start=(n == 0), stop=(n == pairs - 1))
                last.then_inc(used, 1)


def expert_tiles(nc, t, it, KT, F, func):
    psum, W1, W2, B1 = t["psum"], 0, F * P, 2 * F * P
    B2 = B1 + F
    NX, NST = PLACES, 3
    with stage(nc, "indices", "staged", "turned", "x_ready", "hidden", "activated", "y_done", "y_ready") as \
            (block, indices, staged, turned, x_ready, hidden, activated, y_done, y_ready):
        def moved(sems, counts, i):
            n = i % NX
            turns = len(range(n, KT, NX))
            return sems[n], it * (16 * turns) + (counts[n] + 16 * (i // NX + 1))

        @block.gpsimd
        def _(pool):
            pool.tensor_copy(t["token_now"][:, 0:KT], t["token_of"][:, bass.ds(it * KT, KT)]).then_inc(indices, 1)
            pool.tensor_copy(t["place_now"][:, 0:KT], t["place_of"][:, bass.ds(it * KT, KT)]).then_inc(indices, 1)
            pool.wait_ge(indices, 2)

            def gather(i):
                if i >= NX:
                    pool.wait_ge(turned, i - NX + 1)
                pool.indirect_dma_start(t["x_in"][:, i % NX, :], None, t["n_rows"],
                                        bass.IndirectOffsetOnAxis(ap=t["token_now"][:, i:i + 1], axis=0))\
                    .then_inc(t["gathered"][i % NX], 16)

            for i in range(NX - 1):
                gather(i)
            for i in range(KT):
                if i + NX - 1 < KT:
                    gather(i + NX - 1)
                pool.wait_ge(y_ready, i + 1)
                pool.indirect_dma_start(t["answers"],
                                        bass.IndirectOffsetOnAxis(ap=t["place_now"][:, i:i + 1], axis=0),
                                        t["y_out"][:, i % NX, :], None).then_inc(t["scattered"][i % NX], 16)
            for i in range(KT - NX, KT):
                pool.wait_ge(*moved(t["scattered"], t["scatters"], i))

        @block.tensor
        def _(pe):
            def turn(i):
                pe.wait_ge(*moved(t["gathered"], t["gathers"], i))
                if i >= 2:
                    pe.wait_ge(x_ready, i - 1)
                pe.transpose(psum[:, i % 2, 0:P], t["x_in"][:, i % NX, :], t["ident"][:, :]).then_inc(turned, 1)

            def up(i):
                pe.wait_ge(x_ready, i + 1)
                pe.wait_ge(staged, i + 1)
                if i >= 2:
                    pe.wait_ge(activated, F * (i - 1))
                for f in range(F):
                    last = pe.matmul(psum[:, 2 + i % 2, f * P:(f + 1) * P],
                                     t["stage"][:, i % NST, W1 + f * P:W1 + (f + 1) * P], t["x_t"][:, i % 2, :],
                                     start=True, stop=True)
                last.then_inc(hidden, 1)

            def down(i):
                pe.wait_ge(activated, F * (i + 1))
                if i >= 2:
                    pe.wait_ge(y_ready, i - 1)
                for f in range(F):
                    last = pe.matmul(psum[:, 4 + i % 2, 0:P], t["hid"][:, i % 2, f, :],
                                     t["stage"][:, i % NST, W2 + f * P:W2 + (f + 1) * P],
                                     start=(f == 0), stop=(f == F - 1))
                last.then_inc(y_done, 1)

            for i in range(KT + 2):
                if i < KT:
                    turn(i)
                if 1 <= i <= KT:
                    up(i - 1)
                if i >= 2:
                    down(i - 2)

        @block.scalar
        def _(act):
            for i in range(KT):
                act.wait_ge(hidden, i + 1)
                if i >= 2:
                    act.wait_ge(y_done, i - 1)
                for f in range(F):
                    act.activation(t["hid"][:, i % 2, f, :], psum[:, 2 + i % 2, f * P:(f + 1) * P], func,
                                   bias=t["stage"][:, i % NST, B1 + f:B1 + f + 1]).then_inc(activated, 1)

        @block.vector
        def _(dve):
            def x_copy(i):
                dve.wait_ge(turned, i + 1)
                if i >= 2:
                    dve.wait_ge(hidden, i - 1)
                dve.tensor_copy(t["x_t"][:, i % 2, :], psum[:, i % 2, 0:P]).then_inc(x_ready, 1)

            def y_copy(i):
                dve.wait_ge(y_done, i + 1)
                if i >= NX:
                    dve.wait_ge(*moved(t["scattered"], t["scatters"], i - NX))
                dve.tensor_tensor(t["y_out"][:, i % NX, :], psum[:, 4 + i % 2, 0:P],
                                  t["stage"][:, i % NST, B2:B2 + P], ALU.add).then_inc(y_ready, 1)

            def stage_weights(i):
                e = dve.value_load(t["expert_of"][0:1, bass.ds(it * KT + i, 1)], min_val=0, max_val=t["E"] - 1)
                if i >= NST:
                    dve.wait_ge(y_ready, i - NST + 1)
                dve.tensor_copy(t["stage"][:, i % NST, :], t["ew"][:, bass.ds(e, 1), :]
                                .rearrange("p a c -> p (a c)")).then_inc(staged, 1)

            stage_weights(0)
            for i in range(KT + 2):
                if i < KT:
                    x_copy(i)
                if i >= 2:
                    y_copy(i - 2)
                if i + 1 < KT:
                    stage_weights(i + 1)


def fetch(sp, t, b, sem):
    sp.dma_start(t["back"][:, :, :, :], t["answers"][bass.ds(b * (2 * L), 2 * L), :]
                 .rearrange("(i p k) d -> p i k d", p=P, k=2)).then_inc(sem, 16)


def combine(dve, t, b, copied, mixed, out, base):
    dve.tensor_copy(t["w_now"][:, :, :], t["wt"][:, bass.ds(b * NT, NT), :]).then_inc(copied, 1)
    dve.wait_ge(copied, 1)
    for i in range(NT):
        dve.scalar_tensor_tensor(t["mixed"][:, i, :], t["back"][:, i, 0, :], t["w_now"][:, i, 0:1],
                                 base(i, 1).rearrange("p a d -> p (a d)"), ALU.mult, ALU.add).then_inc(mixed, 1)
    for i in range(NT):
        dve.wait_ge(mixed, i + 1)
        dve.scalar_tensor_tensor(out(i, 1).rearrange("p a d -> p (a d)"), t["back"][:, i, 1, :],
                                 t["w_now"][:, i, 1:2], t["mixed"][:, i, :], ALU.mult, ALU.add).then_inc(mixed, 1)
    dve.wait_ge(mixed, 2 * NT)


def gate_logits(nc, t, w, layer, b, E, src, row_gain=None, row_shift=None):
    with stage(nc, *NORM, "done", "logit_step", "stored") as (block, *sems, done, logit_step, stored):
        @block.sync
        def _(sp):
            sp.wait_ge(sems[3], NT)
            sp.dma_start(t["n_rows"][bass.ds(b * L, L), :].rearrange("(i p) d -> p i d", p=P),
                         t["xn"][:, :, :]).then_inc(stored, 16)
            sp.wait_ge(stored, 16)

        if layer == 1:
            @block.gpsimd
            def _(pool):
                pool.wait_ge(sems[3], NT)
                pool.tensor_copy(t["n_view"](), t["xn"][:, :, :])

        @block.scalar
        def _(act):
            norm_scalar_root(act, t, sems)
            norm_scalar_copy(act, t, sems, t["y_t"])

        @block.tensor
        def _(pe):
            norm_tensor(pe, t, sems, t["xn"])
            for i in range(NT):
                pe.wait_ge(sems[5], i // TPH + 1)
                last = pe.matmul(t["psum"][:, 2, i * E:(i + 1) * E], t["y_t"][:, i * P:(i + 1) * P],
                                 w.gate[layer][:, 0:E], start=True, stop=True)
            last.then_inc(done, 1)

        @block.vector
        def _(dve):
            norm_vector(dve, t, sems, src, t["xn"], row_gain=row_gain, row_shift=row_shift)
            v = t["lg"][:, bass.ds(b * NT, NT), :]
            dve.wait_ge(done, 1)
            dve.tensor_tensor(v, t["psum"][:, 2, 0:NT * E].rearrange("p (t e) -> p t e", e=E),
                              t["grow"](f"moe{layer}_bg", E), ALU.add).then_inc(logit_step, 1)
            if layer == 0:
                dve.wait_ge(logit_step, 1)
                dve.tensor_tensor(v, v, t["grow"]("moe0_bias", E), ALU.add)


def finish(nc, t, b):
    xn, x2, x = t["xn"], t["x2"], t["x"]
    with stage(nc, *NORM, "copied", "mixed", "fetched", "added") as (block, *sems, copied, mixed, fetched, added):
        @block.sync
        def _(sp):
            sp.wait_ge(mixed, 2 * NT)
            fetch(sp, t, (b + 1) % B, fetched)
            for h in range(NH):
                sp.wait_ge(added, h + 1)
                sp.dma_start(t["out_v"][bass.ds(b, 1), :, h * TPH:(h + 1) * TPH, :], x(h * TPH, TPH))\
                    .then_inc(t["out_stored"], 16)
            sp.wait_ge(fetched, 16)

        @block.scalar
        def _(act):
            norm_scalar_root(act, t, sems)

        @block.vector
        def _(dve):
            combine(dve, t, b, copied, mixed, lambda i, n: xn[:, i:i + n, :], t["n_view"])
            norm_vector(dve, t, sems, xn, x2, row_gain=t["row"]("g2"), row_shift=t["row"]("be2"))
            dve.wait_ge(sems[3], NT)
            for h in range(NH):
                dve.tensor_tensor(x(h * TPH, TPH), x(h * TPH, TPH), x2[:, h * TPH:(h + 1) * TPH, :],
                                  ALU.add).then_inc(added, 1)


def attention_inputs(nc, t, w, layer, a, b):
    psum, col = t["psum"], t["col"]
    wq, wk, wqr, wkr, wv, wo = w.att[layer]
    jobs = [(k, h) for k in range(2) for h in range(NH)]
    with stage(nc, *NORM, "proj_done", "rot_used", "summed", "high", "low", "v_done", "rot_a", "fetched",
               "copied", "mixed") as \
            (block, *sems, proj_done, rot_used, summed, high, low, v_done, rot_a, fetched, copied, mixed):
        stored, before = t["parts_stored"], b * 64 + (1 + 64 * B * layer)
        @block.sync
        def _(sp):
            if layer == 0:
                sp.wait_ge(mixed, 2 * NT)
                fetch(sp, t, (b + 1) % B, fetched)
            for k, (hi, lo) in enumerate((("qh", "ql"), ("kh", "kl"))):
                sp.wait_ge(high, NH * (k + 1))
                sp.dma_start(t["parts"][bass.ds(b, 1), 2 * k, :, :], a[hi][:, :].bitcast(F32)).then_inc(stored, 16)
                sp.wait_ge(low, NH * (k + 1))
                sp.dma_start(t["parts"][bass.ds(b, 1), 2 * k + 1, :, :], a[lo][:, :].bitcast(F32)).then_inc(stored, 16)
            if layer == 0:
                sp.wait_ge(fetched, 16)

        @block.tensor
        def _(pe):
            norm_tensor(pe, t, sems, t["xn"], 6)
            for n, (k, h) in enumerate(jobs):
                if n >= 2:
                    pe.wait_ge(rot_used, n - 1)
                pe.wait_ge(sems[5], h + 1)
                for i, m in enumerate(((wq, wqr), (wk, wkr))[k]):
                    pe.matmul(psum[:, 2 * (n % 2) + i, :], m, t["y_t"][:, h * HALF:(h + 1) * HALF],
                              start=True, stop=True).then_inc(proj_done, 1)
            for i in range(NT):
                last = pe.matmul(psum[:, 4 + i // TPH, (i % TPH) * P:(i % TPH + 1) * P], t["y_t"][:, i * P:(i + 1) * P],
                                 wv, start=True, stop=True)
                if i % TPH == TPH - 1:
                    last.then_inc(v_done, 1)

        @block.vector
        def _(dve):
            if layer == 0:
                combine(dve, t, b, copied, mixed, t["x"], t["x"])
            norm_vector(dve, t, sems, t["x"](), t["xn"])
            for n, (k, h) in enumerate(jobs):
                s = slice(h * HALF, (h + 1) * HALF)
                name = "qk"[k]
                dve.wait_ge(proj_done, 2 * n + 1)
                if n >= 2:
                    dve.wait_ge(summed, n - 1)
                    dve.wait_ge(low, n - 1)
                dve.scalar_tensor_tensor(a["ra"][:, n % 2, :], psum[:, 2 * (n % 2), :], col(f"att{layer}_b{name}"),
                                         t["cos"][:, s], ALU.add, ALU.mult).then_inc(rot_a, 1)
                dve.wait_ge(proj_done, 2 * n + 2)
                dve.scalar_tensor_tensor(a["rb"][:, n % 2, :], psum[:, 2 * (n % 2) + 1, :],
                                         col(f"att{layer}_b{name}r"), t["sin"][:, s],
                                         ALU.add, ALU.mult).then_inc(rot_used, 1)
                dve.wait_ge(rot_a, n + 1)
                dve.wait_ge(rot_used, n + 1)
                dve.tensor_tensor(a["rot"][:, n % 2, :], a["ra"][:, n % 2, :], a["rb"][:, n % 2, :],
                                  ALU.add).then_inc(summed, 1)
            for h in range(NH):
                dve.wait_ge(v_done, h + 1)
                bias = t["rows"][:, ROWS[f"att{layer}_bv"]:ROWS[f"att{layer}_bv"] + 1, :].to_broadcast([P, TPH, D])
                dve.tensor_tensor(t["v_all"][:, bass.ds(b * NT + h * TPH, TPH), :],
                                  psum[:, 4 + h, :].rearrange("p (i d) -> p i d", d=D), bias, ALU.add)

        @block.gpsimd
        def _(pool):
            def take_low(n):
                k, h = jobs[n]
                s = slice(h * HALF, (h + 1) * HALF)
                hi, lo = ((a["qh"], a["ql"]), (a["kh"], a["kl"]))[k]
                pool.wait_ge(high, n + 1)
                pool.wait_ge(stored, before)
                pool.tensor_tensor(lo[:, s], a["rot"][:, n % 2, :], hi[:, s].bitcast(F32),
                                  ALU.subtract).then_inc(low, 1)

            pool.wait_ge(sems[3], NT)
            pool.tensor_tensor(t["sum"](), (t["x"]() if layer == 0 else t["xn"][:, :, :]),
                               t["row"](f"att{layer}_bo"), ALU.add)
            for n in range(len(jobs)):
                take_low(n)

        @block.scalar
        def _(act):
            norm_scalar_root(act, t, sems)
            norm_scalar_copy(act, t, sems, t["y_t"], bank0=6)
            for n, (k, h) in enumerate(jobs):
                s = slice(h * HALF, (h + 1) * HALF)
                act.wait_ge(summed, n + 1)
                act.wait_ge(stored, before)
                act.activation((a["qh"], a["kh"])[k][:, s], a["rot"][:, n % 2, :], ACT.Copy).then_inc(high, 1)


UN = GH * NT
NKF = 2
NP = 8
S_BANK, NS = 0, 3
M_BANK, NM = 3, 3
O_BANK = 6
MAX_UNITS = 30


def load_group(sp, t, a, b, g, place, sem):
    r = slice(g * GR, (g + 1) * GR)
    for i, (q, k) in enumerate(((0, 2), (0, 3), (1, 2))):
        rows = slice(i * GR, (i + 1) * GR)
        sp.dma_start(a["qs"][rows, g, :].bitcast(F32), t["parts"][bass.ds(b, 1), q, r, :]).then_inc(sem, 16)
        sp.dma_start(a["kf"][rows, place, :].bitcast(F32), t["parts"][bass.ds(b, 1), k, r, :]).then_inc(sem, 16)


def mask_group(pool, t, a, g, place, masked):
    for j in range(GH):
        pool.tensor_scalar(a["kp"][:, g, j, :], a["kf"][:, place, :].bitcast(F32),
                           t["col"]("head_mask", j), 1.0, ALU.mult, ALU.mult).then_inc(masked, 1)


def score_for_maximum(pe, a, bank, g, u, h):
    j, i = divmod(u, NT)
    return pe.matmul(bank, a["qs"][:, g, i * P:(i + 1) * P], a["kp"][:, g, j, h * HALF:(h + 1) * HALF],
                     start=True, stop=True)


def subtract_maxima(dve, t, a, g, turned):
    return dve.tensor_tensor(a["qs"][3 * GR:P, g, :].rearrange("p (i c) -> p i c", c=P),
                             turned.unsqueeze(1).to_broadcast([UN, NT, P]), t["neg_diag"][3 * GR:P, :, :], ALU.mult)


def attention_start(nc, t, layer, a):
    psum = t["psum"]
    with stage(nc, "loaded0", "loaded1", "loaded2", "cleared", "masked", "filled", "used", "merged", "turned") as \
            (block, loaded0, loaded1, loaded2, cleared, masked, filled, used, merged, turned):
        loaded = (loaded0, loaded1, loaded2)

        @block.sync
        def _(sp):
            sp.wait_ge(t["parts_stored"], 1 + 64 * B * (layer + 1))
            for g in range(3):
                if g >= NKF:
                    sp.wait_ge(masked, GH * (g - NKF + 1))
                load_group(sp, t, a, 0, g, g % NKF, loaded[g])

        @block.gpsimd
        def _(pool):
            pool.wait_ge(t["parts_stored"], 1 + 64 * B * (layer + 1))
            link = chain(pool, cleared)
            for n in range(NKF):
                link(pool.memset(a["kf"][3 * GR:P, n, :].bitcast(F32), 1.0))
            link(pool.memset(a["qs"][3 * GR:P, 0, :].bitcast(F32), 0.0))
            for g in range(3):
                pool.wait_ge(loaded[g], 96)
                mask_group(pool, t, a, g, g % NKF, masked)

        @block.tensor
        def _(pe):
            pe.wait_ge(loaded[0], 96)
            pe.wait_ge(cleared, NKF + 1)
            for n in range(UN * NH):
                u, h = divmod(n, NH)
                if u % NT == 0 and h == 0:
                    pe.wait_ge(masked, u // NT + 1)
                if n >= NM:
                    pe.wait_ge(used, n - NM + 1)
                score_for_maximum(pe, a, psum[:, M_BANK + n % NM, :], 0, u, h).then_inc(filled, 1)
            pe.wait_ge(merged, 1)
            pe.transpose(psum[0:UN, M_BANK, 0:P], a["mx"][:, 0, :], t["ident"][:, :]).then_inc(turned, 1)

        @block.vector
        def _(dve):
            dve.wait_ge(t["parts_stored"], 1 + 64 * B * (layer + 1))
            dve.memset(a["v"][:, :, :, DH:DH + 1], 1.0)
            dve.memset(a["v"][:, :, :, DH + 1:VW], 0.0)
            for g in range(1, NG):
                dve.memset(a["qs"][3 * GR:P, g, :].bitcast(F32), 0.0)
            for n in range(UN * NH):
                dve.wait_ge(filled, n + 1)
                dve.tensor_reduce(a["mh"][:, n // NH, n % NH:n % NH + 1], psum[:, M_BANK + n % NM, :],
                                  AX.X, ALU.max).then_inc(used, 1)
            dve.wait_ge(used, UN * NH)
            dve.tensor_reduce(a["mx"][:, 0, :], a["mh"][:, :, :], AX.X, ALU.max).then_inc(merged, 1)
            dve.wait_ge(turned, 1)
            subtract_maxima(dve, t, a, 0, psum[0:UN, M_BANK, 0:P])


def attention(nc, t, w, layer, a, b):
    psum = t["psum"]
    fills, per_group = [], []
    for g in range(NG):
        at_unit = {u: [] for u in range(UN + 1)}
        for u in range(UN):
            at_unit[u] += [("max", g + 1, *divmod(n, NH)) for n in range(NH * UN)
                           if n * MAX_UNITS // (NH * UN) == u]
            if u == UN - 1:
                at_unit[u].append(("turn_max", g + 1, 0, 0))
            if u == UN - 1 and g >= 1:
                at_unit[u] += [("turn_out", g - 1, 0, h) for h in range(NH)]
        if g == NG - 1:
            at_unit[UN] += [("turn_out", g, 0, h) for h in range(NH)]
        per_group.append(at_unit)
        for u in range(UN + 1):
            fills += at_unit[u]
    with stage(nc, "loaded0", "loaded1", "loaded2", "loaded3", "cleared", "masked", "v_set", "filled", "used",
               "merged", "ext_set", "scored", "exped", "weighed", "out_copied", "recip", "o_turned", "o_copied",
               "y_done") as \
            (block, loaded0, loaded1, loaded2, loaded3, cleared, masked, v_set, filled, used,
             merged, ext_set, scored, exped, weighed, out_copied, recip, o_turned, o_copied, y_done):
        loaded = (loaded0, loaded1, loaded2, loaded3)
        ahead = [(b, NG - 1)] + [((b + 1) % B, g) for g in range(NG - 1)]

        @block.sync
        def _(sp):
            for m, (seq, g) in enumerate(ahead):
                if m:
                    sp.wait_ge(scored, NH * UN * m)
                if m >= NKF:
                    sp.wait_ge(masked, GH * (m - NKF + 1))
                load_group(sp, t, a, seq, g, m % NKF, loaded[m])

        @block.gpsimd
        def _(pool):
            pool.tensor_copy(a["v"][:, :, :, 0:DH],
                             t["v_all"][:, bass.ds(b * NT, NT), :].rearrange("p i (h d) -> p i h d", d=DH))\
                .then_inc(v_set, 1)
            pool.wait_ge(v_set, 1)
            for m, (seq, g) in enumerate(ahead):
                if m:
                    pool.wait_ge(scored, NH * UN * m)
                    pool.wait_ge(masked, GH * m)
                pool.memset(a["qs"][3 * GR:P, g, :].bitcast(F32), 0.0).then_inc(cleared, 1)
                pool.wait_ge(cleared, m + 1)
                pool.wait_ge(loaded[m], 96)
                mask_group(pool, t, a, g, m % NKF, masked)

        @block.tensor
        def _(pe):
            made = [0]

            def fill(kind, g, u, h):
                n = made[0]
                made[0] += 1
                bank = psum[:, M_BANK + n % NM, :]
                if n >= NM:
                    pe.wait_ge(used, n - NM + 1)
                if kind == "max":
                    m = g - (NG - 1)
                    if m >= 0 and (u, h) == (0, 0):
                        pe.wait_ge(loaded[m], 96)
                        pe.wait_ge(cleared, m + 1)
                    if m >= 0 and u % NT == 0 and h == 0:
                        pe.wait_ge(masked, GH * m + u // NT + 1)
                    score_for_maximum(pe, a, bank, g % NG, u, h).then_inc(filled, 1)
                elif kind == "turn_max":
                    pe.wait_ge(merged, g)
                    pe.transpose(bank[0:UN, 0:P], a["mx"][:, g % 2, :], t["ident"][:, :]).then_inc(filled, 1)
                else:
                    pe.wait_ge(out_copied, g + 1 + (h if g == NG - 1 else 0))
                    for i in range(TPH):
                        q = (h * TPH + i) * P
                        last = pe.transpose(bank[:, i * P:(i + 1) * P], a["o_raw"][:, q:q + P], t["ident"][:, :])
                    last.then_inc(filled, 1)

            def score(g, u, h):
                i, j = divmod(u, GH)
                n = NH * (UN * g + u) + h
                if (u, h) == (0, 0) and g:
                    pe.wait_ge(ext_set, g)
                if n >= NS:
                    pe.wait_ge(exped, n - NS + 1)
                pe.matmul(psum[:, S_BANK + n % NS, :], a["kp"][:, g, j, i * P:(i + 1) * P],
                          a["qs"][:, g, h * HALF:(h + 1) * HALF], start=True, stop=True).then_inc(scored, 1)

            def weigh(k):
                g, (i, h) = k // (NT * NH), divmod(k % (NT * NH), NH)
                pe.wait_ge(exped, NH * (UN * g + GH * (i + 1)))
                if (i, h) == (0, 0):
                    if g:
                        pe.wait_ge(out_copied, g)
                    else:
                        pe.wait_ge(v_set, 1)
                for j in range(GH):
                    slot = (GH * i + j) % NP
                    last = pe.matmul(psum[GR * j:GR * j + VW, O_BANK + h, :], a["v"][:, i, GH * g + j, :],
                                     a["p"][:, slot, h * HALF:(h + 1) * HALF], start=(i == 0), stop=(i == NT - 1))
                last.then_inc(weighed, 1)

            for g in range(NG):
                for u in range(UN):
                    todo = list(per_group[g][u])
                    for h in range(NH):
                        score(g, u, h)
                        if todo:
                            fill(*todo.pop(0))

                    n = UN * g + u
                    if n % 2 and n >= GH + 1:
                        weigh((n - GH - 1) // 2)
                    for f in todo:
                        fill(*f)
                    n = UN * g + u
            for k in range(NG * NT * NH - 2, NG * NT * NH):
                weigh(k)
            for f in per_group[NG - 1][UN]:
                fill(*f)
            for i in range(NT):
                pe.wait_ge(used, len(fills) - NH + i // TPH + 1)
                pe.transpose(psum[:, S_BANK + i // TPH, (i % TPH) * P:(i % TPH + 1) * P], a["o"][:, i, :],
                             t["ident"][:, :]).then_inc(o_turned, 1)
            for i in range(NT):
                pe.wait_ge(o_copied, i // TPH + 1)
                last = pe.matmul(psum[:, M_BANK + i // TPH, (i % TPH) * P:(i % TPH + 1) * P], t["y_t"][:, i * P:(i + 1) * P],
                                 w.att[layer][5], start=True, stop=True)
                if i % TPH == TPH - 1:
                    last.then_inc(y_done, 1)

        @block.scalar
        def _(act):
            def copy_out(g):
                act.wait_ge(weighed, NT * NH * (g + 1))
                if g >= 1:
                    act.wait_ge(filled, fills.index(("turn_out", g - 1, 0, NH - 1)) + 1)
                act.activation(a["o_raw"][:, :], psum[:, O_BANK:O_BANK + 2, :].rearrange("p a d -> p (a d)"),
                               ACT.Copy).then_inc(out_copied, 1)

            for g in range(NG):
                for u in range(UN):
                    n = UN * g + u
                    if u == GH and g >= 1:
                        copy_out(g - 1)
                    if n >= NP:
                        act.wait_ge(weighed, NH * ((n - NP) // GH + 1))
                    for h in range(NH):
                        act.wait_ge(scored, NH * n + h + 1)
                        act.activation(a["p"][:, n % NP, h * HALF:(h + 1) * HALF],
                                       psum[:, S_BANK + (NH * n + h) % NS, :],
                                       ACT.Exp, scale=DH ** -0.5).then_inc(exped, 1)
            act.wait_ge(filled, fills.index(("turn_out", NG - 2, 0, NH - 1)) + 1)
            for h in range(NH):
                act.wait_ge(weighed, NT * NH * NG - NH + h + 1)
                act.activation(a["o_raw"][:, h * HALF:(h + 1) * HALF], psum[:, O_BANK + h, :],
                               ACT.Copy).then_inc(out_copied, 1)
            for h in range(NH):
                act.wait_ge(o_turned, TPH * (h + 1))
                act.activation(t["y_t"][:, h * HALF:(h + 1) * HALF], psum[:, S_BANK + h, :], ACT.Copy)\
                    .then_inc(o_copied, 1)

        @block.vector
        def _(dve):
            recips = 0
            for n, (kind, g, u, h) in enumerate(fills):
                bank = psum[:, M_BANK + n % NM, :]
                dve.wait_ge(filled, n + 1)
                if kind == "max":
                    if (u, h) == (0, 0) and g >= 2:
                        dve.wait_ge(merged, g - 1)
                    dve.tensor_reduce(a["mh"][:, u, h:h + 1], bank, AX.X, ALU.max).then_inc(used, 1)
                    if (u, h) == (UN - 1, NH - 1):
                        dve.wait_ge(used, n + 1)
                        dve.tensor_reduce(a["mx"][:, g % 2, :], a["mh"][:, :, :], AX.X, ALU.max).then_inc(merged, 1)
                elif kind == "turn_max":
                    dve.wait_ge(used, n)
                    subtract_maxima(dve, t, a, g % NG, bank[0:UN, 0:P]).then_inc(ext_set, 1)
                    dve.wait_ge(ext_set, g)
                    dve.sem_inc(used, 1)
                else:
                    out = bank.rearrange("p (i j c) -> p i j c", i=TPH, j=GH)
                    recips += 1
                    dve.reciprocal(a["rs"][:, recips % 2, :, :], out[:, :, :, DH]).then_inc(recip, 1)
                    dve.wait_ge(recip, recips)
                    o = a["o"][:, h * TPH:(h + 1) * TPH, g * GR:(g + 1) * GR].rearrange("p i (j c) -> p i j c", c=DH)
                    dve.tensor_tensor(o, out[:, :, :, 0:DH],
                                      a["rs"][:, recips % 2, :, :].unsqueeze(3).to_broadcast([P, TPH, GH, DH]),
                                      ALU.mult).then_inc(used, 1)
            for h in range(NH):
                dve.wait_ge(y_done, h + 1)
                dve.tensor_tensor(t["sum"](h * TPH, TPH), psum[:, M_BANK + h, :].rearrange("p (a d) -> p a d", d=D),
                                  t["sum"](h * TPH, TPH), ALU.add)


class Weights:
    pass


def build(nc, x_in, cols_in, rows_in, gates_in, ident_in, cos_in, sin_in, diag_in, w0_in, wo_in, w1_in, w2_in,
          att_in, gate_in, consts_in, moe0_in, moe1_in, out):
    with ExitStack() as ctx:
        names = {}

        def sb(name, shape, dt=F32, where=ctx):
            names[name] = names.get(name, 0) + 1
            return where.enter_context(nc.sbuf_tensor(f"{name}_{names[name]}", shape, dt))

        t = {}
        t["psum"] = ctx.enter_context(nc.psum_tensor("psum", [P, 8, HALF], F32))
        for name in ("xn", "x2"):
            t[name] = sb(name, [P, NT, D])
        x_all, n_all = sb("x_all", [P, B * NT, D]), sb("n_all", [P, B * NT, D])
        t["y_t"] = sb("y_t", [P, L])
        cols, rows, gates = sb("cols", [P, NCOLS]), sb("rows", [P, len(ROWS), D]), sb("gates", [P, len(GATES), 16])
        t["rows"] = rows
        t["ident"] = sb("ident", [P, P])
        t["parts"] = nc.dram_tensor("qk_parts", [B, 4, P, L], F32).ap()
        t["moe_loaded"] = ctx.enter_context(nc.semaphore("moe_loaded"))
        t["weights_loaded"] = ctx.enter_context(nc.semaphore("weights_loaded"))
        t["first_loaded"] = ctx.enter_context(nc.semaphore("first_loaded"))
        t["neg_diag"] = sb("neg_diag", [P, NT, P])
        t["decay"] = sb("decay", [P, CH])
        t["stats"], t["mv"] = sb("stats", [P, NT, 6]), sb("mv", [P, NT, 2])
        for name in ("var", "std", "rstd", "tmp"):
            t[name] = sb(name, [P, 2, NT])
        t["col"] = lambda name, i=0: cols[:, COLS[name][0] + i:COLS[name][0] + i + 1]
        t["row"] = lambda name: rows[:, ROWS[name]:ROWS[name] + 1, :].to_broadcast([P, NT, D])
        t["grow"] = lambda name, E: gates[:, GATES[name]:GATES[name] + 1, 0:E].to_broadcast([P, NT, E])

        w = Weights()
        att = sb("att", [P, 2, 6, P])
        w.att = [[att[:, i, k, :] for k in range(6)] for i in range(2)]
        gate_w = sb("gate_w", [P, 2, 16])
        w.gate = [gate_w[:, i, :] for i in range(2)]
        t["wt"], t["w_now"] = sb("wt", [P, B * NT, 2]), sb("w_now", [P, NT, 2])
        t["n_rows"] = nc.dram_tensor("n_rows", [B * L, D], F32).ap()
        t["answers"] = nc.dram_tensor("answers", [2 * B * L + SLOT_TILES * P, D], F32).ap()
        t["parts_stored"], t["out_stored"] = (ctx.enter_context(nc.semaphore(n)) for n in ("parts_stored", "out_stored"))
        nc.sync.sem_inc(t["parts_stored"], 1)
        t["gathered"], t["scattered"] = ([ctx.enter_context(nc.semaphore(f"{n}{i}")) for i in range(PLACES)]
                                         for n in ("gathered", "scattered"))
        t["gathers"], t["scatters"] = [0] * PLACES, [0] * PLACES

        def view(tiles, b):
            return lambda i=0, n=NT: tiles[:, bass.ds(b * NT + i, n), :]

        x_v = x_in.rearrange("b (i p) d -> p (b i) d", p=P)
        with stage(nc, "loaded") as (block, loaded):
            @block.sync
            def _(sp):
                for to, of in ((x_all[:, 0:NT, :], x_v[:, 0:NT, :]), (cols[:, :], cols_in), (t["ident"][:, :], ident_in)):
                    sp.dma_start(to, of).then_inc(loaded, 16)
                sp.wait_ge(loaded, 48)

            @block.scalar
            def _(act):
                act.wait_ge(loaded, 48)
                lo, hi = COLS["decay"]
                act.activation(t["decay"][:, :], cols[:, lo:hi], ACT.Sigmoid)

        t["out_v"] = out.rearrange("b (i p) d -> b p i d", p=P)

        experts = ctx.enter_context(ExitStack())

        def room_for_experts(E, F):
            t["ew"] = sb("ew", [P, E, 2 * F * P + F + D], where=experts)

        def load_experts(layer):
            nc.sync.dma_start(t["ew"][:, :, :], (moe0_in, moe1_in)[layer]).then_inc(t["moe_loaded"], 16)

        room_for_experts(16, 2)
        with ExitStack() as scope:
            w.high, w.low = (sb(n, [P, 4, CH * P], F32R, where=scope) for n in ("w_high", "w_low"))
            w.o = wo = sb("wo", [P, CH, D], where=scope)
            w.w1, w.w2 = sb("w1", [P, FF * P], where=scope), sb("w2", [P, FF, D], where=scope)
            for name, n in (("v", 2), ("g", 2), ("kv", 2), ("state", 2), ("qg", 2), ("gated", 3)):
                t[name] = sb(name, [P, n, HALF], where=scope)
            t["ffh"] = sb("ffh", [P, FF, L], where=scope)
            t["yn"], t["y_f"] = sb("yn", [P, NT, D], where=scope), sb("y_f", [P, L], where=scope)
            t["y_high"], t["y_low"] = (sb(n, [P, L], F32R, where=scope) for n in ("y_high", "y_low"))
            loads = [(t["ffh"][:, i, :], w0_in[i]) for i in range(4)]
            loads += [(wo[:, :, :], wo_in), (w.w1[:, :], w1_in), (w.w2[:, :, :], w2_in)]
            loads += [(x_all[:, NT:B * NT, :], x_v[:, NT:B * NT, :]), (rows[:, :, :], rows_in), (gates[:, :, :], gates_in),
                      (t["neg_diag"][3 * GR:P, :, :], diag_in), (att[:, :, :, :], att_in), (gate_w[:, :, :], gate_in)]
            assert len(loads) == FIRST_LOADS and FF == 4 and L == CH * P
            for n, (to, of) in enumerate(loads):
                nc.sync.dma_start(to, of).then_inc(t["weights_loaded" if n < 4 else "first_loaded"], 16)
            load_experts(0)
            t["x"] = view(x_all, 0)
            recurrence_start(nc, t, w)
            with nc.Fori(0, B) as b:
                t["x"], t["x_next"] = view(x_all, b), view(x_all, (b + 1) % B)
                recurrence(nc, t, w)
                feed_forward(nc, t, w)

        def mixture(layer, E, F, func, rounds, KT, prepare):
            W, tiles, T = 2 * F * P + F + D, rounds * KT, B * NT
            with ExitStack() as scope:
                t["E"] = E
                for name in ("lg", "oh0", "oh1", "both", "pos"):
                    t[name] = sb(name, [P, T, E], where=scope)
                for name in ("cnt", "upto", "over"):
                    t[name] = sb(name, [P, E, T], where=scope)
                for name in ("per", "end", "base"):
                    t[name] = sb(name, [P, 16], where=scope)
                consts = sb("consts", [P, NCONSTS], where=scope)
                for name, (lo, hi) in CONSTS.items():
                    t[name] = consts[:, lo:hi]
                t["mx8"], t["ix8"] = sb("mx8", [P, T, 8], where=scope), sb("ix8", [P, T, 8], U32, where=scope)
                t["sel"], t["tmp2"] = sb("sel", [P, T, 2], where=scope), sb("tmp2", [P, T, 2], where=scope)
                t["ended"], t["who"] = sb("ended", [1, tiles, E], where=scope), sb("who", [1, tiles], where=scope)
                t["expert_of"] = sb("expert_of", [1, tiles], U32, where=scope)
                t["stage"] = sb("stage", [P, 3, W], where=scope)
                t["hi"], t["lo"] = sb("hi", [P, T, 2], where=scope), sb("lo", [P, T, 2], where=scope)
                t["lo_hot"], t["hi_hot"] = sb("lo_hot", [P, 2, INV, P], where=scope), sb("hi_hot", [P, 2 * INV, tiles], where=scope)
                for name in ("place_f", "token_f"):
                    t[name] = sb(name, [P, tiles], where=scope)
                for name in ("place_of", "token_of"):
                    t[name] = sb(name, [P, tiles], U32, where=scope)
                for name in ("place_now", "token_now"):
                    t[name] = sb(name, [P, KT], U32, where=scope)
                for name in ("x_in", "y_out"):
                    t[name] = sb(name, [P, PLACES, D], where=scope)
                t["x_t"], t["hid"] = sb("x_t", [P, 2, P], where=scope), sb("hid", [P, 2, F, P], where=scope)
                nc.sync.dma_start(consts[:, :], consts_in).then_inc(t["moe_loaded"], 16)
                with nc.Fori(0, B) as b:
                    t["x"], t["n_view"] = view(x_all, b), view(n_all, b)
                    prepare(b)
                for eng in (nc.vector, nc.tensor, nc.gpsimd):
                    eng.wait_ge(t["moe_loaded"], 32 * (layer + 1))
                route(nc, t, layer, E, tiles)
                invert(nc, t, tiles)
                with nc.Fori(0, rounds) as it:
                    expert_tiles(nc, t, it, KT, F, func)
                for n in range(PLACES):
                    for counts in (t["gathers"], t["scatters"]):
                        counts[n] += 16 * rounds * len(range(n, KT, PLACES))

        def fetch_first(scope):
            t["back"] = sb("back", [P, NT, 2, D], where=scope)
            t["mixed"] = sb("mixed", [P, NT, D], where=scope)
            with stage(nc, "fetched") as (block, fetched):
                @block.sync
                def _(sp):
                    fetch(sp, t, 0, fetched)
                    sp.wait_ge(fetched, 16)

        mixture(0, 16, 2, ACT.Relu, 4, 20, lambda b: gate_logits(nc, t, w, 0, b, 16, t["x"]()))

        experts.close()

        for layer in range(2):
            with ExitStack() as scope:
                a = {}
                t["v_all"] = sb("v_all", [P, B * NT, D], where=scope)
                target = (x_all, n_all)[layer]
                with ExitStack() as inner:
                    t["cos"], t["sin"] = sb("cos", [P, L], where=inner), sb("sin", [P, L], where=inner)
                    for name in ("qh", "ql", "kh", "kl"):
                        a[name] = sb(name, [P, L], F32R, where=inner)
                    for name in ("ra", "rb", "rot"):
                        a[name] = sb(name, [P, 2, HALF], where=inner)
                    with stage(nc, "loaded") as (block, loaded):
                        @block.sync
                        def _(sp):
                            sp.dma_start(t["cos"][:, :], cos_in).then_inc(loaded, 16)
                            sp.dma_start(t["sin"][:, :], sin_in).then_inc(loaded, 16)
                            sp.wait_ge(loaded, 32)
                    if layer == 0:
                        fetch_first(inner)
                    with nc.Fori(0, B) as b:
                        t["x"], t["sum"] = view(x_all, b), view(target, b)
                        attention_inputs(nc, t, w, layer, a, b)
                a["v"] = sb("v_ext", [P, NT, HEADS, VW], where=scope)
                a["qs"] = sb("qs", [P, NG, L], F32R, where=scope)
                a["kf"] = sb("kf", [P, NKF, L], F32R, where=scope)
                a["kp"] = sb("kp", [P, NG, GH, L], F32R, where=scope)
                a["p"] = sb("p", [P, NP, L], where=scope)
                a["o_raw"] = sb("o_raw", [P, L], where=scope)
                a["o"] = t["x2"]
                a["mh"] = sb("mh", [P, UN, NH], where=scope)
                a["mx"] = sb("mx", [P, 2, UN], where=scope)
                a["rs"] = sb("rs", [P, 2, TPH, GH], where=scope)
                attention_start(nc, t, layer, a)
                with nc.Fori(0, B) as b:
                    t["sum"] = view(target, b)
                    attention(nc, t, w, layer, a, b)

        room_for_experts(8, 4)
        load_experts(1)
        mixture(1, 8, 4, ACT.Gelu, 3, 24,
                lambda b: gate_logits(nc, t, w, 1, b, 8, t["n_view"](), t["row"]("g1"), t["row"]("be1")))
        experts.close()
        with ExitStack() as scope:
            fetch_first(scope)
            with nc.Fori(0, B) as b:
                t["x"], t["n_view"] = view(x_all, b), view(n_all, b)
                finish(nc, t, b)
            nc.sync.wait_ge(t["out_stored"], 16 * NH * B)


def layout(i):
    def cols(a):
        return np.reshape(a, (-1, P)).T

    def swap(a):
        s = np.reshape(a, (*a.shape[:-1], HEADS, 2, DH // 2))
        return np.reshape(s[..., ::-1, :], a.shape)

    c = np.zeros((P, NCOLS), np.float32)
    r = np.arange(P)

    def put(name, a):
        c[:, COLS[name][0]:COLS[name][1]] = a

    put("ln1_g", cols(i["L0_attn_ln1_g"])), put("ln1_b", cols(i["L0_attn_ln1_b"]))
    for n in "qkvg":
        put("b" + n, cols(i["L0_attn_b" + n]))
    put("decay", cols(np.repeat(i["L0_attn_decay_logit"], 64)))
    put("ln2_g", cols(i["L0_attn_ln2_g"])), put("ln2_b", cols(i["L0_attn_ln2_b"]))
    put("b1", cols(i["L0_attn_b1"]))
    for k, name in enumerate(("L1_attn_", "L1_ffn_")):
        for n in "qk":
            put(f"att{k}_b{n}", cols(i[f"{name}b{n}"]))
            put(f"att{k}_b{n}r", cols(swap(i[f"{name}b{n}"])))
    put("head_mask", (r[:, None] % GR // DH == np.arange(GH)[None]).astype(np.float32))
    rows = {"bo": "L0_attn_bo", "b2": "L0_attn_b2", "att0_bv": "L1_attn_bv", "att0_bo": "L1_attn_bo",
            "att1_bv": "L1_ffn_bv", "att1_bo": "L1_ffn_bo", "g1": "L1_ffn_g1", "be1": "L1_ffn_be1",
            "g2": "L1_ffn_g2", "be2": "L1_ffn_be2"}
    row = np.stack([i[rows[n]] for n in ROWS])
    gates = np.zeros((len(GATES), 16), np.float32)
    gates[0], gates[1], gates[2, 0:8] = i["L0_ffn_bg"], i["L0_ffn_bias"], i["L1_ffn_bg"]

    inv = (1.0 / np.float32(10000.0) ** (np.arange(0, DH, 2, dtype=np.float32) / np.float32(DH))).astype(np.float32)
    angle = (np.arange(L, dtype=np.float32)[None] * inv[r % (DH // 2)][:, None]).astype(np.float32)
    sign = np.where(r % DH < DH // 2, -1, 1).astype(np.float32)[:, None]
    diag = np.zeros((GR, NT, P), np.float32)
    diag[np.arange(GR), np.arange(GR) % NT, :] = -1.0

    att = []
    for wq, wk, wv, wo in ((i["L1_attn_Wq"].T, i["L1_attn_Wk"].T, i["L1_attn_Wv"].T, i["L1_attn_Wo"].T),
                           (i["L1_ffn_Wq"], i["L1_ffn_Wk"], i["L1_ffn_Wv"], i["L1_ffn_Wo"])):
        att.append(np.stack([wq, wk, swap(wq), swap(wk), wv, wo], 1))
    gate_w = np.zeros((P, 2, 16), np.float32)
    gate_w[:, 0, :], gate_w[:, 1, 0:8] = i["L0_ffn_Wg"], i["L1_ffn_Wg"]
    consts = np.zeros((P, NCONSTS), np.float32)
    for name, value in (("iota", np.arange(P)), ("iota128", P * np.arange(B * NT)),
                        ("keep", np.arange(16 * B * NT) % (B * NT) != 0), ("before", r[:, None] < r[None, :]),
                        ("ones", np.ones(P)),
                        ("place", 1 + (2 * P * np.arange(B * NT)[:, None] + 2 * r[:, None, None]
                                       + np.arange(2)).reshape(P, -1)),
                        ("unfilled", 1 + 2 * B * L + P * np.arange(SLOT_TILES) + r[:, None])):
        consts[:, CONSTS[name][0]:CONSTS[name][1]] = value

    def expert_weights(name):
        w1, w2, b1, b2 = (i[name + n] for n in ("W1", "W2", "b1", "b2"))
        e = w1.shape[0]
        return np.concatenate([
            w1.transpose(1, 0, 2), np.reshape(np.reshape(w2, (e, -1, P, D)).transpose(2, 0, 1, 3), (P, e, -1)),
            np.reshape(b1, (e, -1, P)).transpose(2, 0, 1), np.broadcast_to(b2[None], (P, e, D))], 2)

    arrays = {
        "x": i["L0_attn_x"], "cols": c, "rows": np.broadcast_to(row[None], (P, *row.shape)),
        "gates": np.broadcast_to(gates[None], (P, *gates.shape)), "ident": np.eye(P, dtype=np.float32),
        "cos": np.cos(angle), "sin": np.sin(angle) * sign, "diag": diag,
        "w0": np.stack([i["L0_attn_W" + n] for n in "qkvg"]),
        "wo": np.reshape(i["L0_attn_Wo"], (CH, P, D)).transpose(1, 0, 2), "w1": i["L0_attn_W1"],
        "w2": np.reshape(i["L0_attn_W2"], (FF, P, D)).transpose(1, 0, 2),
        "att": np.stack(att, 1), "gate": gate_w, "consts": consts,
        "moe0": expert_weights("L0_ffn_"), "moe1": expert_weights("L1_ffn_"),
    }
    return {k: np.ascontiguousarray(v) for k, v in arrays.items()}


def kernel(**inputs):
    import concourse.bacc as bacc
    from concourse.bass_utils import run_bass_kernel_spmd

    nc = bacc.Bacc("TRN2", target_bir_lowering=False, num_devices=1, dynamic_dma_scratch_size=2048)
    arrays = {f"in_{k}": v for k, v in layout({k: np.asarray(v) for k, v in inputs.items()}).items()}
    args = [nc.dram_tensor(k, v.shape, mybir.dt.from_np(v.dtype), kind="ExternalInput").ap() for k, v in arrays.items()]
    out = nc.dram_tensor("out", (B, L, D), F32, kind="ExternalOutput").ap()
    build(nc, *args, out)
    return run_bass_kernel_spmd(nc, [arrays], core_ids=[0]).results[0]["out"]
```
